# Optimizing a Trainium2 kernel written in Bass

```python
import numpy as np
import jax
import jax.numpy as jnp

def _softmax(x, axis=-1):
    return jax.nn.softmax(x, axis=axis)

def _gelu(x):
    return jax.nn.gelu(x, approximate=True)

def _silu(x):
    return jax.nn.silu(x)

def _sigmoid(x):
    return jax.nn.sigmoid(x)

def _layernorm(x, axis=-1, eps=1e-05):
    m = jnp.mean(x, axis=axis, keepdims=True)
    v = jnp.var(x, axis=axis, keepdims=True)
    return (x - m) / jnp.sqrt(v + eps)

def _scatter_add(tgt, idx, src, axis=0):
    return tgt.at[idx].add(src)

def _segment_sum(src, seg, n):
    return jax.ops.segment_sum(src, seg, n)
kernel_name = 'mk_recurrent_d1_jaxref_r8_3ea9d3'

def setup_inputs(seed: int=0):
    np.random.seed(seed)
    _w = jnp.asarray

    def _L0_attn_setup():
        import jax, jax.numpy as jnp
        import numpy as np
        B, N, D = (2, 256, 128)
        H, DK, DV = (8, 128, 128)
        key = jax.random.key(seed)
        kx, kq, kk, kv = jax.random.split(key, 4)
        scale = 0.02
        x = jax.random.normal(kx, (B, N, D), dtype=jnp.float32)
        Wq = jax.random.normal(kq, (H, DK, D), dtype=jnp.float32) * scale
        Wk = jax.random.normal(kk, (H, DK, D), dtype=jnp.float32) * scale
        Wv = jax.random.normal(kv, (H, DV, D), dtype=jnp.float32) * scale
        return {'x': x, 'Wq': Wq, 'Wk': Wk, 'Wv': Wv}
    _L0_attn_in = _L0_attn_setup()

    def _L0_ffn_setup():
        import math
        import jax, jax.numpy as jnp
        import numpy as np
        B = 2
        N = 256
        DIM = 128
        HEADS = 16
        DIM_HEAD = 64
        INNER = HEADS * DIM_HEAD
        W = 64
        G = 2
        NQ = 32
        NKV = 128
        EPS = 0.03
        EPS_INIT = 4.0
        EPS_DECAY = 0.7
        N_ITERS = 20
        NEG = -1e+30

        def rotate_half(x):
            x1, x2 = jnp.split(x, 2, axis=-1)
            return jnp.concatenate([-x2, x1], axis=-1)

        def local_mha(x, ln_g, ln_b, w_qkv, w_lo):
            b, n, d = x.shape
            mu = x.mean(-1, keepdims=True)
            var = jnp.mean((x - mu) ** 2, axis=-1, keepdims=True)
            xn = (x - mu) / jnp.sqrt(var + 1e-05) * ln_g + ln_b
            qkv = xn @ w_qkv.T
            q, k, v = jnp.split(qkv, 3, axis=-1)
            sh = lambda t: t.reshape(b, n, HEADS, DIM_HEAD).transpose(0, 2, 1, 3)
            q, k, v = (sh(q), sh(k), sh(v))
            inv_freq = 1.0 / 10000.0 ** (jnp.arange(0, DIM_HEAD, 2, dtype=jnp.float32) / DIM_HEAD)
            t = jnp.arange(n, dtype=jnp.float32)
            freqs = t[:, None] * inv_freq[None, :]
            freqs = jnp.concatenate([freqs, freqs], axis=-1)
            cos, sin = (jnp.cos(freqs), jnp.sin(freqs))
            q = q * cos + rotate_half(q) * sin
            k = k * cos + rotate_half(k) * sin
            nw = n // W
            win = lambda t: t.reshape(b, HEADS, nw, W, DIM_HEAD)

            def look_around(t):
                prev = jnp.pad(t[:, :, :-1], ((0, 0), (0, 0), (1, 0), (0, 0), (0, 0)))
                return jnp.concatenate([prev, t], axis=3)
            bq = win(q)
            bk = look_around(win(k))
            bv = look_around(win(v))
            qpos = jnp.arange(n).reshape(nw, W)
            kprev = jnp.pad(qpos[:-1], ((1, 0), (0, 0)), constant_values=-1)
            kpos = jnp.concatenate([kprev, qpos], axis=-1)
            allow = (kpos[:, None, :] >= 0) & (kpos[:, None, :] <= qpos[:, :, None]) & (qpos[:, :, None] - kpos[:, None, :] <= W)
            sim = jnp.einsum('bhnqd,bhnkd->bhnqk', bq, bk) * DIM_HEAD ** (-0.5)
            sim = jnp.where(allow[None, None], sim, NEG)
            attn = jax.nn.softmax(sim, axis=-1)
            out = jnp.einsum('bhnqk,bhnkd->bhnqd', attn, bv)
            out = out.reshape(b, HEADS, n, DIM_HEAD).transpose(0, 2, 1, 3).reshape(b, n, INNER)
            return out @ w_lo.T

        def coor_descent(s, k, mask):
            logk = math.log(k)
            s = jnp.where(mask, s, NEG)
            bneg = -s
            a = jnp.zeros_like(s[..., :1])
            eps_sched = [max(EPS_INIT * EPS_DECAY ** i, EPS) for i in range(N_ITERS)]
            for ce in eps_sched:
                sb = jnp.where(mask, (s + bneg) / ce, NEG)
                a = ce * (logk - jax.scipy.special.logsumexp(sb, axis=-1, keepdims=True))
                bneg = -jax.nn.relu(s + a)
            fe = max(EPS_INIT * EPS_DECAY ** N_ITERS, EPS)
            scores = jnp.exp((s + a + bneg) / fe)
            return jnp.where(mask, scores, 0.0)

        def router(x, routing_tokens, mask, num_tokens):
            Bx, n, d = x.shape
            s = jnp.einsum('bnd,gd->bgn', x, routing_tokens)
            k = min(num_tokens * 9.0 / 8.0, float(n))
            scores = coor_descent(s, k, mask[:, None, :])
            sel_scores, sel_idx = jax.lax.top_k(scores, num_tokens)
            sel_scores = sel_scores + jax.lax.stop_gradient(1.0 - sel_scores)
            sel_mask = jnp.take_along_axis(jnp.broadcast_to(mask[:, None, :], s.shape), sel_idx, axis=-1)
            sel_scores = jnp.where(sel_mask, sel_scores, 0.0)
            routed = x[jnp.arange(Bx)[:, None, None], sel_idx]
            return (sel_idx, sel_scores, routed, sel_mask)

        def grouped_attention(qt, kvt, kv_mask, v_scale, out_scale, qnorm_g, cnorm_g, null_kv, w_q, w_kv, w_out):
            Bq = qt.shape[0]
            rms_scale = DIM ** 0.5

            def rms(t, g):
                nrm = jnp.maximum(jnp.linalg.norm(t, axis=-1, keepdims=True), 1e-12)
                return t / nrm * rms_scale * g[None, :, None, :]
            xq = rms(qt, qnorm_g)
            xc = rms(kvt, cnorm_g)
            q = jnp.einsum('bgnd,god->bgno', xq, w_q)
            kv = jnp.einsum('bgnd,god->bgno', xc, w_kv)
            k, v = jnp.split(kv, 2, axis=-1)
            sh = lambda t: t.reshape(Bq, G, t.shape[2], HEADS, DIM_HEAD).transpose(0, 1, 3, 2, 4)
            q, k, v = (sh(q), sh(k), sh(v))
            v = v * v_scale[:, :, None, :, None]
            nk = jnp.broadcast_to(null_kv[0][None], (Bq, G, HEADS, 1, DIM_HEAD))
            nv = jnp.broadcast_to(null_kv[1][None], (Bq, G, HEADS, 1, DIM_HEAD))
            k = jnp.concatenate([nk, k], axis=3)
            v = jnp.concatenate([nv, v], axis=3)
            kmask = jnp.pad(kv_mask, ((0, 0), (0, 0), (1, 0)), constant_values=True)
            sim = jnp.einsum('bghqd,bghkd->bghqk', q, k) * DIM_HEAD ** (-0.5)
            sim = jnp.where(kmask[:, :, None, None, :], sim, NEG)
            attn = jax.nn.softmax(sim, axis=-1)
            o = jnp.einsum('bghqk,bghkd->bghqd', attn, v)
            o = o.transpose(0, 1, 3, 2, 4).reshape(Bq, G, -1, INNER)
            o = jnp.einsum('bgno,gdo->bgnd', o, w_out)
            return o * out_scale[..., None]

        def _forward(x, ln_g, ln_b, w_qkv, w_lo, rt_q, rt_kv, qnorm_g, cnorm_g, null_kv, w_q, w_kv, w_out):
            b, n, d = x.shape
            nwins = n // W - 1
            local_out = local_mha(x, ln_g, ln_b, w_qkv, w_lo)
            nctx = n - W
            ctx = jnp.broadcast_to(x[:, None, :-W, :], (b, nwins, nctx, d)).reshape(b * nwins, nctx, d)
            tril = jnp.tril(jnp.ones((nwins, nwins), bool))
            ctx_mask = jnp.broadcast_to(tril[None, :, :, None], (b, nwins, nwins, W)).reshape(b * nwins, nctx)
            xw = x.reshape(b, n // W, W, d)[:, 1:].reshape(b * nwins, W, d)
            qmask = jnp.ones((b * nwins, W), bool)
            q_idx, q_scores, queries, q_sel_mask = router(xw, rt_q, qmask, NQ)
            _, kv_scores, key_values, kv_sel_mask = router(ctx, rt_kv, ctx_mask, NKV)
            attn_out = grouped_attention(queries, key_values, kv_sel_mask, kv_scores, q_scores, qnorm_g, cnorm_g, null_kv, w_q, w_kv, w_out)
            Bq = b * nwins
            rows = jnp.arange(Bq)[:, None]
            flat_idx = q_idx.reshape(Bq, G * NQ)
            flat_out = attn_out.reshape(Bq, G * NQ, d)
            summed = jnp.zeros((Bq, W, d), x.dtype).at[rows, flat_idx].add(flat_out)
            ones = q_sel_mask.reshape(Bq, G * NQ).astype(x.dtype)
            counts = jnp.zeros((Bq, W), x.dtype).at[rows, flat_idx].add(ones)
            summed = summed.reshape(b, nwins * W, d)
            counts = counts.reshape(b, nwins * W)
            summed = jnp.pad(summed, ((0, 0), (W, 0), (0, 0)))[:, :n]
            counts = jnp.pad(counts, ((0, 0), (W, 0)))[:, :n]
            summed = summed + local_out
            counts = counts + 1.0
            return summed / jnp.maximum(counts[..., None], 1e-05)
        key = jax.random.key(seed)
        ks = jax.random.split(key, 10)
        nrm = lambda k, shape, fan_in: jax.random.normal(k, shape, jnp.float32) / math.sqrt(fan_in)
        return {'x': jax.random.normal(ks[0], (B, N, DIM), jnp.float32), 'ln_g': jnp.ones((DIM,), jnp.float32), 'ln_b': jnp.zeros((DIM,), jnp.float32), 'w_qkv': nrm(ks[1], (3 * INNER, DIM), DIM), 'w_lo': nrm(ks[2], (DIM, INNER), INNER), 'rt_q': jax.random.normal(ks[3], (G, DIM), jnp.float32), 'rt_kv': jax.random.normal(ks[4], (G, DIM), jnp.float32), 'qnorm_g': jnp.ones((G, DIM), jnp.float32), 'cnorm_g': jnp.ones((G, DIM), jnp.float32), 'null_kv': jax.random.normal(ks[5], (2, G, HEADS, 1, DIM_HEAD), jnp.float32), 'w_q': nrm(ks[6], (G, INNER, DIM), DIM), 'w_kv': nrm(ks[7], (G, 2 * INNER, DIM), DIM), 'w_out': nrm(ks[8], (G, DIM, INNER), INNER)}
    _L0_ffn_in = _L0_ffn_setup()
    _d = {'L0_attn_x': _L0_attn_in['x'], 'L0_attn_Wq': _L0_attn_in['Wq'], 'L0_attn_Wk': _L0_attn_in['Wk'], 'L0_attn_Wv': _L0_attn_in['Wv'], 'L0_ffn_ln_g': _L0_ffn_in['ln_g'], 'L0_ffn_ln_b': _L0_ffn_in['ln_b'], 'L0_ffn_w_qkv': _L0_ffn_in['w_qkv'], 'L0_ffn_w_lo': _L0_ffn_in['w_lo'], 'L0_ffn_rt_q': _L0_ffn_in['rt_q'], 'L0_ffn_rt_kv': _L0_ffn_in['rt_kv'], 'L0_ffn_qnorm_g': _L0_ffn_in['qnorm_g'], 'L0_ffn_cnorm_g': _L0_ffn_in['cnorm_g'], 'L0_ffn_null_kv': _L0_ffn_in['null_kv'], 'L0_ffn_w_q': _L0_ffn_in['w_q'], 'L0_ffn_w_kv': _L0_ffn_in['w_kv'], 'L0_ffn_w_out': _L0_ffn_in['w_out']}
    _x0 = _d['L0_attn_x']
    _d['L0_attn_x'] = jax.random.normal(jax.random.fold_in(jax.random.key(seed), 1), (4, 512, 128), dtype=_x0.dtype)
    del _x0
    return _d

def reference(L0_attn_x, L0_attn_Wq, L0_attn_Wk, L0_attn_Wv, L0_ffn_ln_g, L0_ffn_ln_b, L0_ffn_w_qkv, L0_ffn_w_lo, L0_ffn_rt_q, L0_ffn_rt_kv, L0_ffn_qnorm_g, L0_ffn_cnorm_g, L0_ffn_null_kv, L0_ffn_w_q, L0_ffn_w_kv, L0_ffn_w_out):

    def _L0_attn_ref(x, Wq, Wk, Wv):
        import jax, jax.numpy as jnp
        import numpy as np
        B, N, D = (2, 256, 128)
        H, DK, DV = (8, 128, 128)
        n = x.shape[-2]
        Q = jnp.einsum('bnd,hed->bhne', x, Wq)
        K = jnp.einsum('bnd,hed->bhne', x, Wk)
        V = jnp.einsum('bnd,hvd->bhnv', x, Wv)
        scores = jnp.einsum('bhne,bhme->bhnm', Q, K)
        causal = jnp.tril(jnp.ones((n, n), dtype=bool))
        sim = jnp.where(causal, jax.nn.relu(scores), jnp.float32(0.0)) / jnp.float32(n)
        head_out = jnp.einsum('bhnm,bhmv->bnv', sim, V)
        return x + head_out

    def _L0_ffn_ref(x, ln_g, ln_b, w_qkv, w_lo, rt_q, rt_kv, qnorm_g, cnorm_g, null_kv, w_q, w_kv, w_out):
        import math
        import jax, jax.numpy as jnp
        import numpy as np
        B = 2
        N = 256
        DIM = 128
        HEADS = 16
        DIM_HEAD = 64
        INNER = HEADS * DIM_HEAD
        W = 64
        G = 2
        NQ = 32
        NKV = 128
        EPS = 0.03
        EPS_INIT = 4.0
        EPS_DECAY = 0.7
        N_ITERS = 20
        NEG = -1e+30

        def rotate_half(x):
            x1, x2 = jnp.split(x, 2, axis=-1)
            return jnp.concatenate([-x2, x1], axis=-1)

        def local_mha(x, ln_g, ln_b, w_qkv, w_lo):
            b, n, d = x.shape
            mu = x.mean(-1, keepdims=True)
            var = jnp.mean((x - mu) ** 2, axis=-1, keepdims=True)
            xn = (x - mu) / jnp.sqrt(var + 1e-05) * ln_g + ln_b
            qkv = xn @ w_qkv.T
            q, k, v = jnp.split(qkv, 3, axis=-1)
            sh = lambda t: t.reshape(b, n, HEADS, DIM_HEAD).transpose(0, 2, 1, 3)
            q, k, v = (sh(q), sh(k), sh(v))
            inv_freq = 1.0 / 10000.0 ** (jnp.arange(0, DIM_HEAD, 2, dtype=jnp.float32) / DIM_HEAD)
            t = jnp.arange(n, dtype=jnp.float32)
            freqs = t[:, None] * inv_freq[None, :]
            freqs = jnp.concatenate([freqs, freqs], axis=-1)
            cos, sin = (jnp.cos(freqs), jnp.sin(freqs))
            q = q * cos + rotate_half(q) * sin
            k = k * cos + rotate_half(k) * sin
            nw = n // W
            win = lambda t: t.reshape(b, HEADS, nw, W, DIM_HEAD)

            def look_around(t):
                prev = jnp.pad(t[:, :, :-1], ((0, 0), (0, 0), (1, 0), (0, 0), (0, 0)))
                return jnp.concatenate([prev, t], axis=3)
            bq = win(q)
            bk = look_around(win(k))
            bv = look_around(win(v))
            qpos = jnp.arange(n).reshape(nw, W)
            kprev = jnp.pad(qpos[:-1], ((1, 0), (0, 0)), constant_values=-1)
            kpos = jnp.concatenate([kprev, qpos], axis=-1)
            allow = (kpos[:, None, :] >= 0) & (kpos[:, None, :] <= qpos[:, :, None]) & (qpos[:, :, None] - kpos[:, None, :] <= W)
            sim = jnp.einsum('bhnqd,bhnkd->bhnqk', bq, bk) * DIM_HEAD ** (-0.5)
            sim = jnp.where(allow[None, None], sim, NEG)
            attn = jax.nn.softmax(sim, axis=-1)
            out = jnp.einsum('bhnqk,bhnkd->bhnqd', attn, bv)
            out = out.reshape(b, HEADS, n, DIM_HEAD).transpose(0, 2, 1, 3).reshape(b, n, INNER)
            return out @ w_lo.T

        def coor_descent(s, k, mask):
            logk = math.log(k)
            s = jnp.where(mask, s, NEG)
            bneg = -s
            a = jnp.zeros_like(s[..., :1])
            eps_sched = [max(EPS_INIT * EPS_DECAY ** i, EPS) for i in range(N_ITERS)]
            for ce in eps_sched:
                sb = jnp.where(mask, (s + bneg) / ce, NEG)
                a = ce * (logk - jax.scipy.special.logsumexp(sb, axis=-1, keepdims=True))
                bneg = -jax.nn.relu(s + a)
            fe = max(EPS_INIT * EPS_DECAY ** N_ITERS, EPS)
            scores = jnp.exp((s + a + bneg) / fe)
            return jnp.where(mask, scores, 0.0)

        def router(x, routing_tokens, mask, num_tokens):
            Bx, n, d = x.shape
            s = jnp.einsum('bnd,gd->bgn', x, routing_tokens)
            k = min(num_tokens * 9.0 / 8.0, float(n))
            scores = coor_descent(s, k, mask[:, None, :])
            sel_scores, sel_idx = jax.lax.top_k(scores, num_tokens)
            sel_scores = sel_scores + jax.lax.stop_gradient(1.0 - sel_scores)
            sel_mask = jnp.take_along_axis(jnp.broadcast_to(mask[:, None, :], s.shape), sel_idx, axis=-1)
            sel_scores = jnp.where(sel_mask, sel_scores, 0.0)
            routed = x[jnp.arange(Bx)[:, None, None], sel_idx]
            return (sel_idx, sel_scores, routed, sel_mask)

        def grouped_attention(qt, kvt, kv_mask, v_scale, out_scale, qnorm_g, cnorm_g, null_kv, w_q, w_kv, w_out):
            Bq = qt.shape[0]
            rms_scale = DIM ** 0.5

            def rms(t, g):
                nrm = jnp.maximum(jnp.linalg.norm(t, axis=-1, keepdims=True), 1e-12)
                return t / nrm * rms_scale * g[None, :, None, :]
            xq = rms(qt, qnorm_g)
            xc = rms(kvt, cnorm_g)
            q = jnp.einsum('bgnd,god->bgno', xq, w_q)
            kv = jnp.einsum('bgnd,god->bgno', xc, w_kv)
            k, v = jnp.split(kv, 2, axis=-1)
            sh = lambda t: t.reshape(Bq, G, t.shape[2], HEADS, DIM_HEAD).transpose(0, 1, 3, 2, 4)
            q, k, v = (sh(q), sh(k), sh(v))
            v = v * v_scale[:, :, None, :, None]
            nk = jnp.broadcast_to(null_kv[0][None], (Bq, G, HEADS, 1, DIM_HEAD))
            nv = jnp.broadcast_to(null_kv[1][None], (Bq, G, HEADS, 1, DIM_HEAD))
            k = jnp.concatenate([nk, k], axis=3)
            v = jnp.concatenate([nv, v], axis=3)
            kmask = jnp.pad(kv_mask, ((0, 0), (0, 0), (1, 0)), constant_values=True)
            sim = jnp.einsum('bghqd,bghkd->bghqk', q, k) * DIM_HEAD ** (-0.5)
            sim = jnp.where(kmask[:, :, None, None, :], sim, NEG)
            attn = jax.nn.softmax(sim, axis=-1)
            o = jnp.einsum('bghqk,bghkd->bghqd', attn, v)
            o = o.transpose(0, 1, 3, 2, 4).reshape(Bq, G, -1, INNER)
            o = jnp.einsum('bgno,gdo->bgnd', o, w_out)
            return o * out_scale[..., None]

        def _forward(x, ln_g, ln_b, w_qkv, w_lo, rt_q, rt_kv, qnorm_g, cnorm_g, null_kv, w_q, w_kv, w_out):
            b, n, d = x.shape
            nwins = n // W - 1
            local_out = local_mha(x, ln_g, ln_b, w_qkv, w_lo)
            nctx = n - W
            ctx = jnp.broadcast_to(x[:, None, :-W, :], (b, nwins, nctx, d)).reshape(b * nwins, nctx, d)
            tril = jnp.tril(jnp.ones((nwins, nwins), bool))
            ctx_mask = jnp.broadcast_to(tril[None, :, :, None], (b, nwins, nwins, W)).reshape(b * nwins, nctx)
            xw = x.reshape(b, n // W, W, d)[:, 1:].reshape(b * nwins, W, d)
            qmask = jnp.ones((b * nwins, W), bool)
            q_idx, q_scores, queries, q_sel_mask = router(xw, rt_q, qmask, NQ)
            _, kv_scores, key_values, kv_sel_mask = router(ctx, rt_kv, ctx_mask, NKV)
            attn_out = grouped_attention(queries, key_values, kv_sel_mask, kv_scores, q_scores, qnorm_g, cnorm_g, null_kv, w_q, w_kv, w_out)
            Bq = b * nwins
            rows = jnp.arange(Bq)[:, None]
            flat_idx = q_idx.reshape(Bq, G * NQ)
            flat_out = attn_out.reshape(Bq, G * NQ, d)
            summed = jnp.zeros((Bq, W, d), x.dtype).at[rows, flat_idx].add(flat_out)
            ones = q_sel_mask.reshape(Bq, G * NQ).astype(x.dtype)
            counts = jnp.zeros((Bq, W), x.dtype).at[rows, flat_idx].add(ones)
            summed = summed.reshape(b, nwins * W, d)
            counts = counts.reshape(b, nwins * W)
            summed = jnp.pad(summed, ((0, 0), (W, 0), (0, 0)))[:, :n]
            counts = jnp.pad(counts, ((0, 0), (W, 0)))[:, :n]
            summed = summed + local_out
            counts = counts + 1.0
            return summed / jnp.maximum(counts[..., None], 1e-05)
        return _forward(x, ln_g, ln_b, w_qkv, w_lo, rt_q, rt_kv, qnorm_g, cnorm_g, null_kv, w_q, w_kv, w_out)
    x = L0_attn_x
    xn = _layernorm(x, axis=-1)
    s = _L0_attn_ref(xn, L0_attn_Wq, L0_attn_Wk, L0_attn_Wv)
    g = _silu(_L0_ffn_ref(xn, L0_ffn_ln_g, L0_ffn_ln_b, L0_ffn_w_qkv, L0_ffn_w_lo, L0_ffn_rt_q, L0_ffn_rt_kv, L0_ffn_qnorm_g, L0_ffn_cnorm_g, L0_ffn_null_kv, L0_ffn_w_q, L0_ffn_w_kv, L0_ffn_w_out))
    x = x + s * g
    return x

_drawn_inputs = setup_inputs


def setup_inputs(seed=0):
    import zlib

    import numpy as np

    out = dict(_drawn_inputs(seed))
    spreads = {'L0_ffn_ln_g': (1.0, 0.2),
     'L0_ffn_ln_b': (0.0, 0.1),
     'L0_ffn_qnorm_g': (1.0, 0.6),
     'L0_ffn_cnorm_g': (1.0, 0.6)}
    factors = {'L0_attn_Wq': 8.0, 'L0_attn_Wk': 8.0, 'L0_attn_Wv': 8.0, 'L0_ffn_null_kv': 8.0}
    for name, (base, spread) in spreads.items():
        noise = np.random.default_rng([zlib.crc32(name.encode()), seed]).standard_normal(out[name].shape)
        drawn = base * np.exp(spread * noise) if base else spread * noise
        out[name] = jnp.asarray(drawn.astype(out[name].dtype))
    for name, factor in factors.items():
        out[name] = (out[name] * factor).astype(out[name].dtype)
    return out
```

```python
from contextlib import ExitStack

import numpy as np

import concourse.bass as bass
from concourse import mybir

P = 128
B, N, D = 4, 512, 128
BLK = N // P
NB = B * BLK
HA = 8
DH = 64
H = 16
PAIRS = H // 2
W = 64
NW = N // W
WQ = NW - 1
G = 2
NQ, NKV = 32, 128
NITER = 20
CTX = N - W
KV_W0 = 2
KV_ROWS = (WQ - KV_W0) * B * G
Q_ROWS = WQ * B * G
Q_AT = 64
NEG = -1.0e30
TAKEN = -3.0e38
EPS = [max(4.0 * 0.7**i, 0.03) for i in range(NITER + 1)]
LOWEST = -87.33655
SCALE = DH**-0.5
UNITS = 4

F32 = mybir.dt.float32
BF16 = mybir.dt.bfloat16
ALU = mybir.AluOpType
ACT = mybir.ActivationFunctionType
AX = mybir.AxisListType


def kv_row(w, g, b):
    return (w - KV_W0) * G * B + g * B + b


def q_row(w, g, b):
    return w * G * B + g * B + b


def shape_constants():
    f = np.float32
    c = {}
    c["ident"] = np.eye(P, dtype=f)
    i = np.arange(P)
    c["causal"] = ((i[:, None] <= i[None, :]) / f(N)).astype(f)
    inv = (f(1.0) / np.power(f(10000.0), np.arange(0, DH, 2, dtype=f) / f(DH))).astype(f)
    ang = (np.arange(N, dtype=f)[:, None] * inv[None, :]).astype(f)
    cos, sin = np.cos(ang).astype(f), np.sin(ang).astype(f)
    by_block = lambda t: t.reshape(BLK, P, -1).transpose(1, 0, 2).copy()
    c["cos"] = by_block(np.concatenate([cos, cos], 1))
    c["sin"] = by_block(np.concatenate([-sin, sin], 1))
    q, k = np.arange(P)[:, None] % W, np.arange(P)[None, :]
    first = np.where(k <= q, 0.0, NEG)
    later = np.where((k >= q) & (k - W <= q), 0.0, NEG)
    c["window"] = np.concatenate([first] + [later] * 4, 1).astype(f)
    rmask = np.zeros((P, CTX), f)
    rinvk = np.ones((P, 1), f)
    half = np.zeros((P, 3), f)
    for g in range(G):
        for b in range(B):
            for w in range(KV_W0, WQ):
                rmask[kv_row(w, g, b), W * (w + 1):] = NEG
                rinvk[kv_row(w, g, b)] = 1.0 / (NKV * 9.0 / 8.0)
            for w in range(WQ):
                r = Q_AT + q_row(w, g, b)
                rmask[r, W:] = NEG
                rinvk[r] = 1.0 / (NQ * 9.0 / 8.0)
                odd = (w + 1) % 2
                half[r] = [NQ * odd, 1 - odd, odd]
    c["rmask"], c["rinvk"], c["half"] = rmask, rinvk, half
    e = np.array(EPS[:NITER], np.float64)
    c["eps"] = np.tile(np.stack([1.0 / e, e]).astype(f)[None], (P, 1, 1))
    c["iota"] = np.tile(np.arange(1, P + 1, dtype=f), (P, 1))
    h4, qq = np.arange(P) // NQ, np.arange(P) % NQ
    c["own"] = (h4[:, None] == np.arange(H)[None, :] % 4).astype(f)
    c["fold"] = (qq[:, None] == np.arange(NQ)[None, :]).astype(f)
    return c


CONSTS = ["ident", "causal", "cos", "sin", "window", "rmask", "rinvk", "half", "eps", "iota", "own", "fold"]


def build(nc, dram, out):
    ctx = ExitStack()
    with ctx:
        def sb(name, shape, dt=F32):
            return ctx.enter_context(nc.sbuf_tensor(name, shape, dt))

        def sem(name):
            return ctx.enter_context(nc.semaphore(name))

        x = sb("x", [P, NB, D])
        xhat = sb("xhat", [P, NB, D])
        G2 = sb("G2", [P, G * H, D])
        W2C = sb("W2C", [P, G * H, D])
        sT = sb("sT", [P, B, N])
        loc = sb("loc", [P, B, N])
        ident = sb("ident", [P, P])
        identb = sb("identb", [P, P], BF16)
        causal = sb("causal", [P, P])
        zerob = sb("zerob", [P, N], BF16)
        cos = sb("cos", [P, BLK, DH])
        sin = sb("sin", [P, BLK, DH])
        windowf = sb("windowf", [P, 5 * P])
        windowb = sb("windowb", [P, 5 * P], BF16)
        rmask = sb("rmask", [P, CTX])
        rinvk = sb("rinvk", [P, 1])
        half = sb("half", [P, 3])
        eps = sb("eps", [P, 2, NITER])
        iota = sb("iota", [P, P])
        own = sb("own", [P, H])
        fold = sb("fold", [P, NQ])
        lng = sb("lng", [P, 1])
        lnb = sb("lnb", [P, 1])
        qg = sb("qg", [P, G])
        nkv = sb("nkv", [P, 2, G, PAIRS])
        cg = sb("cg", [P, G, D])
        rtq = sb("rtq", [P, G])
        rtk = sb("rtk", [P, G])
        NK = sb("NK", [P, G, H])
        NV = sb("NV", [H, G, D])
        wscr = sb("wscr", [P, 2, D])
        gscr = sb("gscr", [P, D])
        RS = sb("RS", [P, CTX])
        RU = sb("RU", [P, CTX])
        RE = sb("RE", [P, CTX])
        rsmax = sb("rsmax", [P, 1])
        rm = sb("rm", [P, 1])
        rna = sb("rna", [P, 1])
        rsum = sb("rsum", [P, 1])
        rln = sb("rln", [P, 1])
        rm8 = sb("rm8", [P, 8])
        qhalf = sb("qhalf", [P, P])
        kvcode = sb("kvcode", [P, 4, KV_ROWS])
        qrow_t = sb("qrow_t", [P, Q_ROWS])
        qcode = sb("qcode", [P, BLK, G * B])
        rcount = sb("rcount", [P, BLK, G * B])
        rcnt = sb("rcnt", [P, BLK, B])

        EARLY = 14080
        early = sb("early", [P, EARLY])
        STAGE = 14720
        stage = sb("stage", [P, STAGE])

        def part(region, at, shape):
            size = int(np.prod(shape))
            names = "abcd"[:len(shape)]
            v = region[:, at:at + size]
            if len(shape) == 1:
                return v, at + size
            spec = f"p ({' '.join(names)}) -> p {' '.join(names)}"
            return v.rearrange(spec, **{n: s for n, s in zip(names, shape)}), at + size

        o = 0
        xnT, o = part(early, o, [B, N])
        xlnT, o = part(early, o, [B, N])
        xln, o = part(early, o, [B * 7, D])
        wqk, o = part(early, o, [PAIRS, 2 * P])
        W2B, o = part(early, o, [H, D])
        GA, o = part(early, o, [HA, D])
        wvT, o = part(early, o, [HA, D])
        assert o <= EARLY, o

        o = 0
        xn = sT[:].rearrange("p b (k d) -> p (b k) d", d=D)
        xh2 = loc[:].rearrange("p b (k d) -> p (b k) d", d=D)
        cq, o = part(stage, o, [G * PAIRS, D])
        ck, o = part(stage, o, [G * PAIRS, D])
        cv, o = part(stage, o, [G * PAIRS, D])
        co, o = part(stage, o, [G * PAIRS, D])
        bv, o = part(stage, o, [PAIRS, D])
        bo, o = part(stage, o, [PAIRS, D])
        aq, o = part(stage, o, [HA, D])
        ak, o = part(stage, o, [HA, D])
        nkb, o = part(stage, o, [G, PAIRS, H])
        nvb, o = part(stage, o, [G, PAIRS, H])
        RTk, o = part(stage, o, [B, KV_ROWS])
        RTq, o = part(stage, o, [WQ * B, Q_ROWS])
        assert o <= STAGE, o
        stats = sb("stats", [P, NB, 6])
        mv = sb("mv", [P, NB, 2])
        var3 = sb("var3", [P, 3, NB])
        rs3 = sb("rs3", [P, 3, NB])
        tmp3 = sb("tmp3", [P, 3, NB])

        o = 0
        yT, o = part(stage, o, [2, N])
        vN, o = part(stage, o, [2, BLK, D])
        simA, o = part(stage, o, [2, 3, N])

        o = 0
        r1, o = part(stage, o, [2, BLK, 4, DH])
        r2, o = part(stage, o, [2, BLK, 4, DH])
        rot, o = part(stage, o, [2, BLK, 2 * P])
        qbd, o = part(stage, o, [NW, P])
        kT, o = part(stage, o, [N])
        pB, o = part(stage, o, [2, NW, P])
        pTB, o = part(stage, o, [2, NW, P])
        axB, o = part(stage, o, [2, NW, P])
        nmB = sb("nmB", [P, 2, NW])
        rsB = sb("rsB", [P, 2, NW])
        riB = sb("riB", [P, NW])
        assert o <= STAGE, o

        o = 0
        U, o = part(early, o, [WQ, H, NQ])
        axC, o = part(early, o, [H, WQ, NQ])
        pC, o = part(early, o, [2, 4, P])
        pTC, o = part(early, o, [2, 4 * P])
        XN, o = part(early, o, [4, D])
        XT, o = part(early, o, [2, P])
        OH, o = part(early, o, [2, 4, P])
        qsel, o = part(early, o, [G, B, 2 * P])
        qrep, o = part(early, o, [WQ, 4, NQ])
        ntmp, o = part(early, o, [WQ, H])
        assert o <= EARLY, o
        o = 0
        oT, o = part(stage, o, [B, BLK, G, W])
        OHQ, o = part(stage, o, [NB, P])
        OHS, o = part(stage, o, [2, BLK, P])
        oN, o = part(stage, o, [2, BLK, D])
        sN, o = part(stage, o, [2, BLK, D])
        yN, o = part(stage, o, [2, BLK, D])
        eN, o = part(stage, o, [2, BLK, D])
        res, o = part(stage, o, [NB, D])
        assert o <= STAGE, o
        nsC = sb("nsC", [P, WQ * 4])
        nmC = sb("nmC", [P, 2, 4])
        dnC = sb("dnC", [P, 2, 4])
        pnC = sb("pnC", [P, 2, 4])
        rsC = sb("rsC", [P, 2, 4])
        riC = sb("riC", [P, 4])
        pnall = sb("pnall", [P, WQ * 4])
        pn16 = sb("pn16", [P, WQ * 4, 4])
        pnT = sb("pnT", [H, WQ * NQ])

        ps = ctx.enter_context(nc.psum_tensor("ps", [P, 8, N], F32))

        s_x = [sem(f"s_x{b}") for b in range(B)]
        s_const = sem("s_const")
        s_wa = sem("s_wa")
        s_wb = sem("s_wb")
        s_wv = sem("s_wv")
        s_wqk = sem("s_wqk")
        s_wc = sem("s_wc")
        s_null = sem("s_null")
        s_cleared = sem("s_cleared")
        s_rt = sem("s_rt")
        s_var = sem("s_var")
        s_ln = sem("s_ln")
        s_xn = sem("s_xn")
        s_xh2 = sem("s_xh2")
        s_xhat = sem("s_xhat")
        s_bf = sem("s_bf")
        prep_out = sem("prep_out")
        prep_in = sem("prep_in")
        logits = sem("logits")
        r_start = sem("r_start")
        r_u = sem("r_u")
        r_l = sem("r_l")
        g_loaded = sem("g_loaded")
        y_out = sem("y_out")
        y_in = sem("y_in")
        v_out = sem("v_out")
        v_in = sem("v_in")
        sc_out = sem("sc_out")
        relu_in = sem("relu_in")
        diag_in = sem("diag_in")
        pv_done = sem("pv_done")
        sT_in = sem("sT_in")
        codes = sem("codes")
        qk_out = sem("qk_out")
        roped = sem("roped")
        rot_in = sem("rot_in")
        qkT_out = sem("qkT_out")
        qkT_in = sem("qkT_in")
        sim_out = sem("sim_out")
        max_in = sem("max_in")
        exp_in = sem("exp_in")
        norm_in = sem("norm_in")
        pT_out = sem("pT_out")
        pT_in = sem("pT_in")
        ax_out = sem("ax_out")
        ax_in = sem("ax_in")
        w2_loaded = sem("w2_loaded")
        out_out = sem("out_out")
        loc_in = sem("loc_in")
        loc_zero = sem("loc_zero")
        qbd_zero = sem("qbd_zero")
        code_out = sem("code_out")
        ohq_in = sem("ohq_in")
        qsel_out = sem("qsel_out")
        qsel_in = sem("qsel_in")
        rep_in = sem("rep_in")
        oT_zero = sem("oT_zero")
        u_out = sem("u_out")
        u_act = sem("u_act")
        u_dve = sem("u_dve")
        null_out = sem("null_out")
        null_in = sem("null_in")
        oh_in = sem("oh_in")
        gx_out = sem("gx_out")
        xn_in = sem("xn_in")
        xt_out = sem("xt_out")
        xt_in = sem("xt_in")
        csim_out = sem("csim_out")
        cmax_in = sem("cmax_in")
        cexp_in = sem("cexp_in")
        cnorm_in = sem("cnorm_in")
        cpT_out = sem("cpT_out")
        cpT_in = sem("cpT_in")
        cax_out = sem("cax_out")
        cax_in = sem("cax_in")
        pn16_in = sem("pn16_in")
        pnT_out = sem("pnT_out")
        pnT_in = sem("pnT_in")
        cout_out = sem("cout_out")
        cout_in = sem("cout_in")
        ft_out = sem("ft_out")
        ft_act = sem("ft_act")
        ft_dve = sem("ft_dve")
        fin_out = sem("fin_out")
        y_ready = sem("y_ready")
        e_ready = sem("e_ready")
        res_in = sem("res_in")
        s_out = sem("s_out")

        N_CONST = len(CONSTS) + 7

        def at_least(eng, s, n):
            if not isinstance(n, int) or n > 0:
                eng.wait_ge(s, n)

        def sweep(eng, n, body):
            body(0, True, False)
            with eng.Fori(1, n - 1) as i:
                body(i, False, False)
            body(n - 1, False, True)

        def sequences(eng, g, body):
            if g == 0:
                body(0, 0)
            with eng.Fori(1 if g == 0 else 0, B) as b:
                body(b, b + g * B)

        A_STEPS = [[(m, m * P, m * P, (m + 1) * P) for m in range(BLK)],
                   [(0, 0, P, N), (2, 3 * P, 3 * P, N)],
                   [(1, 0, 2 * P, N)]]

        block = ctx.enter_context(nc.Block())

        J_GA, J_W2B, J_G2, J_W2C, J_NULL, J_XLN, J_END = 8, 10, 14, 22, 30, 31, 38

        @block.sync
        def _(sp):
            xv = dram["x"].rearrange("b (k p) d -> p (b k) d", p=P)
            for b in range(B):
                sp.dma_start(x[:, b * BLK:(b + 1) * BLK, :], xv[:, b * BLK:(b + 1) * BLK, :]).then_inc(s_x[b], 16)
            tiles = [ident, causal, cos, sin, windowf, rmask, rinvk, half, eps, iota, own, fold]
            for name, t in zip(CONSTS, tiles):
                sp.dma_start(t[:], dram[name]).then_inc(s_const, 16)
            sp.dma_start(lng[:], dram["ln_g"]).then_inc(s_const, 16)
            sp.dma_start(lnb[:], dram["ln_b"]).then_inc(s_const, 16)
            sp.dma_start(qg[:], dram["qg"]).then_inc(s_const, 16)
            sp.dma_start(cg[:], dram["cg"].partition_broadcast(P)).then_inc(s_const, 16)
            sp.dma_start(rtq[:], dram["rt_q"]).then_inc(s_const, 16)
            sp.dma_start(rtk[:], dram["rt_kv"]).then_inc(s_const, 16)
            sp.dma_start(nkv[:], dram["null"]).then_inc(s_const, 16)
            sp.dma_start(aq[:], dram["Wq"].rearrange("h e d -> e h d")).then_inc(s_wa, 16)
            sp.dma_start(ak[:], dram["Wk"].rearrange("h e d -> e h d")).then_inc(s_wa, 16)
            sp.dma_start(bv, dram["bv"]).then_inc(s_wb, 16)
            sp.dma_start(bo, dram["bo"]).then_inc(s_wb, 16)
            for t, name in ((cq, "cq"), (ck, "ck"), (cv, "cv"), (co, "co")):
                sp.dma_start(t, dram[name]).then_inc(s_wc, 16)
            sp.dma_start(wvT, dram["WvT"]).then_inc(s_wv, 16)
            sp.dma_start(wqk, dram["wqk"]).then_inc(s_wqk, 16)
            ov = out.rearrange("b (k p) d -> p (b k) d", p=P)
            for b in range(B):
                sp.wait_ge(res_in, b + 1)
                sp.dma_start(ov[:, b * BLK:(b + 1) * BLK, :], res[:, b * BLK:(b + 1) * BLK, :]).then_inc(s_out, 16)
            sp.wait_ge(s_out, 16 * B)

        @block.gpsimd
        def _(pool):
            pool.memset(nkb, 0.0).then_inc(s_cleared, 1)
            pool.memset(nvb, 0.0).then_inc(s_cleared, 1)
            pool.memset(RTk, 0.0).then_inc(s_cleared, 1)
            pool.memset(RTq, 0.0).then_inc(s_cleared, 1)
            pool.wait_ge(s_cleared, 4)
            pool.wait_ge(s_const, 16 * N_CONST)
            flat = RTk.rearrange("p b r -> p (b r)")
            for w in range(KV_W0, WQ):
                for g in range(G):
                    at = kv_row(w, g, 0)
                    pool.tensor_copy(flat[:, at:at + (B - 1) * (KV_ROWS + 1) + 1:KV_ROWS + 1],
                                     rtk[:, g:g + 1].broadcast_to([P, B]))
            flat = RTq.rearrange("p c r -> p (c r)")
            for w in range(WQ):
                for g in range(G):
                    at = w * B * Q_ROWS + q_row(w, g, 0)
                    last = pool.tensor_copy(flat[:, at:at + (B - 1) * (Q_ROWS + 1) + 1:Q_ROWS + 1],
                                            rtq[:, g:g + 1].broadcast_to([P, B]))
            pool.drain()
            pool.tensor_copy(identb[:], ident[:]).then_inc(s_rt, 1)
            for i, t in enumerate((nkb, nvb)):
                for hf in range(2):
                    rows = slice(hf * DH, (hf + 1) * DH)
                    pool.drain()
                    for g in range(G):
                        flat = t[rows, g].rearrange("p a b -> p (a b)")
                        last = pool.tensor_copy(flat[:, hf::H + 2], nkv[rows, i, g, :])
            last.then_inc(s_null, 1)
            pool.drain()
            pool.memset(zerob[:], 0.0)
            pool.tensor_copy(windowb[:], windowf[:]).then_inc(s_bf, 1)

            pool.wait_ge(prep_in, J_GA + 2)

            def head(h, first, last):
                if not first:
                    pool.wait_ge(y_out, 4 * h)
                pool.tensor_copy(gscr[:], GA[:, h, :]).then_inc(g_loaded, 1)
            sweep(pool, HA, head)

            pool.wait_ge(pv_done, 1)
            pool.memset(qbd, 0.0).then_inc(qbd_zero, 1)
            pool.memset(loc[:], 0.0).then_inc(loc_zero, 1)

            def add(p, b, ahead):
                u = 4 * p + b + ahead
                k = (b + ahead) % 2
                pool.wait_ge(roped, u + 1)
                at_least(pool, qkT_out, u - 1)
                pool.tensor_tensor(rot[:, k].rearrange("p a b -> p (a b)"),
                                   r1[:, k].rearrange("p a b c -> p (a b c)"),
                                   r2[:, k].rearrange("p a b c -> p (a b c)"), ALU.add).then_inc(rot_in, 1)

            def w2_load(p):
                if not isinstance(p, int) or p > 0:
                    pool.wait_ge(out_out, 4 * p)
                pool.tensor_copy(wscr[:], W2B[:, bass.ts(p, 2), :]).then_inc(w2_loaded, 1)

            add(0, 0, 0)
            add(0, 0, 1)

            def pair(p, first, last):
                for b in range(UNITS):
                    if not (last and b >= 2):
                        add(p, b, 2)
                    if b == 0:
                        w2_load(p)
            sweep(pool, PAIRS, pair)

            pool.wait_ge(loc_in, UNITS * PAIRS)
            pool.memset(oT[:], 0.0).then_inc(oT_zero, 1)
            for g in range(G):
                pool.wait_ge(qsel_in, B)
                def sequence(b, it):
                    at_least(pool, null_out, it)
                    src = qsel[:, g, bass.ds(b, 1), NQ:].rearrange("p o (w q) -> p (o w) q", q=NQ)
                    for r in range(4):
                        c = pool.tensor_copy(qrep[:, :, r, :], src)
                    c.then_inc(rep_in, 1)
                sequences(pool, g, sequence)

        @block.tensor
        def _(pe):
            def bank(i, n=1):
                return ps[:, i] if n == 1 else ps[:, i:i + n]

            def job(k):
                at_least(pe, prep_in, k - 3)
                return bank(4 + k % 4)

            pe.wait_ge(s_const, 16 * N_CONST)
            for b in range(B):
                to = job(b)
                pe.wait_ge(s_xn, b + 1)
                for k in range(BLK):
                    t = pe.transpose(to[:, k * P:(k + 1) * P], xn[:, b * BLK + k, :], ident[:])
                t.then_inc(prep_out, 1)
            for b in range(B):
                to = job(4 + b)
                pe.wait_ge(s_xh2, b + 1)
                for k in range(BLK):
                    t = pe.transpose(to[:, k * P:(k + 1) * P], xh2[:, b * BLK + k, :], ident[:])
                t.then_inc(prep_out, 1)
            pe.wait_ge(prep_in, 4)
            pe.wait_ge(s_rt, 1)
            for b in range(B):
                t = pe.matmul(ps[0:KV_ROWS, 0, 0:CTX], RTk[:, b, :], xnT[:, b, 0:CTX],
                              start=(b == 0), stop=(b == B - 1))
            t.then_inc(logits, 1)
            for w in range(WQ):
                for b in range(B):
                    t = pe.matmul(ps[Q_AT:Q_AT + Q_ROWS, 1, 0:W], RTq[:, w * B + b, :],
                                  xnT[:, b, W * (w + 1):W * (w + 2)],
                                  start=(w == 0 and b == 0), stop=(w == WQ - 1 and b == B - 1))
            t.then_inc(logits, 1)
            pe.wait_ge(s_wa, 32)
            for j in range(2):
                to = job(J_GA + j)
                for k in range(4):
                    t = pe.matmul(to[:, k * D:(k + 1) * D], aq[:, 4 * j + k, :], ak[:, 4 * j + k, :],
                                  start=True, stop=True)
                t.then_inc(prep_out, 1)

            def products(j0, n, lhs, rhs):
                for j in range(n):
                    to = job(j0 + j)
                    for k in range(4):
                        h = 8 * (j // 2) + 2 * k + j % 2
                        rows = slice(DH * (h % 2), DH * (h % 2 + 1))
                        t = pe.matmul(to[:, k * D:(k + 1) * D], lhs[rows, h // 2, :], rhs[rows, h // 2, :],
                                      start=True, stop=True)
                    t.then_inc(prep_out, 1)

            pe.wait_ge(s_wb, 32)
            products(J_W2B, 4, bv, bo)
            pe.wait_ge(s_wc, 64)
            products(J_G2, 8, cq, ck)
            products(J_W2C, 8, cv, co)
            to = job(J_NULL)
            pe.wait_ge(s_null, 1)
            for g in range(G):
                for p in range(PAIRS):
                    pe.matmul(to[:, g * H:(g + 1) * H], cq[:, g * PAIRS + p, :], nkb[:, g, p, :],
                              start=(p == 0), stop=(p == PAIRS - 1))
                for p in range(PAIRS):
                    t = pe.matmul(to[0:H, P * (g + 1):P * (g + 2)], nvb[:, g, p, :], co[:, g * PAIRS + p, :],
                                  start=(p == 0), stop=(p == PAIRS - 1))
            t.then_inc(prep_out, 1)
            for j in range(7):
                to = job(J_XLN + j)
                for k in range(4):
                    b, w = divmod(4 * j + k, 7)
                    t = pe.transpose(to[:, k * P:(k + 1) * P], xlnT[:, b, W * w:W * w + P], ident[:])
                t.then_inc(prep_out, 1)

            pe.wait_ge(prep_in, J_END)
            pe.wait_ge(r_start, 1)
            pe.wait_ge(s_wv, 16)
            pe.wait_ge(s_bf, 1)
            for b in range(B):
                pe.matmul(bank(b), identb[:], zerob[:], start=True, stop=False)

            def a_y(h, b):
                u = 4 * h + b
                pe.wait_ge(g_loaded, h + 1)
                at_least(pe, v_in, u)
                pe.matmul(bank(7), gscr[:], xnT[:, b, :], start=True, stop=True).then_inc(y_out, 1)

            def a_v(h, b):
                u = 4 * h + b
                pe.wait_ge(y_in, u + 1)
                for k in range(BLK):
                    t = pe.matmul(ps[:, 7, k * D:(k + 1) * D], xnT[:, b, k * P:(k + 1) * P],
                                  wvT[:, bass.ds(h, 1), :].rearrange("p o d -> p (o d)"), start=True, stop=True)
                t.then_inc(v_out, 1)

            def a_scores(h, b, s):
                u = 4 * h + b
                if s == 0:
                    pe.wait_ge(y_in, u + 1)
                if s == 0:
                    at_least(pe, diag_in, u)
                else:
                    at_least(pe, relu_in, 2 * u + s - 2)
                for m, at, q0, q1 in A_STEPS[s]:
                    t = pe.matmul(ps[:, 4 + s, at:at + q1 - q0], xnT[:, b, m * P:(m + 1) * P],
                                  yT[:, b % 2, q0:q1], start=True, stop=True)
                t.then_inc(sc_out, 1)

            def a_sums(h, b, s):
                u = 4 * h + b
                if s == 0:
                    pe.wait_ge(v_in, u + 1)
                    pe.wait_ge(diag_in, u + 1)
                else:
                    pe.wait_ge(relu_in, 2 * u + s)
                for m, at, q0, q1 in A_STEPS[s]:
                    t = pe.matmul(ps[:, b, q0:q1], vN[:, b % 2, m, :], simA[:, b % 2, s, at:at + q1 - q0],
                                  start=False, stop=False, skip_group_check=True)
                return t

            a_y(0, 0)
            a_v(0, 0)

            def head(h, first, last):
                for b in range(UNITS):
                    nh, nb = (h, b + 1) if b < UNITS - 1 else (h + 1, 0)
                    more = not (last and b == UNITS - 1)
                    a_scores(h, b, 0)
                    if b > 0:
                        a_sums(h, b - 1, 2)
                    elif not first:
                        a_sums(h - 1, UNITS - 1, 2)
                    if more:
                        a_y(nh, nb)
                    a_scores(h, b, 1)
                    a_sums(h, b, 0)
                    if more:
                        a_v(nh, nb)
                    a_scores(h, b, 2)
                    a_sums(h, b, 1)
            sweep(pe, HA, head)
            a_sums(HA - 1, UNITS - 1, 2)
            for b in range(B):
                t = pe.matmul(bank(b), ident[:], xnT[:, b, :], start=False, stop=True)
            t.then_inc(pv_done, 1)

            pe.wait_ge(sT_in, B)
            pe.wait_ge(s_wqk, 16)
            pe.wait_ge(s_bf, 1)

            def b_project(p, b, ahead):
                u = 4 * p + b + ahead
                at_least(pe, roped, u)
                q, c = (p, b + ahead) if b + ahead < UNITS else (p + 1, b + ahead - UNITS)
                to = ps[:, 0:2].rearrange("p k (a n) -> p (k a) n", a=2)
                for k in range(BLK):
                    t = pe.matmul(to[:, k, :], xlnT[:, c, k * P:(k + 1) * P],
                                  wqk[:, bass.ds(q, 1), :].rearrange("p o n -> p (o n)"), start=True, stop=True)
                t.then_inc(qk_out, 1)

            def b_turn(p, b, ahead):
                u = 4 * p + b + ahead
                k = (b + ahead) % 2
                pe.wait_ge(rot_in, u + 1)
                at_least(pe, pT_in, u - 1)
                for i in range(2):
                    for t4 in range(BLK):
                        t = pe.transpose(ps[:, 2 + i, t4 * P:(t4 + 1) * P], rot[:, k, t4, i * P:(i + 1) * P],
                                         ident[:])
                t.then_inc(qkT_out, 1)

            def b_scores(p, b):
                u = 4 * p + b
                pe.wait_ge(qkT_in, 3 * u + 3)
                at_least(pe, exp_in, u)
                for i in range(2):
                    for k in range(4):
                        w = 4 * i + k
                        at = W * max(w - 1, 0)
                        pe.matmul(ps[:, 4 + i, k * P:(k + 1) * P], qbd[:, w, :], kT[:, at:at + P],
                                  start=(k == 0), stop=False)
                    t = pe.matmul(bank(4 + i), identb[:], windowb[:, i * P:i * P + N], start=False, stop=True)
                t.then_inc(sim_out, 1)

            def b_turn_probs(p, b, ahead_turned):
                u = 4 * p + b
                pe.wait_ge(norm_in, u + 1)
                if ahead_turned:
                    pe.wait_ge(qkT_in, 3 * u + 6)
                for w in range(NW):
                    t = pe.transpose(ps[:, 2 + w // 4, (w % 4) * P:(w % 4 + 1) * P], pB[:, b % 2, w, :], ident[:])
                t.then_inc(pT_out, 1)

            def b_mix(p, b, i):
                u = 4 * p + b
                pe.wait_ge(pT_in, u + 1)
                at_least(pe, ax_in, 2 * u + i)
                for k in range(4):
                    w = 4 * i + k
                    t = pe.matmul(ps[:, 6, k * P:(k + 1) * P], xln[:, b * 7 + max(w - 1, 0), :],
                                  pTB[:, b % 2, w, :], start=True, stop=True)
                t.then_inc(ax_out, 1)

            def b_out(p, b):
                u = 4 * p + b
                pe.wait_ge(w2_loaded, p + 1)
                at_least(pe, loc_in, u)
                pe.wait_ge(ax_in, 2 * u + 2)
                for hf in range(2):
                    t = pe.matmul(ps[:, 7].rearrange("p (w q) -> p w q", q=W), wscr[:, hf, :],
                                  axB[:, b % 2, :, hf * W:(hf + 1) * W], start=(hf == 0), stop=(hf == 1))
                t.then_inc(out_out, 1)

            b_project(0, 0, 0)
            b_project(0, 0, 1)
            b_turn(0, 0, 0)
            pe.wait_ge(qbd_zero, 1)

            def pair(p, first, last):
                for b in range(UNITS):
                    before = (p, b - 1) if b > 0 else (None if first else (p - 1, UNITS - 1))
                    b_scores(p, b)
                    turned = not (last and b == UNITS - 1)
                    if turned:
                        b_turn(p, b, 1)
                    if before:
                        b_mix(*before, 0)
                    if not (last and b >= 2):
                        b_project(p, b, 2)
                    if before:
                        b_mix(*before, 1)
                        b_out(*before)
                    b_turn_probs(p, b, turned)
            sweep(pe, PAIRS, pair)
            end = (PAIRS - 1, UNITS - 1)
            b_mix(*end, 0)
            b_mix(*end, 1)
            b_out(*end)

            pe.wait_ge(codes, 1)
            pe.wait_ge(loc_in, UNITS * PAIRS)
            for c in range(4):
                n = min(P, CTX - c * P)
                pe.transpose(ps[0:n, 4, c * KV_ROWS:(c + 1) * KV_ROWS], RE[0:KV_ROWS, c * P:c * P + n],
                             ident[0:KV_ROWS, 0:KV_ROWS])
            rows = slice(Q_AT, Q_AT + Q_ROWS)
            pe.transpose(ps[:, 5, 0:Q_ROWS], qhalf[rows, :], ident[rows, rows]).then_inc(code_out, 1)
            for b in range(B):
                pe.wait_ge(ohq_in, b + 1)
                for j in range(BLK):
                    t = pe.matmul(ps[:, b, j * P:(j + 1) * P], xhat[:, b * BLK + j, :], OHQ[:, b * BLK + j, :],
                                  start=True, stop=True)
                t.then_inc(qsel_out, 1)
            pe.wait_ge(qsel_in, B)

            for g in range(G):
                def sequence(b, it):
                    def gather(k):
                        n = 1 if k == 0 else (k + 3) // 2
                        at_least(pe, xn_in, it * 6 + k)
                        if k > 0:
                            at_least(pe, oh_in, it * 5 + k)
                        for c in range(n):
                            rows = P if k == 0 else min(P, W * (k + 2) - c * P)
                            onehot = ident[:] if k == 0 else OH[0:rows, k % 2, c, :]
                            t = pe.matmul(ps[:, 4, 0:D], onehot,
                                          xhat[0:rows, bass.ds(b * BLK + c, 1), :].rearrange("p o d -> p (o d)"),
                                          start=(c == 0), stop=(c == n - 1))
                        t.then_inc(gx_out, 1)

                    def turn(k):
                        at_least(pe, xn_in, it * 6 + k + 1)
                        at_least(pe, xt_in, it * 6 + k)
                        if k == 0:
                            at_least(pe, null_in, it + 1)
                        pe.transpose(ps[:, 2, P:2 * P], XN[:, k % 4, :], ident[:]).then_inc(xt_out, 1)

                    def scores(w):
                        k, n = max(w - 1, 0), (W if w == 0 else P)
                        at_least(pe, xt_in, it * 6 + k + 1)
                        if w >= 2:
                            at_least(pe, cexp_in, it * WQ + w - 1)
                        for hg in range(4):
                            t = pe.matmul(ps[:, 5 + w % 2, hg * P:hg * P + n],
                                          U[:, w, 4 * hg:4 * hg + 4, :].rearrange("p h q -> p (h q)"),
                                          XT[:, k % 2, 0:n], start=True, stop=True)
                        t.then_inc(csim_out, 1)

                    for s in range(8):
                        if s == 0:
                            at_least(pe, cax_in, it * WQ)
                        elif s % 2 == 0:
                            at_least(pe, u_act, it * 4 + s // 2)
                        elif s > 1:
                            at_least(pe, u_dve, it * 4 + s // 2)
                        for i in range(2):
                            t = pe.matmul(ps[:, s % 2, i * WQ * NQ:(i + 1) * WQ * NQ], G2[:, g * H + 2 * s + i, :],
                                          qsel[:, g, bass.ds(b, 1), NQ:].rearrange("p o n -> p (o n)"),
                                          start=True, stop=True)
                        t.then_inc(u_out, 1)
                    at_least(pe, rep_in, it + 1)
                    at_least(pe, pnT_in, it)
                    for w in range(WQ):
                        t = pe.matmul(ps[:, 2, w * H:(w + 1) * H], qrep[:, w].rearrange("p r q -> p (r q)"),
                                      NK[:, g, :], start=True, stop=True)
                    t.then_inc(null_out, 1)
                    gather(0)
                    turn(0)
                    gather(1)
                    at_least(pe, u_act, it * 4 + 4)
                    at_least(pe, u_dve, it * 4 + 4)
                    scores(0)
                    for w in range(WQ):
                        if w + 1 < WQ:
                            scores(w + 1)
                        if w + 1 <= 5:
                            turn(w + 1)
                        if w + 2 <= 5:
                            gather(w + 2)
                        n = W if w == 0 else P
                        at_least(pe, cnorm_in, it * WQ + w + 1)
                        at_least(pe, cpT_in, it * WQ + w)
                        for hg in range(4):
                            t = pe.transpose(ps[:, 7, hg * P:(hg + 1) * P], pC[:, w % 2, hg, :], ident[:])
                        t.then_inc(cpT_out, 1)
                        at_least(pe, cpT_in, it * WQ + w + 1)
                        if w >= 2:
                            at_least(pe, cax_in, it * WQ + w - 1)
                        pe.matmul(ps[:, w % 2, :], XN[0:n, max(w - 1, 0) % 4, :], pTC[0:n, w % 2, :],
                                  start=True, stop=True).then_inc(cax_out, 1)
                    at_least(pe, pn16_in, it + 1)
                    for w in range(WQ):
                        t = pe.matmul(ps[0:H, 2, 256 + w * NQ:256 + (w + 1) * NQ],
                                      pn16[:, 4 * w:4 * w + 4, :].rearrange("p a b -> p (a b)"), fold[:],
                                      start=True, stop=True)
                    t.then_inc(pnT_out, 1)
                    at_least(pe, cout_in, it)
                    at_least(pe, cax_in, it * WQ + WQ)
                    for h in range(H):
                        pe.matmul(ps[:, 3, 0:WQ * NQ], W2C[:, g * H + h, :],
                                  axC[:, h].rearrange("p w q -> p (w q)"), start=(h == 0), stop=False)
                    at_least(pe, pnT_in, it + 1)
                    pe.matmul(ps[:, 3, 0:WQ * NQ], NV[:, g, :], pnT[:], start=False, stop=True).then_inc(cout_out, 1)
                sequences(pe, g, sequence)

            pe.wait_ge(cout_in, G * B)
            for b in range(B):
                if b >= 1:
                    pe.wait_ge(ft_act, 2 * b)
                    pe.wait_ge(ft_dve, b)
                for j in range(BLK):
                    blk = b * BLK + j
                    to = slice(j * P, (j + 1) * P)
                    pe.transpose(ps[:, 0, to], OHQ[:, blk, :], ident[:])
                    pe.transpose(ps[:, 1, to], oT[:, b, j].rearrange("p g s -> p (g s)"), ident[:])
                    t = pe.transpose(ps[:, 2, to], sT[:, b, to], ident[:])
                t.then_inc(ft_out, 1)
                pe.wait_ge(ft_act, 2 * b + 2)
                pe.wait_ge(ft_dve, b + 1)
                if b >= 2:
                    pe.wait_ge(y_ready, b - 1)
                for j in range(BLK):
                    to = slice(j * P, (j + 1) * P)
                    pe.matmul(ps[:, 3 + b % 2, to], OHS[:, b % 2, j, :], oN[:, b % 2, j, :], start=True, stop=False)
                    t = pe.matmul(ps[:, 3 + b % 2, to], loc[:, b, to], ident[:], start=False, stop=True)
                t.then_inc(fin_out, 1)

        @block.scalar
        def _(act):
            act.preload_act_table_set("natural_log_exp_and_others")
            act.wait_ge(s_var, 1)
            act.activation(tmp3[:, 0, :], var3[:, 0, :], ACT.Ln)
            act.drain()
            act.activation(rs3[:, 0, :], tmp3[:, 0, :], ACT.Exp, scale=-0.5).then_inc(s_ln, 1)
            act.wait_ge(s_var, 2)
            act.activation(tmp3[:, 1:3, :], var3[:, 1:3, :], ACT.Ln)
            act.drain()
            act.activation(rs3[:, 1:3, :], tmp3[:, 1:3, :], ACT.Exp, scale=-0.5).then_inc(s_ln, 1)
            act.wait_ge(s_const, 16 * N_CONST)

            def job(k):
                act.wait_ge(prep_out, k + 1)
                return ps[:, 4 + k % 4, :]

            for b in range(B):
                act.activation(xnT[:, b, :], job(b), ACT.Copy).then_inc(prep_in, 1)
            for b in range(B):
                act.activation(xlnT[:, b, :], job(4 + b), ACT.Identity, bias=lnb[:, 0:1],
                               scale=lng[:, 0:1]).then_inc(prep_in, 1)

            def evacuate(j0, n, to):
                for j in range(n):
                    act.activation(to[:, 4 * j:4 * j + 4, :], job(j0 + j).rearrange("p (a b) -> p a b", b=D),
                                   ACT.Copy).then_inc(prep_in, 1)
            evacuate(J_GA, 2, GA)

            def evacuate_products(j0, n, to):
                for j in range(n):
                    at = 8 * (j // 2) + j % 2
                    act.activation(to[:, at:at + 7:2, :], job(j0 + j).rearrange("p (a b) -> p a b", b=D),
                                   ACT.Copy).then_inc(prep_in, 1)
            evacuate_products(J_W2B, 4, W2B)
            evacuate_products(J_G2, 8, G2)
            evacuate_products(J_W2C, 8, W2C)
            null = job(J_NULL)
            act.activation(NK[:], null[:, 0:G * H].rearrange("p (g h) -> p g h", g=G), ACT.Copy)
            act.activation(NV[:], null[0:H, P:P * (1 + G)].rearrange("p (g d) -> p g d", g=G),
                           ACT.Copy).then_inc(prep_in, 1)
            evacuate(J_XLN, 7, xln)

            act.wait_ge(r_start, 1)

            def descend(i, first=False):
                if not first:
                    act.wait_ge(r_u, i)
                act.activation(RE[:], rmask[:] if first else RU[:], ACT.Exp, scale=eps[:, 0, bass.ds(i, 1)],
                               accum_out=rsum[:])
                act.drain()
                act.activation(rln[:], rsum[:], ACT.Ln, scale=rinvk[:, 0:1]).then_inc(r_l, 1)

            def a_y(h, b):
                act.wait_ge(y_out, 4 * h + b + 1)
                act.activation(yT[:, b % 2, :], ps[:, 7, :], ACT.Copy).then_inc(y_in, 1)

            def a_relu(h, b, s):
                act.wait_ge(sc_out, 3 * (4 * h + b) + s + 1)
                n = (N, 2 * P)[s - 1]
                act.activation(simA[:, b % 2, s, 0:n], ps[:, 4 + s, 0:n], ACT.Relu,
                               scale=1.0 / N).then_inc(relu_in, 1)

            a_y(0, 0)

            def head(h, first, last):
                for b in range(UNITS):
                    if not (last and b == UNITS - 1):
                        a_y(*((h, b + 1) if b < UNITS - 1 else (h + 1, 0)))
                    a_relu(h, b, 1)
                    a_relu(h, b, 2)
                    if first and b in (1, 2):
                        descend(b - 1, first=(b == 1))
                    if not first and not last and b < 3:
                        descend(3 * h - 1 + b)
            sweep(act, HA, head)
            act.wait_ge(pv_done, 1)
            for b in range(B):
                act.activation(sT[:, b, :], ps[:, b, :], ACT.Copy).then_inc(sT_in, 1)

            def b_turned(p, b, ahead):
                u = 4 * p + b + ahead
                act.wait_ge(qkT_out, u + 1)
                at_least(act, sim_out, u)
                q = ps[:, 2, :].rearrange("p (w q) -> p w q", q=W)
                act.activation(kT, ps[:, 3, :], ACT.Copy).then_inc(qkT_in, 1)
                for hf in range(2):
                    rows = slice(DH * hf, DH * (hf + 1))
                    act.activation(qbd[rows, :, W * hf:W * (hf + 1)], q[rows], ACT.Copy,
                                   scale=SCALE).then_inc(qkT_in, 1)

            def b_exp(p, b, i):
                u = 4 * p + b
                if i == 0:
                    act.wait_ge(max_in, u + 1)
                    at_least(act, pT_out, u - 1)
                for w in range(4 * i, 4 * i + 4):
                    t = act.activation(pB[:, b % 2, w, :], ps[:, 4 + w // 4, (w % 4) * P:(w % 4 + 1) * P], ACT.Exp,
                                       bias=nmB[:, b % 2, w:w + 1], accum_out=rsB[:, b % 2, w:w + 1])
                if i == 1:
                    t.then_inc(exp_in, 1)

            def b_mixed(p, b, i):
                u = 4 * p + b
                act.wait_ge(ax_out, 2 * u + i + 1)
                if i == 0:
                    at_least(act, out_out, u - 1)
                act.activation(axB[:, b % 2, 4 * i:4 * i + 4, :],
                               ps[:, 6, :].rearrange("p (w n) -> p w n", n=P), ACT.Copy).then_inc(ax_in, 1)

            act.wait_ge(qbd_zero, 1)
            b_turned(0, 0, 0)

            def pair(p, first, last):
                for b in range(UNITS):
                    before = (p, b - 1) if b > 0 else (None if first else (p - 1, UNITS - 1))
                    b_exp(p, b, 0)
                    if before:
                        b_mixed(*before, 0)
                    b_exp(p, b, 1)
                    if before:
                        b_mixed(*before, 1)
                    if not (last and b == UNITS - 1):
                        b_turned(p, b, 1)
            sweep(act, PAIRS, pair)
            b_mixed(PAIRS - 1, UNITS - 1, 0)
            b_mixed(PAIRS - 1, UNITS - 1, 1)

            act.wait_ge(out_out, UNITS * PAIRS)
            for g in range(G):
                def sequence(b, it):
                    def turned(k):
                        at_least(act, xt_out, it * 6 + k + 1)
                        act.activation(XT[:, k % 2, :], ps[:, 2, P:2 * P], ACT.Copy).then_inc(xt_in, 1)

                    def probs(w):
                        n = W if w == 0 else P
                        at_least(act, cmax_in, it * WQ + w + 1)
                        if w >= 2:
                            at_least(act, cpT_out, it * WQ + w - 1)
                        for hg in range(4):
                            act.activation(pC[:, w % 2, hg, 0:n], ps[:, 5 + w % 2, hg * P:hg * P + n], ACT.Exp,
                                           bias=nmC[:, w % 2, hg:hg + 1], accum_out=rsC[:, w % 2, hg:hg + 1])
                        act.activation(pnC[:, w % 2, :], dnC[:, w % 2, :], ACT.Exp).then_inc(cexp_in, 1)

                    for s in range(0, 8, 2):
                        at_least(act, u_out, it * 8 + s + 1)
                        act.activation(U[:, :, 2 * s:2 * s + 2, :].rearrange("p w h q -> p h w q"),
                                       ps[:, 0, 0:2 * WQ * NQ].rearrange("p (h w q) -> p h w q", h=2, q=NQ),
                                       ACT.Copy, scale=SCALE).then_inc(u_act, 1)
                    turned(0)
                    probs(0)
                    for w in range(WQ):
                        if w + 1 <= 5:
                            turned(w + 1)
                        if w + 1 < WQ:
                            probs(w + 1)
                        at_least(act, cax_out, it * WQ + w + 1)
                        act.activation(axC[:, :, w, :], ps[:, w % 2, :].rearrange("p (h q) -> p h q", q=NQ),
                                       ACT.Copy).then_inc(cax_in, 1)
                    at_least(act, pnT_out, it + 1)
                    act.activation(pnT[:], ps[0:H, 2, 256:256 + WQ * NQ], ACT.Copy).then_inc(pnT_in, 1)
                sequences(act, g, sequence)

            for b in range(B):
                act.wait_ge(ft_out, b + 1)
                if b >= 2:
                    act.wait_ge(fin_out, b - 1)
                for t, i in ((OHS, 0), (oN, 1)):
                    act.activation(t[:, b % 2], ps[:, i, :].rearrange("p (j n) -> p j n", j=BLK),
                                   ACT.Copy).then_inc(ft_act, 1)
                act.wait_ge(y_ready, b + 1)
                if b >= 2:
                    act.wait_ge(res_in, b - 1)
                act.activation(eN[:, b % 2], yN[:, b % 2], ACT.Exp, scale=-1.0).then_inc(e_ready, 1)

        @block.vector
        def _(dve):
            def rsqrt_step(n0, n1):
                r, v, t = rs3[:, n0:n1], var3[:, n0:n1], tmp3[:, n0:n1]
                dve.tensor_tensor(t, r, r, ALU.mult)
                dve.drain()
                dve.tensor_tensor(t, t, v, ALU.mult)
                dve.drain()
                dve.tensor_scalar(t, t, -0.5, 1.5, ALU.mult, ALU.add)
                dve.drain()
                dve.tensor_tensor(r, r, t, ALU.mult)
                dve.drain()

            for b in range(B):
                dve.wait_ge(s_x[b], 16)
                for k in range(b * BLK, (b + 1) * BLK):
                    dve.bn_stats(stats[:, k, :], x[:, k, :])
            dve.drain()
            for k in range(NB):
                dve.bn_aggr(mv[:, k, :], stats[:, k, :])
            dve.drain()
            dve.tensor_scalar(var3[:, 0, :], mv[:, :, 1], 1e-5, None, ALU.add).then_inc(s_var, 1)
            dve.wait_ge(s_ln, 1)
            rsqrt_step(0, 1)
            for k in range(NB):
                t = dve.tensor_scalar(xn[:, k, :], x[:, k, :], mv[:, k, 0:1], rs3[:, 0, k:k + 1],
                                      ALU.subtract, ALU.mult)
                if k % BLK == BLK - 1:
                    t.then_inc(s_xn, 1)
            dve.tensor_tensor(tmp3[:, 0, :], rs3[:, 0, :], rs3[:, 0, :], ALU.mult)
            dve.drain()
            dve.tensor_tensor(tmp3[:, 0, :], tmp3[:, 0, :], mv[:, :, 1], ALU.mult)
            dve.drain()
            dve.tensor_scalar(var3[:, 1, :], tmp3[:, 0, :], 1e-5, None, ALU.add)
            dve.tensor_scalar(var3[:, 2, :], tmp3[:, 0, :], 1e-24 / D, 2.0**40, ALU.max, ALU.mult).then_inc(s_var, 1)
            dve.wait_ge(s_ln, 2)
            rsqrt_step(1, 3)
            for k in range(NB):
                t = dve.tensor_scalar(xh2[:, k, :], xn[:, k, :], rs3[:, 1, k:k + 1], None, ALU.mult)
                if k % BLK == BLK - 1:
                    t.then_inc(s_xh2, 1)
            for k in range(NB):
                t = dve.tensor_scalar(xhat[:, k, :], xn[:, k, :], rs3[:, 2, k:k + 1], 2.0**20, ALU.mult, ALU.mult)
            t.then_inc(s_xhat, 1)
            dve.wait_ge(s_const, 16 * N_CONST)
            dve.memset(RS[:], 0.0)
            dve.drain()
            qrows = slice(Q_AT, Q_AT + Q_ROWS)
            dve.tensor_copy(RS[qrows, W:], rmask[qrows, W:])
            dve.wait_ge(logits, 2)
            dve.tensor_tensor(RS[0:KV_ROWS, :], ps[0:KV_ROWS, 0, 0:CTX], rmask[0:KV_ROWS, :], ALU.add)
            dve.tensor_copy(RS[qrows, 0:W], ps[qrows, 1, 0:W])
            dve.drain()
            dve.tensor_reduce(rsmax[:], RS[:], AX.X, ALU.max)
            dve.memset(rm[:], 0.0)
            dve.drain()
            dve.nop().then_inc(r_start, 1)

            def new_bound(i):
                dve.wait_ge(r_l, i + 1)
                dve.tensor_scalar(rna[:], rln[:], eps[:, 1, bass.ds(i, 1)], rm[:, 0:1], ALU.mult, ALU.add)
                dve.drain()

            def descend(i):
                new_bound(i - 1)
                dve.tensor_tensor(rm[:], rsmax[:], rna[:], ALU.min)
                dve.drain()
                dve.tensor_scalar(RU[:], RS[:], rna[:, 0:1], rm[:, 0:1], ALU.min, ALU.subtract).then_inc(r_u, 1)

            def pick(rows, n):
                dve.max(rm8[rows, :], RU[rows, 0:n])
                dve.drain()
                dve.match_replace(RU[rows, 0:n], rm8[rows, :], RU[rows, 0:n], TAKEN)
                dve.drain()

            def a_v(h, b):
                dve.wait_ge(v_out, 4 * h + b + 1)
                dve.tensor_copy(vN[:, b % 2], ps[:, 7, :].rearrange("p (k d) -> p k d", d=D)).then_inc(v_in, 1)

            def a_diag(h, b):
                dve.wait_ge(sc_out, 3 * (4 * h + b) + 1)
                blocks = lambda t: t.rearrange("p (m n) -> p m n", n=P)
                dve.scalar_tensor_tensor(out=blocks(simA[:, b % 2, 0, :]), in0=blocks(ps[:, 4, :]), scalar=0.0,
                                         in1=causal[:].unsqueeze(1).broadcast_to([P, BLK, P]),
                                         op0=ALU.max, op1=ALU.mult).then_inc(diag_in, 1)

            a_v(0, 0)

            def head(h, first, last):
                for b in range(UNITS):
                    a_diag(h, b)
                    if not (last and b == UNITS - 1):
                        a_v(*((h, b + 1) if b < UNITS - 1 else (h + 1, 0)))
                    if first and b == 2:
                        descend(1)
                    if not first and not last and b < 3:
                        descend(3 * h - 1 + b)
                    if last:
                        if b == 0:
                            new_bound(NITER - 1)
                            dve.tensor_scalar(RU[:], RS[:], rna[:, 0:1], 0.0, ALU.subtract, ALU.min)
                            dve.drain()
                            dve.tensor_scalar(RU[:], RU[:], 1.0 / EPS[NITER], LOWEST, ALU.mult, ALU.max)
                            dve.drain()
                        for _ in range(NKV // 8 // UNITS):
                            pick(slice(0, KV_ROWS), CTX)
                        pick(qrows, W)
            sweep(dve, HA, head)
            assert NQ // 8 == UNITS
            dve.tensor_scalar(RS[:], RU[:], TAKEN / 2, None, ALU.is_lt)
            dve.drain()
            dve.memset(RU[:], 1.0)
            dve.drain()
            dve.tensor_tensor_scan(RE[:], RU[:], RS[:], 0.0, ALU.mult, ALU.add)
            dve.drain()
            dve.scalar_tensor_tensor(out=RE[:], in0=RE[:], scalar=half[:, 0:1], in1=RS[:], op0=ALU.add, op1=ALU.mult)
            dve.drain()
            for i in range(2):
                t = dve.tensor_scalar(qhalf[qrows, i * W:(i + 1) * W], RE[qrows, 0:W], half[qrows, i + 1:i + 2],
                                      None, ALU.mult)
            t.then_inc(codes, 1)

            def b_rope(p, b, ahead):
                u = 4 * p + b + ahead
                k, c = (b + ahead) % 2, (b + ahead) % UNITS
                dve.wait_ge(qk_out, u + 1)
                at_least(dve, rot_in, u - 1)
                src = ps[:, 0:2].rearrange("p k (a h e) -> p (k a) h e", a=2, e=DH)
                e2 = DH // 2
                table = lambda t, lo, n: t[:, :, lo:lo + n].unsqueeze(2).broadcast_to([P, BLK, 4, n])
                dve.tensor_tensor(r1[:, k], src, table(cos, 0, DH), ALU.mult)
                dve.tensor_tensor(r2[:, k, :, :, 0:e2], src[:, :, :, e2:DH], table(sin, 0, e2), ALU.mult)
                dve.tensor_tensor(r2[:, k, :, :, e2:DH], src[:, :, :, 0:e2], table(sin, e2, e2),
                                  ALU.mult).then_inc(roped, 1)

            def b_max(p, b):
                dve.wait_ge(sim_out, 4 * p + b + 1)
                dve.tensor_reduce(nmB[:, b % 2, :], ps[:, 4:6].rearrange("p k (w n) -> p (k w) n", n=P), AX.X,
                                  ALU.max, negate=True).then_inc(max_in, 1)

            def b_norm(p, b):
                dve.wait_ge(exp_in, 4 * p + b + 1)
                dve.reciprocal(riB[:], rsB[:, b % 2, :])
                dve.drain()
                dve.tensor_tensor(pB[:, b % 2], pB[:, b % 2], riB[:].unsqueeze(2).broadcast_to([P, NW, P]),
                                  ALU.mult).then_inc(norm_in, 1)

            def b_probs(p, b):
                u = 4 * p + b
                dve.wait_ge(pT_out, u + 1)
                at_least(dve, ax_out, 2 * u - 2)
                dve.tensor_copy(pTB[:, b % 2], ps[:, 2:4].rearrange("p k (w n) -> p (k w) n", n=P)).then_inc(pT_in, 1)

            def b_add(p, b):
                dve.wait_ge(out_out, 4 * p + b + 1)
                dve.tensor_tensor(loc[:, b, :], loc[:, b, :], ps[:, 7, :], ALU.add).then_inc(loc_in, 1)

            dve.wait_ge(pv_done, 1)
            dve.wait_ge(loc_zero, 1)
            b_rope(0, 0, 0)
            b_rope(0, 0, 1)

            def pair(p, first, last):
                for b in range(UNITS):
                    before = (p, b - 1) if b > 0 else (None if first else (p - 1, UNITS - 1))
                    b_max(p, b)
                    if not (last and b >= 2):
                        b_rope(p, b, 2)
                    b_norm(p, b)
                    if before:
                        b_add(*before)
                    b_probs(p, b)
            sweep(dve, PAIRS, pair)
            b_add(PAIRS - 1, UNITS - 1)

            dve.wait_ge(code_out, 1)
            dve.memset(pC[:, 0], 0.0)
            dve.tensor_copy(kvcode[:, 0:3, :], ps[:, 4, 0:3 * KV_ROWS].rearrange("p (c r) -> p c r", c=3))
            dve.tensor_copy(kvcode[0:W, 3, :], ps[0:W, 4, 3 * KV_ROWS:4 * KV_ROWS])
            dve.tensor_copy(qrow_t[:], ps[:, 5, 0:Q_ROWS])
            dve.drain()
            gb = G * B
            dve.tensor_copy(qcode[:, 0, :], qrow_t[:, 0:gb])
            odd_even = qrow_t[:, gb:].rearrange("p (j o r) -> p j o r", o=2, r=gb)
            dve.tensor_tensor(qcode[:, 1:, :], odd_even[:, :, 0, :], odd_even[:, :, 1, :], ALU.add)
            dve.drain()
            for b in range(B):
                for j in range(BLK):
                    for g in range(G):
                        r = g * B + b
                        t = dve.tensor_scalar(OHQ[:, b * BLK + j, g * W:(g + 1) * W], iota[:, 0:W],
                                              qcode[:, j, r:r + 1], None, ALU.is_equal)
                t.then_inc(ohq_in, 1)
            dve.tensor_scalar(rcount[:], qcode[:], 0.5, None, ALU.is_gt)
            dve.drain()
            dve.tensor_tensor(rcnt[:], rcount[:, :, 0:B], rcount[:, :, B:], ALU.add)
            dve.drain()
            dve.tensor_scalar(rcnt[:], rcnt[:], 1.0, None, ALU.add)
            dve.drain()
            dve.reciprocal(rcnt[:], rcnt[:])
            for b in range(B):
                dve.wait_ge(qsel_out, b + 1)
                src = ps[:, b, :].rearrange("p (j g s) -> p j g s", g=G, s=W)
                for g in range(G):
                    t = dve.tensor_scalar(qsel[:, g, b, :].rearrange("p (j s) -> p j s", s=W), src[:, :, g, :],
                                          qg[:, g:g + 1], None, ALU.mult)
                t.then_inc(qsel_in, 1)
            dve.wait_ge(oT_zero, 1)

            for g in range(G):
                def sequence(b, it):
                    def onehots(k):
                        at_least(dve, gx_out, it * 6 + k - 1)
                        n = (k + 3) // 2
                        for c in range(n):
                            rows = min(P, W * (k + 2) - c * P)
                            col = (k + 1 - KV_W0) * gb + g * B
                            t = dve.tensor_scalar(OH[0:rows, k % 2, c, :], iota[0:rows, :],
                                                  kvcode[0:rows, c, bass.ds(b + col, 1)], None, ALU.is_equal)
                        t.then_inc(oh_in, 1)

                    def gathered(k):
                        at_least(dve, gx_out, it * 6 + k + 1)
                        dve.tensor_tensor(XN[:, k % 4, :], ps[:, 4, 0:D], cg[:, g, :], ALU.mult).then_inc(xn_in, 1)

                    def maxima(w):
                        n = W if w == 0 else P
                        at_least(dve, csim_out, it * WQ + w + 1)
                        nm = nmC[:, w % 2, :]
                        null = nsC[:, 4 * w:4 * w + 4]
                        dve.tensor_reduce(nm, ps[:, 5 + w % 2, :].rearrange("p (h n) -> p h n", n=P)[:, :, 0:n], AX.X,
                                          ALU.max, negate=True)
                        dve.drain()
                        dve.tensor_tensor(nm, nm, null, ALU.min)
                        dve.drain()
                        dve.tensor_tensor(dnC[:, w % 2, :], nm, null, ALU.subtract).then_inc(cmax_in, 1)

                    def norms(w):
                        n = W if w == 0 else P
                        at_least(dve, cexp_in, it * WQ + w + 1)
                        dve.tensor_tensor(riC[:], rsC[:, w % 2, :], pnC[:, w % 2, :], ALU.add)
                        dve.drain()
                        dve.reciprocal(riC[:], riC[:])
                        dve.drain()
                        dve.tensor_tensor(pnall[:, 4 * w:4 * w + 4], pnC[:, w % 2, :], riC[:], ALU.mult)
                        dve.tensor_tensor(pC[:, w % 2, :, 0:n], pC[:, w % 2, :, 0:n],
                                          riC[:].unsqueeze(2).broadcast_to([P, 4, n]), ALU.mult).then_inc(cnorm_in, 1)

                    for s in range(1, 8, 2):
                        at_least(dve, u_out, it * 8 + s + 1)
                        dve.tensor_scalar(U[:, :, 2 * s:2 * s + 2, :].rearrange("p w h q -> p h w q"),
                                          ps[:, 1, 0:2 * WQ * NQ].rearrange("p (h w q) -> p h w q", h=2, q=NQ),
                                          SCALE, None, ALU.mult).then_inc(u_dve, 1)
                    at_least(dve, null_out, it + 1)
                    dve.tensor_tensor(ntmp, ps[:, 2, 0:WQ * H].rearrange("p (w h) -> p w h", h=H),
                                      own[:].unsqueeze(1).broadcast_to([P, WQ, H]), ALU.mult)
                    dve.drain()
                    dve.tensor_reduce(nsC[:], ntmp.rearrange("p w (a b) -> p (w a) b", b=4), AX.X, ALU.add,
                                      negate=True)
                    dve.drain()
                    dve.tensor_scalar(nsC[:], nsC[:], SCALE, None, ALU.mult).then_inc(null_in, 1)
                    onehots(1)
                    gathered(0)
                    onehots(2)
                    gathered(1)
                    maxima(0)
                    for w in range(WQ):
                        if w + 1 < WQ:
                            maxima(w + 1)
                        if w + 3 <= 5:
                            onehots(w + 3)
                        if w + 2 <= 5:
                            gathered(w + 2)
                        norms(w)
                        at_least(dve, cpT_out, it * WQ + w + 1)
                        if w >= 2:
                            at_least(dve, cax_out, it * WQ + w - 1)
                        n = W if w == 0 else P
                        dve.tensor_copy(pTC[0:n, w % 2, :], ps[0:n, 7, :]).then_inc(cpT_in, 1)
                    dve.drain()
                    dve.tensor_tensor(pn16[:], pnall[:].unsqueeze(2).broadcast_to([P, WQ * 4, 4]),
                                      own[:, 0:4].unsqueeze(1).broadcast_to([P, WQ * 4, 4]),
                                      ALU.mult).then_inc(pn16_in, 1)
                    at_least(dve, cout_out, it + 1)
                    dve.tensor_copy(oT[:, bass.ds(b, 1), 0, g, NQ:].rearrange("p o s -> p (o s)"), ps[:, 3, 0:NQ])
                    dve.tensor_copy(oT[:, bass.ds(b, 1), 1:, g, :].rearrange("p o j s -> p (o j) s"),
                                    ps[:, 3, NQ:WQ * NQ].rearrange("p (j s) -> p j s", s=W)).then_inc(cout_in, 1)
                sequences(dve, g, sequence)

            for b in range(B):
                k = b % 2
                dve.wait_ge(ft_out, b + 1)
                dve.tensor_copy(sN[:, k], ps[:, 2, :].rearrange("p (j n) -> p j n", j=BLK)).then_inc(ft_dve, 1)
                dve.wait_ge(fin_out, b + 1)
                dve.tensor_tensor(yN[:, k], ps[:, 3 + k, :].rearrange("p (j n) -> p j n", j=BLK),
                                  rcnt[:, :, b:b + 1].broadcast_to([P, BLK, D]), ALU.mult).then_inc(y_ready, 1)
                dve.wait_ge(e_ready, b + 1)
                dve.drain()
                dve.tensor_tensor(sN[:, k], sN[:, k], yN[:, k], ALU.mult)
                dve.tensor_scalar(eN[:, k], eN[:, k], 1.0, None, ALU.add)
                dve.drain()
                dve.reciprocal(eN[:, k], eN[:, k])
                dve.drain()
                dve.tensor_tensor(sN[:, k], sN[:, k], eN[:, k], ALU.mult)
                dve.drain()
                dve.tensor_tensor(res[:, b * BLK:(b + 1) * BLK, :], sN[:, k], x[:, b * BLK:(b + 1) * BLK, :],
                                  ALU.add).then_inc(res_in, 1)


def kernel(L0_attn_x, L0_attn_Wq, L0_attn_Wk, L0_attn_Wv, L0_ffn_ln_g, L0_ffn_ln_b, L0_ffn_w_qkv, L0_ffn_w_lo,
           L0_ffn_rt_q, L0_ffn_rt_kv, L0_ffn_qnorm_g, L0_ffn_cnorm_g, L0_ffn_null_kv, L0_ffn_w_q, L0_ffn_w_kv,
           L0_ffn_w_out):
    import concourse.bacc as _bacc
    from concourse.bass_utils import run_bass_kernel_spmd as _run

    a = lambda t: np.asarray(t)
    inner = H * DH
    qkv = a(L0_ffn_w_qkv)
    rows = lambda w: w.reshape(PAIRS, P, D).transpose(1, 0, 2)
    grouped = lambda w: w.reshape(G * PAIRS, P, D).transpose(1, 0, 2)
    kv, null = a(L0_ffn_w_kv), a(L0_ffn_null_kv)
    arrays = {
        "x": a(L0_attn_x), "Wq": a(L0_attn_Wq), "Wk": a(L0_attn_Wk),
        "WvT": a(L0_attn_Wv).transpose(2, 0, 1),
        "ln_g": a(L0_ffn_ln_g).reshape(D, 1), "ln_b": a(L0_ffn_ln_b).reshape(D, 1),
        "wqk": qkv[:2 * inner].reshape(2, PAIRS, P, D).transpose(3, 1, 0, 2).reshape(D, PAIRS, 2 * P),
        "bv": rows(qkv[2 * inner:]), "bo": rows(a(L0_ffn_w_lo).T),
        "qg": a(L0_ffn_qnorm_g).T, "cg": a(L0_ffn_cnorm_g),
        "rt_q": a(L0_ffn_rt_q).T, "rt_kv": a(L0_ffn_rt_kv).T,
        "cq": grouped(a(L0_ffn_w_q)), "ck": grouped(kv[:, :inner]), "cv": grouped(kv[:, inner:]),
        "co": grouped(a(L0_ffn_w_out).transpose(0, 2, 1)),
        "null": null.reshape(2, G, PAIRS, P).transpose(3, 0, 1, 2),
        **shape_constants(),
    }
    arrays = {f"in_{k}": np.ascontiguousarray(v) for k, v in arrays.items()}
    nc = _bacc.Bacc("TRN2", target_bir_lowering=False, num_devices=1)
    dram = {k[3:]: nc.dram_tensor(k, v.shape, mybir.dt.from_np(v.dtype), kind="ExternalInput").ap()
            for k, v in arrays.items()}
    out = nc.dram_tensor("out", (B, N, D), F32, kind="ExternalOutput").ap()
    build(nc, dram, out)
    r = _run(nc, [arrays], core_ids=[0])
    return r.results[0]["out"]
```

```python
from contextlib import ExitStack

import numpy as np

import concourse.bass as bass
from concourse import mybir

P = 128
B, N, D = 4, 512, 128
BLK = N // P
NB = B * BLK
HA = 8
DH = 64
H = 16
PAIRS = H // 2
W = 64
NW = N // W
WQ = NW - 1
G = 2
NQ, NKV = 32, 128
NITER = 20
CTX = N - W
KV_W0 = 2
KV_ROWS = (WQ - KV_W0) * B * G
Q_ROWS = WQ * B * G
Q_AT = 64
NEG = -1.0e30
TAKEN = -3.0e38
EPS = [max(4.0 * 0.7**i, 0.03) for i in range(NITER + 1)]
LOWEST = -87.33655
SCALE = DH**-0.5
UNITS = 4

F32 = mybir.dt.float32
BF16 = mybir.dt.bfloat16
ALU = mybir.AluOpType
ACT = mybir.ActivationFunctionType
AX = mybir.AxisListType


def kv_row(w, g, b):
    return (w - KV_W0) * G * B + g * B + b


def q_row(w, g, b):
    return w * G * B + g * B + b


def shape_constants():
    f = np.float32
    c = {}
    c["ident"] = np.eye(P, dtype=f)
    i = np.arange(P)
    c["causal"] = ((i[:, None] <= i[None, :]) / f(N)).astype(f)
    inv = (f(1.0) / np.power(f(10000.0), np.arange(0, DH, 2, dtype=f) / f(DH))).astype(f)
    ang = (np.arange(N, dtype=f)[:, None] * inv[None, :]).astype(f)
    cos, sin = np.cos(ang).astype(f), np.sin(ang).astype(f)
    by_block = lambda t: t.reshape(BLK, P, -1).transpose(1, 0, 2).copy()
    c["cos"] = by_block(np.concatenate([cos, cos], 1))
    c["sin"] = by_block(np.concatenate([-sin, sin], 1))
    q, k = np.arange(P)[:, None] % W, np.arange(P)[None, :]
    first = np.where(k <= q, 0.0, NEG)
    later = np.where((k >= q) & (k - W <= q), 0.0, NEG)
    c["window"] = np.concatenate([first] + [later] * 4, 1).astype(f)
    rmask = np.zeros((P, CTX), f)
    rinvk = np.ones((P, 1), f)
    half = np.zeros((P, 3), f)
    for g in range(G):
        for b in range(B):
            for w in range(KV_W0, WQ):
                rmask[kv_row(w, g, b), W * (w + 1):] = NEG
                rinvk[kv_row(w, g, b)] = 1.0 / (NKV * 9.0 / 8.0)
            for w in range(WQ):
                r = Q_AT + q_row(w, g, b)
                rmask[r, W:] = NEG
                rinvk[r] = 1.0 / (NQ * 9.0 / 8.0)
                odd = (w + 1) % 2
                half[r] = [NQ * odd, 1 - odd, odd]
    c["rmask"], c["rinvk"], c["half"] = rmask, rinvk, half
    e = np.array(EPS[:NITER], np.float64)
    c["eps"] = np.tile(np.stack([1.0 / e, e]).astype(f)[None], (P, 1, 1))
    c["iota"] = np.tile(np.arange(1, P + 1, dtype=f), (P, 1))
    h4, qq = np.arange(P) // NQ, np.arange(P) % NQ
    c["own"] = (h4[:, None] == np.arange(H)[None, :] % 4).astype(f)
    c["fold"] = (qq[:, None] == np.arange(NQ)[None, :]).astype(f)
    return c


CONSTS = ["ident", "causal", "cos", "sin", "window", "rmask", "rinvk", "half", "eps", "iota", "own", "fold"]


def build(nc, dram, out):
    ctx = ExitStack()
    with ctx:
        def sb(name, shape, dt=F32):
            return ctx.enter_context(nc.sbuf_tensor(name, shape, dt))

        def sem(name):
            return ctx.enter_context(nc.semaphore(name))

        x = sb("x", [P, NB, D])
        xhat = sb("xhat", [P, NB, D])
        G2 = sb("G2", [P, G * H, D])
        W2C = sb("W2C", [P, G * H, D])
        sT = sb("sT", [P, B, N])
        loc = sb("loc", [P, B, N])
        ident = sb("ident", [P, P])
        identb = sb("identb", [P, P], BF16)
        causal = sb("causal", [P, P])
        zerob = sb("zerob", [P, N], BF16)
        cos = sb("cos", [P, BLK, DH])
        sin = sb("sin", [P, BLK, DH])
        windowf = sb("windowf", [P, 5 * P])
        windowb = sb("windowb", [P, 5 * P], BF16)
        rmask = sb("rmask", [P, CTX])
        rinvk = sb("rinvk", [P, 1])
        half = sb("half", [P, 3])
        eps = sb("eps", [P, 2, NITER])
        iota = sb("iota", [P, P])
        own = sb("own", [P, H])
        fold = sb("fold", [P, NQ])
        lng = sb("lng", [P, 1])
        lnb = sb("lnb", [P, 1])
        qg = sb("qg", [P, G])
        nkv = sb("nkv", [P, 2, G, PAIRS])
        cg = sb("cg", [P, G])
        cgs = sb("cgs", [P, G])
        rtq = sb("rtq", [P, G])
        rtk = sb("rtk", [P, G])
        NK = sb("NK", [P, G, H])
        NV = sb("NV", [H, G, D])
        wscr = sb("wscr", [P, 2, D])
        gscr = sb("gscr", [P, D])
        RS = sb("RS", [P, CTX])
        RU = sb("RU", [P, CTX])
        RE = sb("RE", [P, CTX])
        rsmax = sb("rsmax", [P, 1])
        rm = sb("rm", [P, 1])
        rna = sb("rna", [P, 1])
        rsum = sb("rsum", [P, 1])
        rln = sb("rln", [P, 1])
        rm8 = sb("rm8", [P, 8])
        qhalf = sb("qhalf", [P, P])
        kvcode = sb("kvcode", [P, 4, KV_ROWS])
        kvcol = sb("kvcol", [P, 2, 4])
        qrow_t = sb("qrow_t", [P, Q_ROWS])
        qcode = sb("qcode", [P, BLK, G * B])
        rcount = sb("rcount", [P, BLK, G * B])
        rcnt = sb("rcnt", [P, BLK, B])

        EARLY = 14080
        early = sb("early", [P, EARLY])
        STAGE = 14720
        stage = sb("stage", [P, STAGE])

        def part(region, at, shape):
            size = int(np.prod(shape))
            names = "abcd"[:len(shape)]
            v = region[:, at:at + size]
            if len(shape) == 1:
                return v, at + size
            spec = f"p ({' '.join(names)}) -> p {' '.join(names)}"
            return v.rearrange(spec, **{n: s for n, s in zip(names, shape)}), at + size

        o = 0
        xnT, o = part(early, o, [B, N])
        xlnT, o = part(early, o, [B, N])
        xln, o = part(early, o, [B * 7, D])
        wqk, o = part(early, o, [PAIRS, 2 * P])
        W2B, o = part(early, o, [H, D])
        GA, o = part(early, o, [HA, D])
        wvT, o = part(early, o, [HA, D])
        assert o <= EARLY, o

        o = 0
        xn = sT[:].rearrange("p b (k d) -> p (b k) d", d=D)
        xh2 = loc[:].rearrange("p b (k d) -> p (b k) d", d=D)
        cq, o = part(stage, o, [G * PAIRS, D])
        ck, o = part(stage, o, [G * PAIRS, D])
        cv, o = part(stage, o, [G * PAIRS, D])
        co, o = part(stage, o, [G * PAIRS, D])
        bv, o = part(stage, o, [PAIRS, D])
        bo, o = part(stage, o, [PAIRS, D])
        aq, o = part(stage, o, [HA, D])
        ak, o = part(stage, o, [HA, D])
        nkb, o = part(stage, o, [G, PAIRS, H])
        nvb, o = part(stage, o, [G, PAIRS, H])
        RTk, o = part(stage, o, [B, KV_ROWS])
        RTq, o = part(stage, o, [WQ * B, Q_ROWS])
        assert o <= STAGE, o
        stats = sb("stats", [P, NB, 6])
        mv = sb("mv", [P, NB, 2])
        var3 = sb("var3", [P, 3, NB])
        rs3 = sb("rs3", [P, 3, NB])
        tmp3 = sb("tmp3", [P, 3, NB])

        o = 0
        yT, o = part(stage, o, [2, N])
        vN, o = part(stage, o, [2, BLK, D])
        simA, o = part(stage, o, [2, 3, N])

        o = 0
        r1, o = part(stage, o, [2, BLK, 4, DH])
        r2, o = part(stage, o, [2, BLK, 4, DH])
        rot, o = part(stage, o, [2, BLK, 2 * P])
        qbd, o = part(stage, o, [NW, P])
        kT, o = part(stage, o, [N])
        pB, o = part(stage, o, [2, NW, P])
        pTB, o = part(stage, o, [2, NW, P])
        axB, o = part(stage, o, [2, NW, P])
        nmB = sb("nmB", [P, 2, NW])
        rsB = sb("rsB", [P, 2, NW])
        riB = sb("riB", [P, NW])
        assert o <= STAGE, o

        o = 0
        qsel, o = part(early, o, [G, B, 2 * P])
        U, o = part(early, o, [WQ, H, NQ])
        axC, o = part(early, o, [H, WQ, NQ])
        pC, o = part(early, o, [3, 4, P])
        pTC, o = part(early, o, [2, 4 * P])
        XN, o = part(early, o, [6, D])
        XT, o = part(early, o, [2, P])
        OH, o = part(early, o, [2, 4, P])
        assert o <= EARLY, o
        o = 0
        qrep, o = part(stage, o, [WQ, 4, NQ])
        ntmp, o = part(stage, o, [WQ, H])
        oT, o = part(stage, o, [B, BLK, G, W])
        OHQ, o = part(stage, o, [NB, P])
        OHS, o = part(stage, o, [2, BLK, P])
        oN, o = part(stage, o, [2, BLK, D])
        sN, o = part(stage, o, [2, BLK, D])
        yN, o = part(stage, o, [2, BLK, D])
        eN, o = part(stage, o, [2, BLK, D])
        res, o = part(stage, o, [NB, D])
        assert o <= STAGE, o
        nsC = sb("nsC", [P, WQ * 4])
        nmC = sb("nmC", [P, 3, 4])
        dnC = sb("dnC", [P, 3, 4])
        pnC = sb("pnC", [P, 3, 4])
        rsC = sb("rsC", [P, 3, 4])
        riC = sb("riC", [P, 4])
        pnall = sb("pnall", [P, WQ * 4])
        pn16 = sb("pn16", [P, WQ * 4, 4])
        pnT = sb("pnT", [H, WQ * NQ])

        ps = ctx.enter_context(nc.psum_tensor("ps", [P, 8, N], F32))

        s_x = [sem(f"s_x{b}") for b in range(B)]
        s_const = sem("s_const")
        s_wa = sem("s_wa")
        s_wb = sem("s_wb")
        s_wv = sem("s_wv")
        s_wqk = sem("s_wqk")
        s_wc = sem("s_wc")
        s_null = sem("s_null")
        s_cleared = sem("s_cleared")
        s_rt = sem("s_rt")
        s_var = sem("s_var")
        s_ln = sem("s_ln")
        s_xn = sem("s_xn")
        s_xh2 = sem("s_xh2")
        s_xhat = sem("s_xhat")
        s_bf = sem("s_bf")
        prep_out = sem("prep_out")
        prep_in = sem("prep_in")
        logits = sem("logits")
        r_start = sem("r_start")
        r_u = sem("r_u")
        r_l = sem("r_l")
        g_loaded = sem("g_loaded")
        y_out = sem("y_out")
        y_in = sem("y_in")
        v_out = sem("v_out")
        v_in = sem("v_in")
        sc_out = sem("sc_out")
        relu_in = sem("relu_in")
        diag_in = sem("diag_in")
        pv_done = sem("pv_done")
        sT_in = sem("sT_in")
        codes = sem("codes")
        qk_out = sem("qk_out")
        roped = sem("roped")
        rot_in = sem("rot_in")
        qkT_out = sem("qkT_out")
        qkT_in = sem("qkT_in")
        sim_out = sem("sim_out")
        max_in = sem("max_in")
        exp_in = sem("exp_in")
        norm_in = sem("norm_in")
        pT_out = sem("pT_out")
        pT_in = sem("pT_in")
        ax_out = sem("ax_out")
        ax_in = sem("ax_in")
        w2_loaded = sem("w2_loaded")
        out_out = sem("out_out")
        loc_in = sem("loc_in")
        loc_zero = sem("loc_zero")
        qbd_zero = sem("qbd_zero")
        code_out = sem("code_out")
        ohq_in = sem("ohq_in")
        qsel_out = sem("qsel_out")
        qsel_in = sem("qsel_in")
        rep_in = sem("rep_in")
        oT_zero = sem("oT_zero")
        u_out = sem("u_out")
        u_act = sem("u_act")
        u_dve = sem("u_dve")
        null_out = sem("null_out")
        null_in = sem("null_in")
        oh_in = sem("oh_in")
        gx_out = sem("gx_out")
        xn_in = sem("xn_in")
        xt_out = sem("xt_out")
        xt_in = sem("xt_in")
        csim_out = sem("csim_out")
        cmax_in = sem("cmax_in")
        cexp_in = sem("cexp_in")
        cnorm_in = sem("cnorm_in")
        cpT_out = sem("cpT_out")
        cpT_in = sem("cpT_in")
        cax_out = sem("cax_out")
        cax_in = sem("cax_in")
        pn16_in = sem("pn16_in")
        pnT_out = sem("pnT_out")
        pnT_in = sem("pnT_in")
        cout_out = sem("cout_out")
        cout_in = sem("cout_in")
        ft_out = sem("ft_out")
        ft_act = sem("ft_act")
        ft_dve = sem("ft_dve")
        fin_out = sem("fin_out")
        y_ready = sem("y_ready")
        e_ready = sem("e_ready")
        res_in = sem("res_in")
        s_out = sem("s_out")

        N_CONST = len(CONSTS) + 7

        def at_least(eng, s, n):
            if not isinstance(n, int) or n > 0:
                eng.wait_ge(s, n)

        def sweep(eng, n, body):
            body(0, True, False)
            with eng.Fori(1, n - 1) as i:
                body(i, False, False)
            body(n - 1, False, True)

        def sequences(eng, body):
            body(0, 0, 0, None)
            for g in range(G):
                if g > 0:
                    body(g, 0, g * B, (g - 1, B - 1, g * B - 1))
                with eng.Fori(1, B) as b:
                    body(g, b, b + g * B, (g, b - 1, b + (g * B - 1)))

        LAST = (G - 1, B - 1, G * B - 1)

        A_STEPS = [[(m, m * P, m * P, (m + 1) * P) for m in range(BLK)],
                   [(0, 0, P, N), (2, 3 * P, 3 * P, N)],
                   [(1, 0, 2 * P, N)]]

        block = ctx.enter_context(nc.Block())

        J_GA, J_W2B, J_G2, J_W2C, J_NULL, J_XLN, J_END = 8, 10, 14, 22, 30, 31, 38

        @block.sync
        def _(sp):
            xv = dram["x"].rearrange("b (k p) d -> p (b k) d", p=P)
            for b in range(B):
                sp.dma_start(x[:, b * BLK:(b + 1) * BLK, :], xv[:, b * BLK:(b + 1) * BLK, :]).then_inc(s_x[b], 16)
            tiles = [ident, causal, cos, sin, windowf, rmask, rinvk, half, eps, iota, own, fold]
            for name, t in zip(CONSTS, tiles):
                sp.dma_start(t[:], dram[name]).then_inc(s_const, 16)
            sp.dma_start(lng[:], dram["ln_g"]).then_inc(s_const, 16)
            sp.dma_start(lnb[:], dram["ln_b"]).then_inc(s_const, 16)
            sp.dma_start(qg[:], dram["qg"]).then_inc(s_const, 16)
            sp.dma_start(cg[:], dram["cg"]).then_inc(s_const, 16)
            sp.dma_start(rtq[:], dram["rt_q"]).then_inc(s_const, 16)
            sp.dma_start(rtk[:], dram["rt_kv"]).then_inc(s_const, 16)
            sp.dma_start(nkv[:], dram["null"]).then_inc(s_const, 16)
            sp.dma_start(aq[:], dram["Wq"].rearrange("h e d -> e h d")).then_inc(s_wa, 16)
            sp.dma_start(ak[:], dram["Wk"].rearrange("h e d -> e h d")).then_inc(s_wa, 16)
            sp.dma_start(bv, dram["bv"]).then_inc(s_wb, 16)
            sp.dma_start(bo, dram["bo"]).then_inc(s_wb, 16)
            for t, name in ((cq, "cq"), (ck, "ck"), (cv, "cv"), (co, "co")):
                sp.dma_start(t, dram[name]).then_inc(s_wc, 16)
            sp.dma_start(wvT, dram["WvT"]).then_inc(s_wv, 16)
            sp.dma_start(wqk, dram["wqk"]).then_inc(s_wqk, 16)
            ov = out.rearrange("b (k p) d -> p (b k) d", p=P)
            for b in range(B):
                sp.wait_ge(res_in, b + 1)
                sp.dma_start(ov[:, b * BLK:(b + 1) * BLK, :], res[:, b * BLK:(b + 1) * BLK, :]).then_inc(s_out, 16)
            sp.wait_ge(s_out, 16 * B)

        @block.gpsimd
        def _(pool):
            pool.memset(nkb, 0.0).then_inc(s_cleared, 1)
            pool.memset(nvb, 0.0).then_inc(s_cleared, 1)
            pool.memset(RTk, 0.0).then_inc(s_cleared, 1)
            pool.memset(RTq, 0.0).then_inc(s_cleared, 1)
            pool.wait_ge(s_cleared, 4)
            pool.wait_ge(s_const, 16 * N_CONST)
            flat = RTk.rearrange("p b r -> p (b r)")
            for w in range(KV_W0, WQ):
                for g in range(G):
                    at = kv_row(w, g, 0)
                    pool.tensor_copy(flat[:, at:at + (B - 1) * (KV_ROWS + 1) + 1:KV_ROWS + 1],
                                     rtk[:, g:g + 1].broadcast_to([P, B]))
            flat = RTq.rearrange("p c r -> p (c r)")
            for w in range(WQ):
                for g in range(G):
                    at = w * B * Q_ROWS + q_row(w, g, 0)
                    last = pool.tensor_copy(flat[:, at:at + (B - 1) * (Q_ROWS + 1) + 1:Q_ROWS + 1],
                                            rtq[:, g:g + 1].broadcast_to([P, B]))
            pool.drain()
            pool.tensor_copy(identb[:], ident[:]).then_inc(s_rt, 1)
            for i, t in enumerate((nkb, nvb)):
                for hf in range(2):
                    rows = slice(hf * DH, (hf + 1) * DH)
                    pool.drain()
                    for g in range(G):
                        flat = t[rows, g].rearrange("p a b -> p (a b)")
                        last = pool.tensor_copy(flat[:, hf::H + 2], nkv[rows, i, g, :])
            last.then_inc(s_null, 1)
            pool.drain()
            pool.memset(zerob[:], 0.0)
            pool.tensor_copy(windowb[:], windowf[:]).then_inc(s_bf, 1)

            pool.wait_ge(prep_in, J_GA + 2)

            def head(h, first, last):
                if not first:
                    pool.wait_ge(y_out, 4 * h)
                pool.tensor_copy(gscr[:], GA[:, h, :]).then_inc(g_loaded, 1)
            sweep(pool, HA, head)

            pool.wait_ge(pv_done, 1)
            pool.memset(qbd, 0.0).then_inc(qbd_zero, 1)
            pool.memset(loc[:], 0.0).then_inc(loc_zero, 1)

            def add(p, b, ahead):
                u = 4 * p + b + ahead
                k = (b + ahead) % 2
                pool.wait_ge(roped, u + 1)
                at_least(pool, qkT_out, u - 1)
                pool.tensor_tensor(rot[:, k].rearrange("p a b -> p (a b)"),
                                   r1[:, k].rearrange("p a b c -> p (a b c)"),
                                   r2[:, k].rearrange("p a b c -> p (a b c)"), ALU.add).then_inc(rot_in, 1)

            def w2_load(p):
                if not isinstance(p, int) or p > 0:
                    pool.wait_ge(out_out, 4 * p)
                pool.tensor_copy(wscr[:], W2B[:, bass.ts(p, 2), :]).then_inc(w2_loaded, 1)

            add(0, 0, 0)
            add(0, 0, 1)

            def pair(p, first, last):
                for b in range(UNITS):
                    if not (last and b >= 2):
                        add(p, b, 2)
                    if b == 0:
                        w2_load(p)
            sweep(pool, PAIRS, pair)

            pool.wait_ge(loc_in, UNITS * PAIRS)
            pool.memset(oT[:], 0.0).then_inc(oT_zero, 1)
            pool.wait_ge(qsel_in, B)

            def onehots(g, b, it, k):
                at_least(pool, gx_out, it * 6 + k - 1)
                col = (k + 1 - KV_W0) * G * B + g * B
                pool.tensor_copy(kvcol[:, k % 2, :].unsqueeze(2), kvcode[:, :, bass.ds(b + col, 1)])
                pool.drain()
                for c in range((k + 3) // 2):
                    rows = min(P, W * (k + 2) - c * P)
                    if rows < P:
                        pool.drain()
                    t = pool.tensor_scalar(OH[0:rows, k % 2, c, :], iota[0:rows, :], kvcol[0:rows, k % 2, c:c + 1],
                                           None, ALU.is_equal)
                t.then_inc(oh_in, 1)
                if rows < P:
                    pool.drain()

            def sequence(g, b, it, before):
                onehots(g, b, it, 1)
                onehots(g, b, it, 2)
                at_least(pool, null_out, it)
                src = qsel[:, g, bass.ds(b, 1), NQ:].rearrange("p o (w q) -> p (o w) q", q=NQ)
                for r in range(4):
                    c = pool.tensor_copy(qrep[:, :, r, :], src)
                c.then_inc(rep_in, 1)
                for k in range(3, 6):
                    onehots(g, b, it, k)
            sequences(pool, sequence)

        @block.tensor
        def _(pe):
            def bank(i, n=1):
                return ps[:, i] if n == 1 else ps[:, i:i + n]

            def job(k):
                at_least(pe, prep_in, k - 3)
                return bank(4 + k % 4)

            pe.wait_ge(s_const, 16 * N_CONST)
            for b in range(B):
                to = job(b)
                pe.wait_ge(s_xn, b + 1)
                for k in range(BLK):
                    t = pe.transpose(to[:, k * P:(k + 1) * P], xn[:, b * BLK + k, :], ident[:])
                t.then_inc(prep_out, 1)
            for b in range(B):
                to = job(4 + b)
                pe.wait_ge(s_xh2, b + 1)
                for k in range(BLK):
                    t = pe.transpose(to[:, k * P:(k + 1) * P], xh2[:, b * BLK + k, :], ident[:])
                t.then_inc(prep_out, 1)
            pe.wait_ge(prep_in, 4)
            pe.wait_ge(s_rt, 1)
            for b in range(B):
                t = pe.matmul(ps[0:KV_ROWS, 0, 0:CTX], RTk[:, b, :], xnT[:, b, 0:CTX],
                              start=(b == 0), stop=(b == B - 1))
            t.then_inc(logits, 1)
            for w in range(WQ):
                for b in range(B):
                    t = pe.matmul(ps[Q_AT:Q_AT + Q_ROWS, 1, 0:W], RTq[:, w * B + b, :],
                                  xnT[:, b, W * (w + 1):W * (w + 2)],
                                  start=(w == 0 and b == 0), stop=(w == WQ - 1 and b == B - 1))
            t.then_inc(logits, 1)
            pe.wait_ge(s_wa, 32)
            for j in range(2):
                to = job(J_GA + j)
                for k in range(4):
                    t = pe.matmul(to[:, k * D:(k + 1) * D], aq[:, 4 * j + k, :], ak[:, 4 * j + k, :],
                                  start=True, stop=True)
                t.then_inc(prep_out, 1)

            def products(j0, n, lhs, rhs):
                for j in range(n):
                    to = job(j0 + j)
                    for k in range(4):
                        h = 8 * (j // 2) + 2 * k + j % 2
                        rows = slice(DH * (h % 2), DH * (h % 2 + 1))
                        t = pe.matmul(to[:, k * D:(k + 1) * D], lhs[rows, h // 2, :], rhs[rows, h // 2, :],
                                      start=True, stop=True)
                    t.then_inc(prep_out, 1)

            pe.wait_ge(s_wb, 32)
            products(J_W2B, 4, bv, bo)
            pe.wait_ge(s_wc, 64)
            products(J_G2, 8, cq, ck)
            products(J_W2C, 8, cv, co)
            to = job(J_NULL)
            pe.wait_ge(s_null, 1)
            for g in range(G):
                for p in range(PAIRS):
                    pe.matmul(to[:, g * H:(g + 1) * H], cq[:, g * PAIRS + p, :], nkb[:, g, p, :],
                              start=(p == 0), stop=(p == PAIRS - 1))
                for p in range(PAIRS):
                    t = pe.matmul(to[0:H, P * (g + 1):P * (g + 2)], nvb[:, g, p, :], co[:, g * PAIRS + p, :],
                                  start=(p == 0), stop=(p == PAIRS - 1))
            t.then_inc(prep_out, 1)
            for j in range(7):
                to = job(J_XLN + j)
                for k in range(4):
                    b, w = divmod(4 * j + k, 7)
                    t = pe.transpose(to[:, k * P:(k + 1) * P], xlnT[:, b, W * w:W * w + P], ident[:])
                t.then_inc(prep_out, 1)

            pe.wait_ge(prep_in, J_END)
            pe.wait_ge(r_start, 1)
            pe.wait_ge(s_wv, 16)
            pe.wait_ge(s_bf, 1)
            for b in range(B):
                pe.matmul(bank(b), identb[:], zerob[:], start=True, stop=False)

            def a_y(h, b):
                u = 4 * h + b
                pe.wait_ge(g_loaded, h + 1)
                at_least(pe, v_in, u)
                pe.matmul(bank(7), gscr[:], xnT[:, b, :], start=True, stop=True).then_inc(y_out, 1)

            def a_v(h, b):
                u = 4 * h + b
                pe.wait_ge(y_in, u + 1)
                for k in range(BLK):
                    t = pe.matmul(ps[:, 7, k * D:(k + 1) * D], xnT[:, b, k * P:(k + 1) * P],
                                  wvT[:, bass.ds(h, 1), :].rearrange("p o d -> p (o d)"), start=True, stop=True)
                t.then_inc(v_out, 1)

            def a_scores(h, b, s):
                u = 4 * h + b
                if s == 0:
                    pe.wait_ge(y_in, u + 1)
                if s == 0:
                    at_least(pe, diag_in, u)
                else:
                    at_least(pe, relu_in, 2 * u + s - 2)
                for m, at, q0, q1 in A_STEPS[s]:
                    t = pe.matmul(ps[:, 4 + s, at:at + q1 - q0], xnT[:, b, m * P:(m + 1) * P],
                                  yT[:, b % 2, q0:q1], start=True, stop=True)
                t.then_inc(sc_out, 1)

            def a_sums(h, b, s):
                u = 4 * h + b
                if s == 0:
                    pe.wait_ge(v_in, u + 1)
                    pe.wait_ge(diag_in, u + 1)
                else:
                    pe.wait_ge(relu_in, 2 * u + s)
                for m, at, q0, q1 in A_STEPS[s]:
                    t = pe.matmul(ps[:, b, q0:q1], vN[:, b % 2, m, :], simA[:, b % 2, s, at:at + q1 - q0],
                                  start=False, stop=False, skip_group_check=True)
                return t

            a_y(0, 0)
            a_v(0, 0)

            def head(h, first, last):
                for b in range(UNITS):
                    nh, nb = (h, b + 1) if b < UNITS - 1 else (h + 1, 0)
                    more = not (last and b == UNITS - 1)
                    a_scores(h, b, 0)
                    if b > 0:
                        a_sums(h, b - 1, 2)
                    elif not first:
                        a_sums(h - 1, UNITS - 1, 2)
                    if more:
                        a_y(nh, nb)
                    a_scores(h, b, 1)
                    a_sums(h, b, 0)
                    if more:
                        a_v(nh, nb)
                    a_scores(h, b, 2)
                    a_sums(h, b, 1)
            sweep(pe, HA, head)
            a_sums(HA - 1, UNITS - 1, 2)
            for b in range(B):
                t = pe.matmul(bank(b), ident[:], xnT[:, b, :], start=False, stop=True)
            t.then_inc(pv_done, 1)

            pe.wait_ge(sT_in, B)
            pe.wait_ge(s_wqk, 16)
            pe.wait_ge(s_bf, 1)

            def b_project(p, b, ahead):
                u = 4 * p + b + ahead
                at_least(pe, roped, u)
                q, c = (p, b + ahead) if b + ahead < UNITS else (p + 1, b + ahead - UNITS)
                to = ps[:, 0:2].rearrange("p k (a n) -> p (k a) n", a=2)
                for k in range(BLK):
                    t = pe.matmul(to[:, k, :], xlnT[:, c, k * P:(k + 1) * P],
                                  wqk[:, bass.ds(q, 1), :].rearrange("p o n -> p (o n)"), start=True, stop=True)
                t.then_inc(qk_out, 1)

            def b_turn(p, b, ahead):
                u = 4 * p + b + ahead
                k = (b + ahead) % 2
                pe.wait_ge(rot_in, u + 1)
                at_least(pe, pT_in, u - 1)
                for i in range(2):
                    for t4 in range(BLK):
                        t = pe.transpose(ps[:, 2 + i, t4 * P:(t4 + 1) * P], rot[:, k, t4, i * P:(i + 1) * P],
                                         ident[:])
                t.then_inc(qkT_out, 1)

            def b_scores(p, b):
                u = 4 * p + b
                pe.wait_ge(qkT_in, 3 * u + 3)
                at_least(pe, exp_in, u)
                for i in range(2):
                    for k in range(4):
                        w = 4 * i + k
                        at = W * max(w - 1, 0)
                        pe.matmul(ps[:, 4 + i, k * P:(k + 1) * P], qbd[:, w, :], kT[:, at:at + P],
                                  start=(k == 0), stop=False)
                    t = pe.matmul(bank(4 + i), identb[:], windowb[:, i * P:i * P + N], start=False, stop=True)
                t.then_inc(sim_out, 1)

            def b_turn_probs(p, b, ahead_turned):
                u = 4 * p + b
                pe.wait_ge(norm_in, u + 1)
                if ahead_turned:
                    pe.wait_ge(qkT_in, 3 * u + 6)
                for w in range(NW):
                    t = pe.transpose(ps[:, 2 + w // 4, (w % 4) * P:(w % 4 + 1) * P], pB[:, b % 2, w, :], ident[:])
                t.then_inc(pT_out, 1)

            def b_mix(p, b, i):
                u = 4 * p + b
                pe.wait_ge(pT_in, u + 1)
                at_least(pe, ax_in, 2 * u + i)
                for k in range(4):
                    w = 4 * i + k
                    t = pe.matmul(ps[:, 6, k * P:(k + 1) * P], xln[:, b * 7 + max(w - 1, 0), :],
                                  pTB[:, b % 2, w, :], start=True, stop=True)
                t.then_inc(ax_out, 1)

            def b_out(p, b):
                u = 4 * p + b
                pe.wait_ge(w2_loaded, p + 1)
                at_least(pe, loc_in, u)
                pe.wait_ge(ax_in, 2 * u + 2)
                for hf in range(2):
                    t = pe.matmul(ps[:, 7].rearrange("p (w q) -> p w q", q=W), wscr[:, hf, :],
                                  axB[:, b % 2, :, hf * W:(hf + 1) * W], start=(hf == 0), stop=(hf == 1))
                t.then_inc(out_out, 1)

            b_project(0, 0, 0)
            b_project(0, 0, 1)
            b_turn(0, 0, 0)
            pe.wait_ge(qbd_zero, 1)

            def pair(p, first, last):
                for b in range(UNITS):
                    before = (p, b - 1) if b > 0 else (None if first else (p - 1, UNITS - 1))
                    b_scores(p, b)
                    turned = not (last and b == UNITS - 1)
                    if turned:
                        b_turn(p, b, 1)
                    if before:
                        b_mix(*before, 0)
                    if not (last and b >= 2):
                        b_project(p, b, 2)
                    if before:
                        b_mix(*before, 1)
                        b_out(*before)
                    b_turn_probs(p, b, turned)
            sweep(pe, PAIRS, pair)
            end = (PAIRS - 1, UNITS - 1)
            b_mix(*end, 0)
            b_mix(*end, 1)
            b_out(*end)

            pe.wait_ge(codes, 1)
            pe.wait_ge(loc_in, UNITS * PAIRS)
            for c in range(4):
                n = min(P, CTX - c * P)
                pe.transpose(ps[0:n, 4, c * KV_ROWS:(c + 1) * KV_ROWS], RE[0:KV_ROWS, c * P:c * P + n],
                             ident[0:KV_ROWS, 0:KV_ROWS])
            rows = slice(Q_AT, Q_AT + Q_ROWS)
            pe.transpose(ps[:, 5, 0:Q_ROWS], qhalf[rows, :], ident[rows, rows]).then_inc(code_out, 1)
            for b in range(B):
                pe.wait_ge(ohq_in, b + 1)
                for j in range(BLK):
                    t = pe.matmul(ps[:, b, j * P:(j + 1) * P], xhat[:, b * BLK + j, :], OHQ[:, b * BLK + j, :],
                                  start=True, stop=True)
                t.then_inc(qsel_out, 1)
            pe.wait_ge(qsel_in, B)

            def gather(b, it, k):
                at_least(pe, xt_in, it * 6 + k)
                if k > 0:
                    at_least(pe, oh_in, it * 5 + k)
                n = 1 if k == 0 else (k + 3) // 2
                for c in range(n):
                    rows = P if k == 0 else min(P, W * (k + 2) - c * P)
                    onehot = ident[:] if k == 0 else OH[0:rows, k % 2, c, :]
                    t = pe.matmul(ps[:, 4, 0:D], onehot,
                                  xhat[0:rows, bass.ds(b * BLK + c, 1), :].rearrange("p o d -> p (o d)"),
                                  start=(c == 0), stop=(c == n - 1))
                t.then_inc(gx_out, 1)

            def turn(it, k):
                at_least(pe, xn_in, it * 6 + k + 1)
                pe.transpose(ps[:, 4, P:2 * P], XN[:, k, :], ident[:]).then_inc(xt_out, 1)

            def expand(g, b, it, s):
                if s > 1:
                    at_least(pe, (u_act, u_dve)[s % 2], it * 4 + s // 2)
                elif s == 0:
                    at_least(pe, cout_in, it - 1)
                for i in range(2):
                    t = pe.matmul(ps[:, s % 2, i * WQ * NQ:(i + 1) * WQ * NQ], G2[:, g * H + 2 * s + i, :],
                                  qsel[:, g, bass.ds(b, 1), NQ:].rearrange("p o n -> p (o n)"),
                                  start=True, stop=True)
                t.then_inc(u_out, 1)

            def nulls(g, it):
                at_least(pe, rep_in, it + 1)
                pe.wait_ge(u_dve, it * 4 + 4)
                for w in range(WQ):
                    t = pe.matmul(ps[:, 1, w * H:(w + 1) * H], qrep[:, w].rearrange("p r q -> p (r q)"),
                                  NK[:, g, :], start=True, stop=True)
                t.then_inc(null_out, 1)

            def scores(it, w):
                k, n = max(w - 1, 0), (W if w == 0 else P)
                pe.wait_ge(xt_in, it * 6 + k + 1)
                if w == 0:
                    pe.wait_ge(u_act, it * 4 + 4)
                    pe.wait_ge(u_dve, it * 4 + 4)
                    at_least(pe, cexp_in, it * WQ)
                elif w >= 3:
                    pe.wait_ge(cexp_in, it * WQ + w - 2)
                for hg in range(4):
                    t = pe.matmul(ps[:, 5 + w % 3, hg * P:hg * P + n],
                                  U[:, w, 4 * hg:4 * hg + 4, :].rearrange("p h q -> p (h q)"),
                                  XT[:, k % 2, 0:n], start=True, stop=True)
                t.then_inc(csim_out, 1)

            def turn_probs(it, w):
                pe.wait_ge(cnorm_in, it * WQ + w + 1)
                at_least(pe, cpT_in, it * WQ + w)
                for hg in range(4):
                    t = pe.transpose(ps[:, 3, hg * P:(hg + 1) * P], pC[:, w % 3, hg, :], ident[:])
                t.then_inc(cpT_out, 1)

            def mix(it, w):
                n = W if w == 0 else P
                pe.wait_ge(cpT_in, it * WQ + w + 1)
                at_least(pe, cax_in, it * WQ + w)
                pe.matmul(ps[:, 2, :], XN[0:n, max(w - 1, 0), :], pTC[0:n, w % 2, :],
                          start=True, stop=True).then_inc(cax_out, 1)

            def null_probs(it):
                pe.wait_ge(pn16_in, it + 1)
                for w in range(WQ):
                    t = pe.matmul(ps[0:H, 1, 256 + w * NQ:256 + (w + 1) * NQ],
                                  pn16[:, 4 * w:4 * w + 4, :].rearrange("p a b -> p (a b)"), fold[:],
                                  start=True, stop=True)
                t.then_inc(pnT_out, 1)

            def project(g, it, part):
                if part == 0:
                    pe.wait_ge(cax_in, it * WQ + WQ)
                for h in range(part * H // 2, (part + 1) * H // 2):
                    pe.matmul(ps[:, 0, 0:WQ * NQ], W2C[:, g * H + h, :],
                              axC[:, h].rearrange("p w q -> p (w q)"), start=(h == 0), stop=False)
                if part == 1:
                    pe.wait_ge(pnT_in, it + 1)
                    pe.matmul(ps[:, 0, 0:WQ * NQ], NV[:, g, :], pnT[:], start=False, stop=True).then_inc(cout_out, 1)

            def sequence(g, b, it, before):
                if before:
                    pg, _, pit = before
                gather(b, it, 0)
                expand(g, b, it, 0)
                expand(g, b, it, 1)
                if before:
                    turn_probs(pit, 5)
                turn(it, 0)
                expand(g, b, it, 2)
                if before:
                    mix(pit, 4)
                expand(g, b, it, 3)
                if before:
                    turn_probs(pit, 6)
                expand(g, b, it, 4)
                gather(b, it, 1)
                if before:
                    mix(pit, 5)
                expand(g, b, it, 5)
                turn(it, 1)
                expand(g, b, it, 6)
                expand(g, b, it, 7)
                if before:
                    mix(pit, 6)
                gather(b, it, 2)
                nulls(g, it)
                scores(it, 0)
                scores(it, 1)
                turn(it, 2)
                if before:
                    project(pg, pit, 0)
                scores(it, 2)
                if before:
                    pe.wait_ge(null_in, it + 1)
                    null_probs(pit)
                turn_probs(it, 0)
                if before:
                    project(pg, pit, 1)
                for w in range(WQ - 3):
                    if w + 3 <= 5:
                        gather(b, it, w + 3)
                    scores(it, w + 3)
                    if w + 3 <= 5:
                        turn(it, w + 3)
                    turn_probs(it, w + 1)
                    mix(it, w)

            sequences(pe, sequence)
            g, _, it = LAST
            turn_probs(it, 5)
            mix(it, 4)
            turn_probs(it, 6)
            mix(it, 5)
            null_probs(it)
            mix(it, 6)
            project(g, it, 0)
            project(g, it, 1)

            pe.wait_ge(cout_in, G * B)
            for b in range(B):
                if b >= 1:
                    pe.wait_ge(ft_act, 2 * b)
                    pe.wait_ge(ft_dve, b)
                for j in range(BLK):
                    blk = b * BLK + j
                    to = slice(j * P, (j + 1) * P)
                    pe.transpose(ps[:, 0, to], OHQ[:, blk, :], ident[:])
                    pe.transpose(ps[:, 1, to], oT[:, b, j].rearrange("p g s -> p (g s)"), ident[:])
                    t = pe.transpose(ps[:, 2, to], sT[:, b, to], ident[:])
                t.then_inc(ft_out, 1)
                pe.wait_ge(ft_act, 2 * b + 2)
                pe.wait_ge(ft_dve, b + 1)
                if b >= 2:
                    pe.wait_ge(y_ready, b - 1)
                for j in range(BLK):
                    to = slice(j * P, (j + 1) * P)
                    pe.matmul(ps[:, 3 + b % 2, to], OHS[:, b % 2, j, :], oN[:, b % 2, j, :], start=True, stop=False)
                    t = pe.matmul(ps[:, 3 + b % 2, to], loc[:, b, to], ident[:], start=False, stop=True)
                t.then_inc(fin_out, 1)

        @block.scalar
        def _(act):
            act.preload_act_table_set("natural_log_exp_and_others")
            act.wait_ge(s_var, 1)
            act.activation(tmp3[:, 0, :], var3[:, 0, :], ACT.Ln)
            act.drain()
            act.activation(rs3[:, 0, :], tmp3[:, 0, :], ACT.Exp, scale=-0.5).then_inc(s_ln, 1)
            act.wait_ge(s_var, 2)
            act.activation(tmp3[:, 1:3, :], var3[:, 1:3, :], ACT.Ln)
            act.drain()
            act.activation(rs3[:, 1:3, :], tmp3[:, 1:3, :], ACT.Exp, scale=-0.5).then_inc(s_ln, 1)
            act.wait_ge(s_const, 16 * N_CONST)

            def job(k):
                act.wait_ge(prep_out, k + 1)
                return ps[:, 4 + k % 4, :]

            for b in range(B):
                act.activation(xnT[:, b, :], job(b), ACT.Copy).then_inc(prep_in, 1)
            for b in range(B):
                act.activation(xlnT[:, b, :], job(4 + b), ACT.Identity, bias=lnb[:, 0:1],
                               scale=lng[:, 0:1]).then_inc(prep_in, 1)

            def evacuate(j0, n, to):
                for j in range(n):
                    act.activation(to[:, 4 * j:4 * j + 4, :], job(j0 + j).rearrange("p (a b) -> p a b", b=D),
                                   ACT.Copy).then_inc(prep_in, 1)
            evacuate(J_GA, 2, GA)

            def evacuate_products(j0, n, to, gain=None):
                for j in range(n):
                    at = 8 * (j // 2) + j % 2
                    g = at // H
                    act.activation(to[:, at:at + 7:2, :], job(j0 + j).rearrange("p (a b) -> p a b", b=D),
                                   ACT.Copy, scale=1.0 if gain is None else gain[:, g:g + 1]).then_inc(prep_in, 1)
            evacuate_products(J_W2B, 4, W2B)
            evacuate_products(J_G2, 8, G2, qg)
            evacuate_products(J_W2C, 8, W2C, cg)
            null = job(J_NULL)
            for g in range(G):
                act.activation(NK[:, g, :], null[:, g * H:(g + 1) * H], ACT.Copy, scale=qg[:, g:g + 1])
            act.activation(cgs[:], cg[:], ACT.Copy, scale=SCALE)
            act.activation(NV[:], null[0:H, P:P * (1 + G)].rearrange("p (g d) -> p g d", g=G),
                           ACT.Copy).then_inc(prep_in, 1)
            evacuate(J_XLN, 7, xln)

            act.wait_ge(r_start, 1)

            def descend(i, first=False):
                if not first:
                    act.wait_ge(r_u, i)
                act.activation(RE[:], rmask[:] if first else RU[:], ACT.Exp, scale=eps[:, 0, bass.ds(i, 1)],
                               accum_out=rsum[:])
                act.drain()
                act.activation(rln[:], rsum[:], ACT.Ln, scale=rinvk[:, 0:1]).then_inc(r_l, 1)

            def a_y(h, b):
                act.wait_ge(y_out, 4 * h + b + 1)
                act.activation(yT[:, b % 2, :], ps[:, 7, :], ACT.Copy).then_inc(y_in, 1)

            def a_relu(h, b, s):
                act.wait_ge(sc_out, 3 * (4 * h + b) + s + 1)
                n = (N, 2 * P)[s - 1]
                act.activation(simA[:, b % 2, s, 0:n], ps[:, 4 + s, 0:n], ACT.Relu,
                               scale=1.0 / N).then_inc(relu_in, 1)

            a_y(0, 0)

            def head(h, first, last):
                for b in range(UNITS):
                    if not (last and b == UNITS - 1):
                        a_y(*((h, b + 1) if b < UNITS - 1 else (h + 1, 0)))
                    a_relu(h, b, 1)
                    a_relu(h, b, 2)
                    if first and b in (1, 2):
                        descend(b - 1, first=(b == 1))
                    if not first and not last and b < 3:
                        descend(3 * h - 1 + b)
            sweep(act, HA, head)
            act.wait_ge(pv_done, 1)
            for b in range(B):
                act.activation(sT[:, b, :], ps[:, b, :], ACT.Copy).then_inc(sT_in, 1)

            def b_turned(p, b, ahead):
                u = 4 * p + b + ahead
                act.wait_ge(qkT_out, u + 1)
                at_least(act, sim_out, u)
                q = ps[:, 2, :].rearrange("p (w q) -> p w q", q=W)
                act.activation(kT, ps[:, 3, :], ACT.Copy).then_inc(qkT_in, 1)
                for hf in range(2):
                    rows = slice(DH * hf, DH * (hf + 1))
                    act.activation(qbd[rows, :, W * hf:W * (hf + 1)], q[rows], ACT.Copy,
                                   scale=SCALE).then_inc(qkT_in, 1)

            def b_exp(p, b, i):
                u = 4 * p + b
                if i == 0:
                    act.wait_ge(max_in, u + 1)
                    at_least(act, pT_out, u - 1)
                for w in range(4 * i, 4 * i + 4):
                    t = act.activation(pB[:, b % 2, w, :], ps[:, 4 + w // 4, (w % 4) * P:(w % 4 + 1) * P], ACT.Exp,
                                       bias=nmB[:, b % 2, w:w + 1], accum_out=rsB[:, b % 2, w:w + 1])
                if i == 1:
                    t.then_inc(exp_in, 1)

            def b_mixed(p, b, i):
                u = 4 * p + b
                act.wait_ge(ax_out, 2 * u + i + 1)
                if i == 0:
                    at_least(act, out_out, u - 1)
                act.activation(axB[:, b % 2, 4 * i:4 * i + 4, :],
                               ps[:, 6, :].rearrange("p (w n) -> p w n", n=P), ACT.Copy).then_inc(ax_in, 1)

            act.wait_ge(qbd_zero, 1)
            b_turned(0, 0, 0)

            def pair(p, first, last):
                for b in range(UNITS):
                    before = (p, b - 1) if b > 0 else (None if first else (p - 1, UNITS - 1))
                    b_exp(p, b, 0)
                    if before:
                        b_mixed(*before, 0)
                    b_exp(p, b, 1)
                    if before:
                        b_mixed(*before, 1)
                    if not (last and b == UNITS - 1):
                        b_turned(p, b, 1)
            sweep(act, PAIRS, pair)
            b_mixed(PAIRS - 1, UNITS - 1, 0)
            b_mixed(PAIRS - 1, UNITS - 1, 1)

            act.wait_ge(out_out, UNITS * PAIRS)
            def gathered(it, k):
                act.wait_ge(gx_out, it * 6 + k + 1)
                act.activation(XN[:, k, :], ps[:, 4, 0:D], ACT.Copy).then_inc(xn_in, 1)

            def turned(it, k):
                act.wait_ge(xt_out, it * 6 + k + 1)
                act.activation(XT[:, k % 2, :], ps[:, 4, P:2 * P], ACT.Copy).then_inc(xt_in, 1)

            def expanded(g, it, s):
                act.wait_ge(u_out, it * 8 + s + 1)
                act.activation(U[:, :, 2 * s:2 * s + 2, :].rearrange("p w h q -> p h w q"),
                               ps[:, 0, 0:2 * WQ * NQ].rearrange("p (h w q) -> p h w q", h=2, q=NQ),
                               ACT.Copy, scale=cgs[:, g:g + 1]).then_inc(u_act, 1)

            def probs(it, w):
                n, k = (W if w == 0 else P), w % 3
                act.wait_ge(cmax_in, it * WQ + w + 1)
                for hg in range(4):
                    act.activation(pC[:, k, hg, 0:n], ps[:, 5 + k, hg * P:hg * P + n], ACT.Exp,
                                   bias=nmC[:, k, hg:hg + 1], accum_out=rsC[:, k, hg:hg + 1])
                act.activation(pnC[:, k, :], dnC[:, k, :], ACT.Exp).then_inc(cexp_in, 1)

            def mixed(it, w):
                act.wait_ge(cax_out, it * WQ + w + 1)
                act.activation(axC[:, :, w, :], ps[:, 2, :].rearrange("p (h q) -> p h q", q=NQ),
                               ACT.Copy).then_inc(cax_in, 1)

            def projected(g, b, it):
                act.wait_ge(cout_out, it + 1)
                act.activation(oT[:, bass.ds(b, 1), 0, g, NQ:].rearrange("p o s -> p (o s)"), ps[:, 0, 0:NQ], ACT.Copy)
                act.activation(oT[:, bass.ds(b, 1), 1:, g, :].rearrange("p o j s -> p (o j) s"),
                               ps[:, 0, NQ:WQ * NQ].rearrange("p (j s) -> p j s", s=W),
                               ACT.Copy).then_inc(cout_in, 1)

            act.wait_ge(oT_zero, 1)

            def sequence(g, b, it, before):
                if before:
                    mixed(before[2], 3)
                gathered(it, 0)
                expanded(g, it, 0)
                turned(it, 0)
                expanded(g, it, 2)
                if before:
                    mixed(before[2], 4)
                expanded(g, it, 4)
                gathered(it, 1)
                if before:
                    mixed(before[2], 5)
                turned(it, 1)
                expanded(g, it, 6)
                if before:
                    mixed(before[2], 6)
                gathered(it, 2)
                probs(it, 0)
                turned(it, 2)
                probs(it, 1)
                probs(it, 2)
                if before:
                    projected(*before)
                for w in range(WQ - 3):
                    if w + 3 <= 5:
                        gathered(it, w + 3)
                    if w > 0:
                        mixed(it, w - 1)
                    if w + 3 <= 5:
                        turned(it, w + 3)
                    probs(it, w + 3)

            sequences(act, sequence)
            mixed(LAST[2], 3)
            mixed(LAST[2], 4)
            mixed(LAST[2], 5)
            mixed(LAST[2], 6)
            projected(*LAST)

            for b in range(B):
                act.wait_ge(ft_out, b + 1)
                if b >= 2:
                    act.wait_ge(fin_out, b - 1)
                for t, i in ((OHS, 0), (oN, 1)):
                    act.activation(t[:, b % 2], ps[:, i, :].rearrange("p (j n) -> p j n", j=BLK),
                                   ACT.Copy).then_inc(ft_act, 1)
                act.wait_ge(y_ready, b + 1)
                if b >= 2:
                    act.wait_ge(res_in, b - 1)
                act.activation(eN[:, b % 2], yN[:, b % 2], ACT.Exp, scale=-1.0).then_inc(e_ready, 1)

        @block.vector
        def _(dve):
            def rsqrt_step(n0, n1):
                r, v, t = rs3[:, n0:n1], var3[:, n0:n1], tmp3[:, n0:n1]
                dve.tensor_tensor(t, r, r, ALU.mult)
                dve.drain()
                dve.tensor_tensor(t, t, v, ALU.mult)
                dve.drain()
                dve.tensor_scalar(t, t, -0.5, 1.5, ALU.mult, ALU.add)
                dve.drain()
                dve.tensor_tensor(r, r, t, ALU.mult)
                dve.drain()

            for b in range(B):
                dve.wait_ge(s_x[b], 16)
                for k in range(b * BLK, (b + 1) * BLK):
                    dve.bn_stats(stats[:, k, :], x[:, k, :])
            dve.drain()
            for k in range(NB):
                dve.bn_aggr(mv[:, k, :], stats[:, k, :])
            dve.drain()
            dve.tensor_scalar(var3[:, 0, :], mv[:, :, 1], 1e-5, None, ALU.add).then_inc(s_var, 1)
            dve.wait_ge(s_ln, 1)
            rsqrt_step(0, 1)
            for k in range(NB):
                t = dve.tensor_scalar(xn[:, k, :], x[:, k, :], mv[:, k, 0:1], rs3[:, 0, k:k + 1],
                                      ALU.subtract, ALU.mult)
                if k % BLK == BLK - 1:
                    t.then_inc(s_xn, 1)
            dve.tensor_tensor(tmp3[:, 0, :], rs3[:, 0, :], rs3[:, 0, :], ALU.mult)
            dve.drain()
            dve.tensor_tensor(tmp3[:, 0, :], tmp3[:, 0, :], mv[:, :, 1], ALU.mult)
            dve.drain()
            dve.tensor_scalar(var3[:, 1, :], tmp3[:, 0, :], 1e-5, None, ALU.add)
            dve.tensor_scalar(var3[:, 2, :], tmp3[:, 0, :], 1e-24 / D, 2.0**40, ALU.max, ALU.mult).then_inc(s_var, 1)
            dve.wait_ge(s_ln, 2)
            rsqrt_step(1, 3)
            for k in range(NB):
                t = dve.tensor_scalar(xh2[:, k, :], xn[:, k, :], rs3[:, 1, k:k + 1], None, ALU.mult)
                if k % BLK == BLK - 1:
                    t.then_inc(s_xh2, 1)
            for k in range(NB):
                t = dve.tensor_scalar(xhat[:, k, :], xn[:, k, :], rs3[:, 2, k:k + 1], 2.0**20, ALU.mult, ALU.mult)
            t.then_inc(s_xhat, 1)
            dve.wait_ge(s_const, 16 * N_CONST)
            dve.memset(RS[:], 0.0)
            dve.drain()
            qrows = slice(Q_AT, Q_AT + Q_ROWS)
            dve.tensor_copy(RS[qrows, W:], rmask[qrows, W:])
            dve.wait_ge(logits, 2)
            dve.tensor_tensor(RS[0:KV_ROWS, :], ps[0:KV_ROWS, 0, 0:CTX], rmask[0:KV_ROWS, :], ALU.add)
            dve.tensor_copy(RS[qrows, 0:W], ps[qrows, 1, 0:W])
            dve.drain()
            dve.tensor_reduce(rsmax[:], RS[:], AX.X, ALU.max)
            dve.memset(rm[:], 0.0)
            dve.drain()
            dve.nop().then_inc(r_start, 1)

            def new_bound(i):
                dve.wait_ge(r_l, i + 1)
                dve.tensor_scalar(rna[:], rln[:], eps[:, 1, bass.ds(i, 1)], rm[:, 0:1], ALU.mult, ALU.add)
                dve.drain()

            def descend(i):
                new_bound(i - 1)
                dve.tensor_tensor(rm[:], rsmax[:], rna[:], ALU.min)
                dve.drain()
                dve.tensor_scalar(RU[:], RS[:], rna[:, 0:1], rm[:, 0:1], ALU.min, ALU.subtract).then_inc(r_u, 1)

            def pick(rows, n):
                dve.max(rm8[rows, :], RU[rows, 0:n])
                dve.drain()
                dve.match_replace(RU[rows, 0:n], rm8[rows, :], RU[rows, 0:n], TAKEN)
                dve.drain()

            def a_v(h, b):
                dve.wait_ge(v_out, 4 * h + b + 1)
                dve.tensor_copy(vN[:, b % 2], ps[:, 7, :].rearrange("p (k d) -> p k d", d=D)).then_inc(v_in, 1)

            def a_diag(h, b):
                dve.wait_ge(sc_out, 3 * (4 * h + b) + 1)
                blocks = lambda t: t.rearrange("p (m n) -> p m n", n=P)
                dve.scalar_tensor_tensor(out=blocks(simA[:, b % 2, 0, :]), in0=blocks(ps[:, 4, :]), scalar=0.0,
                                         in1=causal[:].unsqueeze(1).broadcast_to([P, BLK, P]),
                                         op0=ALU.max, op1=ALU.mult).then_inc(diag_in, 1)

            a_v(0, 0)

            def head(h, first, last):
                for b in range(UNITS):
                    a_diag(h, b)
                    if not (last and b == UNITS - 1):
                        a_v(*((h, b + 1) if b < UNITS - 1 else (h + 1, 0)))
                    if first and b == 2:
                        descend(1)
                    if not first and not last and b < 3:
                        descend(3 * h - 1 + b)
                    if last:
                        if b == 0:
                            new_bound(NITER - 1)
                            dve.tensor_scalar(RU[:], RS[:], rna[:, 0:1], 0.0, ALU.subtract, ALU.min)
                            dve.drain()
                            dve.tensor_scalar(RU[:], RU[:], 1.0 / EPS[NITER], LOWEST, ALU.mult, ALU.max)
                            dve.drain()
                        for _ in range(NKV // 8 // UNITS):
                            pick(slice(0, KV_ROWS), CTX)
                        pick(qrows, W)
            sweep(dve, HA, head)
            assert NQ // 8 == UNITS
            dve.tensor_scalar(RS[:], RU[:], TAKEN / 2, None, ALU.is_lt)
            dve.drain()
            dve.memset(RU[:], 1.0)
            dve.drain()
            dve.tensor_tensor_scan(RE[:], RU[:], RS[:], 0.0, ALU.mult, ALU.add)
            dve.drain()
            dve.scalar_tensor_tensor(out=RE[:], in0=RE[:], scalar=half[:, 0:1], in1=RS[:], op0=ALU.add, op1=ALU.mult)
            dve.drain()
            for i in range(2):
                t = dve.tensor_scalar(qhalf[qrows, i * W:(i + 1) * W], RE[qrows, 0:W], half[qrows, i + 1:i + 2],
                                      None, ALU.mult)
            t.then_inc(codes, 1)

            def b_rope(p, b, ahead):
                u = 4 * p + b + ahead
                k, c = (b + ahead) % 2, (b + ahead) % UNITS
                dve.wait_ge(qk_out, u + 1)
                at_least(dve, rot_in, u - 1)
                src = ps[:, 0:2].rearrange("p k (a h e) -> p (k a) h e", a=2, e=DH)
                e2 = DH // 2
                table = lambda t, lo, n: t[:, :, lo:lo + n].unsqueeze(2).broadcast_to([P, BLK, 4, n])
                dve.tensor_tensor(r1[:, k], src, table(cos, 0, DH), ALU.mult)
                dve.tensor_tensor(r2[:, k, :, :, 0:e2], src[:, :, :, e2:DH], table(sin, 0, e2), ALU.mult)
                dve.tensor_tensor(r2[:, k, :, :, e2:DH], src[:, :, :, 0:e2], table(sin, e2, e2),
                                  ALU.mult).then_inc(roped, 1)

            def b_max(p, b):
                dve.wait_ge(sim_out, 4 * p + b + 1)
                dve.tensor_reduce(nmB[:, b % 2, :], ps[:, 4:6].rearrange("p k (w n) -> p (k w) n", n=P), AX.X,
                                  ALU.max, negate=True).then_inc(max_in, 1)

            def b_norm(p, b):
                dve.wait_ge(exp_in, 4 * p + b + 1)
                dve.reciprocal(riB[:], rsB[:, b % 2, :])
                dve.drain()
                dve.tensor_tensor(pB[:, b % 2], pB[:, b % 2], riB[:].unsqueeze(2).broadcast_to([P, NW, P]),
                                  ALU.mult).then_inc(norm_in, 1)

            def b_probs(p, b):
                u = 4 * p + b
                dve.wait_ge(pT_out, u + 1)
                at_least(dve, ax_out, 2 * u - 2)
                dve.tensor_copy(pTB[:, b % 2], ps[:, 2:4].rearrange("p k (w n) -> p (k w) n", n=P)).then_inc(pT_in, 1)

            def b_add(p, b):
                dve.wait_ge(out_out, 4 * p + b + 1)
                dve.tensor_tensor(loc[:, b, :], loc[:, b, :], ps[:, 7, :], ALU.add).then_inc(loc_in, 1)

            dve.wait_ge(pv_done, 1)
            dve.wait_ge(loc_zero, 1)
            b_rope(0, 0, 0)
            b_rope(0, 0, 1)

            def pair(p, first, last):
                for b in range(UNITS):
                    before = (p, b - 1) if b > 0 else (None if first else (p - 1, UNITS - 1))
                    b_max(p, b)
                    if not (last and b >= 2):
                        b_rope(p, b, 2)
                    b_norm(p, b)
                    if before:
                        b_add(*before)
                    b_probs(p, b)
            sweep(dve, PAIRS, pair)
            b_add(PAIRS - 1, UNITS - 1)

            dve.wait_ge(code_out, 1)
            dve.wait_ge(loc_in, UNITS * PAIRS)
            dve.memset(pC[:, 0], 0.0)
            dve.memset(kvcode[:, 3], 0.0)
            dve.drain()
            dve.tensor_copy(kvcode[:, 0:3, :], ps[:, 4, 0:3 * KV_ROWS].rearrange("p (c r) -> p c r", c=3))
            dve.tensor_copy(kvcode[0:W, 3, :], ps[0:W, 4, 3 * KV_ROWS:4 * KV_ROWS])
            dve.tensor_copy(qrow_t[:], ps[:, 5, 0:Q_ROWS])
            dve.drain()
            gb = G * B
            dve.tensor_copy(qcode[:, 0, :], qrow_t[:, 0:gb])
            odd_even = qrow_t[:, gb:].rearrange("p (j o r) -> p j o r", o=2, r=gb)
            dve.tensor_tensor(qcode[:, 1:, :], odd_even[:, :, 0, :], odd_even[:, :, 1, :], ALU.add)
            dve.drain()
            for b in range(B):
                for j in range(BLK):
                    for g in range(G):
                        r = g * B + b
                        t = dve.tensor_scalar(OHQ[:, b * BLK + j, g * W:(g + 1) * W], iota[:, 0:W],
                                              qcode[:, j, r:r + 1], None, ALU.is_equal)
                t.then_inc(ohq_in, 1)
            dve.tensor_scalar(rcount[:], qcode[:], 0.5, None, ALU.is_gt)
            dve.drain()
            dve.tensor_tensor(rcnt[:], rcount[:, :, 0:B], rcount[:, :, B:], ALU.add)
            dve.drain()
            dve.tensor_scalar(rcnt[:], rcnt[:], 1.0, None, ALU.add)
            dve.drain()
            dve.reciprocal(rcnt[:], rcnt[:])
            for b in range(B):
                dve.wait_ge(qsel_out, b + 1)
                dve.tensor_copy(qsel[:, :, b, :].rearrange("p g (j s) -> p g j s", s=W),
                                ps[:, b, :].rearrange("p (j g s) -> p g j s", g=G, s=W)).then_inc(qsel_in, 1)

            def expanded(g, it, s):
                dve.wait_ge(u_out, it * 8 + s + 1)
                dve.tensor_scalar(U[:, :, 2 * s:2 * s + 2, :].rearrange("p w h q -> p h w q"),
                                  ps[:, 1, 0:2 * WQ * NQ].rearrange("p (h w q) -> p h w q", h=2, q=NQ),
                                  cgs[:, g:g + 1], None, ALU.mult).then_inc(u_dve, 1)

            def null_logits(it):
                dve.wait_ge(null_out, it + 1)
                dve.tensor_tensor(ntmp, ps[:, 1, 0:WQ * H].rearrange("p (w h) -> p w h", h=H),
                                  own[:].unsqueeze(1).broadcast_to([P, WQ, H]), ALU.mult)
                dve.drain()
                dve.tensor_reduce(nsC[:], ntmp.rearrange("p w (a b) -> p (w a) b", b=4), AX.X, ALU.add,
                                  negate=True)
                dve.drain()
                dve.tensor_scalar(nsC[:], nsC[:], SCALE, None, ALU.mult).then_inc(null_in, 1)
                dve.drain()

            def maxima(it, w):
                n, k = (W if w == 0 else P), w % 3
                dve.wait_ge(csim_out, it * WQ + w + 1)
                nm = nmC[:, k, :]
                null = nsC[:, 4 * w:4 * w + 4]
                dve.tensor_reduce(nm, ps[:, 5 + k, :].rearrange("p (h n) -> p h n", n=P)[:, :, 0:n], AX.X,
                                  ALU.max, negate=True)
                dve.drain()
                dve.tensor_tensor(nm, nm, null, ALU.min)
                dve.drain()
                dve.tensor_tensor(dnC[:, k, :], nm, null, ALU.subtract).then_inc(cmax_in, 1)

            def norms(it, w):
                n, k = (W if w == 0 else P), w % 3
                dve.wait_ge(cexp_in, it * WQ + w + 1)
                dve.tensor_tensor(riC[:], rsC[:, k, :], pnC[:, k, :], ALU.add)
                dve.drain()
                dve.reciprocal(riC[:], riC[:])
                dve.drain()
                dve.tensor_tensor(pnall[:, 4 * w:4 * w + 4], pnC[:, k, :], riC[:], ALU.mult)
                dve.tensor_tensor(pC[:, k, :, 0:n], pC[:, k, :, 0:n],
                                  riC[:].unsqueeze(2).broadcast_to([P, 4, n]), ALU.mult).then_inc(cnorm_in, 1)

            def probs_turned(it, w):
                n = W if w == 0 else P
                dve.wait_ge(cpT_out, it * WQ + w + 1)
                at_least(dve, cax_out, it * WQ + w - 1)
                dve.tensor_copy(pTC[0:n, w % 2, :], ps[0:n, 3, :]).then_inc(cpT_in, 1)

            def spread_null(it):
                dve.drain()
                at_least(dve, pnT_out, it)
                dve.tensor_tensor(pn16[:], pnall[:].unsqueeze(2).broadcast_to([P, WQ * 4, 4]),
                                  own[:, 0:4].unsqueeze(1).broadcast_to([P, WQ * 4, 4]),
                                  ALU.mult).then_inc(pn16_in, 1)

            def null_turned(it):
                dve.wait_ge(pnT_out, it + 1)
                dve.tensor_copy(pnT[:], ps[0:H, 1, 256:256 + WQ * NQ]).then_inc(pnT_in, 1)

            def sequence(g, b, it, before):
                expanded(g, it, 1)
                if before:
                    pit = before[2]
                    dve.drain()
                    norms(pit, 6)
                    probs_turned(pit, 5)
                expanded(g, it, 3)
                if before:
                    probs_turned(pit, 6)
                    spread_null(pit)
                expanded(g, it, 5)
                expanded(g, it, 7)
                null_logits(it)
                maxima(it, 0)
                maxima(it, 1)
                norms(it, 0)
                maxima(it, 2)
                if before:
                    null_turned(pit)
                norms(it, 1)
                probs_turned(it, 0)
                for w in range(WQ - 3):
                    maxima(it, w + 3)
                    norms(it, w + 2)
                    probs_turned(it, w + 1)

            sequences(dve, sequence)
            it = LAST[2]
            dve.drain()
            norms(it, 6)
            probs_turned(it, 5)
            spread_null(it)
            probs_turned(it, 6)
            null_turned(it)

            for b in range(B):
                k = b % 2
                dve.wait_ge(ft_out, b + 1)
                dve.tensor_copy(sN[:, k], ps[:, 2, :].rearrange("p (j n) -> p j n", j=BLK)).then_inc(ft_dve, 1)
                dve.wait_ge(fin_out, b + 1)
                dve.tensor_tensor(yN[:, k], ps[:, 3 + k, :].rearrange("p (j n) -> p j n", j=BLK),
                                  rcnt[:, :, b:b + 1].broadcast_to([P, BLK, D]), ALU.mult).then_inc(y_ready, 1)
                dve.wait_ge(e_ready, b + 1)
                dve.drain()
                dve.tensor_tensor(sN[:, k], sN[:, k], yN[:, k], ALU.mult)
                dve.tensor_scalar(eN[:, k], eN[:, k], 1.0, None, ALU.add)
                dve.drain()
                dve.reciprocal(eN[:, k], eN[:, k])
                dve.drain()
                dve.tensor_tensor(sN[:, k], sN[:, k], eN[:, k], ALU.mult)
                dve.drain()
                dve.tensor_tensor(res[:, b * BLK:(b + 1) * BLK, :], sN[:, k], x[:, b * BLK:(b + 1) * BLK, :],
                                  ALU.add).then_inc(res_in, 1)


def kernel(L0_attn_x, L0_attn_Wq, L0_attn_Wk, L0_attn_Wv, L0_ffn_ln_g, L0_ffn_ln_b, L0_ffn_w_qkv, L0_ffn_w_lo,
           L0_ffn_rt_q, L0_ffn_rt_kv, L0_ffn_qnorm_g, L0_ffn_cnorm_g, L0_ffn_null_kv, L0_ffn_w_q, L0_ffn_w_kv,
           L0_ffn_w_out):
    import concourse.bacc as _bacc
    from concourse.bass_utils import run_bass_kernel_spmd as _run

    a = lambda t: np.asarray(t)
    inner = H * DH
    qkv = a(L0_ffn_w_qkv)
    rows = lambda w: w.reshape(PAIRS, P, D).transpose(1, 0, 2)
    grouped = lambda w: w.reshape(G * PAIRS, P, D).transpose(1, 0, 2)
    kv, null = a(L0_ffn_w_kv), a(L0_ffn_null_kv)
    arrays = {
        "x": a(L0_attn_x), "Wq": a(L0_attn_Wq), "Wk": a(L0_attn_Wk),
        "WvT": a(L0_attn_Wv).transpose(2, 0, 1),
        "ln_g": a(L0_ffn_ln_g).reshape(D, 1), "ln_b": a(L0_ffn_ln_b).reshape(D, 1),
        "wqk": qkv[:2 * inner].reshape(2, PAIRS, P, D).transpose(3, 1, 0, 2).reshape(D, PAIRS, 2 * P),
        "bv": rows(qkv[2 * inner:]), "bo": rows(a(L0_ffn_w_lo).T),
        "qg": a(L0_ffn_qnorm_g).T, "cg": a(L0_ffn_cnorm_g).T,
        "rt_q": a(L0_ffn_rt_q).T, "rt_kv": a(L0_ffn_rt_kv).T,
        "cq": grouped(a(L0_ffn_w_q)), "ck": grouped(kv[:, :inner]), "cv": grouped(kv[:, inner:]),
        "co": grouped(a(L0_ffn_w_out).transpose(0, 2, 1)),
        "null": null.reshape(2, G, PAIRS, P).transpose(3, 0, 1, 2),
        **shape_constants(),
    }
    arrays = {f"in_{k}": np.ascontiguousarray(v) for k, v in arrays.items()}
    nc = _bacc.Bacc("TRN2", target_bir_lowering=False, num_devices=1)
    dram = {k[3:]: nc.dram_tensor(k, v.shape, mybir.dt.from_np(v.dtype), kind="ExternalInput").ap()
            for k, v in arrays.items()}
    out = nc.dram_tensor("out", (B, N, D), F32, kind="ExternalOutput").ap()
    build(nc, dram, out)
    r = _run(nc, [arrays], core_ids=[0])
    return r.results[0]["out"]
```

```python
from contextlib import ExitStack

import numpy as np

import concourse.bass as bass
from concourse import mybir

P = 128
B, N, D = 4, 512, 128
BLK = N // P
NB = B * BLK
HA = 8
DH = 64
H = 16
PAIRS = H // 2
W = 64
NW = N // W
ON_ACT = (3, 4)
WQ = NW - 1
G = 2
NQ, NKV = 32, 128
NITER = 20
CTX = N - W
KV_W0 = 2
KV_ROWS = (WQ - KV_W0) * B * G
Q_ROWS = WQ * B * G
Q_AT = 64
NEG = -1.0e30
TAKEN = -3.0e38
EPS = [max(4.0 * 0.7**i, 0.03) for i in range(NITER + 1)]
LOWEST = -87.33655
SCALE = DH**-0.5
UNITS = 4

F32 = mybir.dt.float32
BF16 = mybir.dt.bfloat16
ALU = mybir.AluOpType
ACT = mybir.ActivationFunctionType
AX = mybir.AxisListType


def kv_row(w, g, b):
    return (w - KV_W0) * G * B + g * B + b


def q_row(w, g, b):
    return w * G * B + g * B + b


def shape_constants():
    f = np.float32
    c = {}
    c["ident"] = np.eye(P, dtype=f)
    i = np.arange(P)
    c["causal"] = ((i[:, None] <= i[None, :]) / f(N)).astype(f)
    inv = (f(1.0) / np.power(f(10000.0), np.arange(0, DH, 2, dtype=f) / f(DH))).astype(f)
    ang = (np.arange(N, dtype=f)[:, None] * inv[None, :]).astype(f)
    cos, sin = np.cos(ang).astype(f), np.sin(ang).astype(f)
    by_block = lambda t: t.reshape(BLK, P, -1).transpose(1, 0, 2).copy()
    c["cos"] = by_block(np.concatenate([cos, cos], 1))
    c["sin"] = by_block(np.concatenate([-sin, sin], 1))
    q, k = np.arange(P)[:, None] % W, np.arange(P)[None, :]
    first = np.where(k <= q, 0.0, NEG)
    later = np.where((k >= q) & (k - W <= q), 0.0, NEG)
    c["window"] = np.concatenate([first] + [later] * 4, 1).astype(f)
    rmask = np.zeros((P, CTX), f)
    rinvk = np.ones((P, 1), f)
    half = np.zeros((P, 3), f)
    for g in range(G):
        for b in range(B):
            for w in range(KV_W0, WQ):
                rmask[kv_row(w, g, b), W * (w + 1):] = NEG
                rinvk[kv_row(w, g, b)] = 1.0 / (NKV * 9.0 / 8.0)
            for w in range(WQ):
                r = Q_AT + q_row(w, g, b)
                rmask[r, W:] = NEG
                rinvk[r] = 1.0 / (NQ * 9.0 / 8.0)
                odd = (w + 1) % 2
                half[r] = [NQ * odd, 1 - odd, odd]
    c["rmask"], c["rinvk"], c["half"] = rmask, rinvk, half
    e = np.array(EPS[:NITER], np.float64)
    c["eps"] = np.tile(np.stack([1.0 / e, e]).astype(f)[None], (P, 1, 1))
    c["iota"] = np.tile(np.arange(1, P + 1, dtype=f), (P, 1))
    h4, qq = np.arange(P) // NQ, np.arange(P) % NQ
    c["own"] = (h4[:, None] == np.arange(H)[None, :] % 4).astype(f)
    c["fold"] = (qq[:, None] == np.arange(NQ)[None, :]).astype(f)
    return c


CONSTS = ["ident", "causal", "cos", "sin", "window", "rmask", "rinvk", "half", "eps", "iota", "own", "fold"]


def build(nc, dram, out):
    ctx = ExitStack()
    with ctx:
        def sb(name, shape, dt=F32):
            return ctx.enter_context(nc.sbuf_tensor(name, shape, dt))

        def sem(name):
            return ctx.enter_context(nc.semaphore(name))

        x = sb("x", [P, NB, D])
        xhat = sb("xhat", [P, NB, D])
        G2 = sb("G2", [P, G * H, D])
        W2C = sb("W2C", [P, G * H, D])
        sT = sb("sT", [P, B, N])
        loc = sb("loc", [P, B, N])
        ident = sb("ident", [P, P])
        identb = sb("identb", [P, P], BF16)
        causal = sb("causal", [P, P])
        zerob = sb("zerob", [P, N], BF16)
        cos = sb("cos", [P, BLK, DH])
        sin = sb("sin", [P, BLK, DH])
        windowf = sb("windowf", [P, 5 * P])
        windowb = sb("windowb", [P, 5 * P], BF16)
        rmask = sb("rmask", [P, CTX])
        rinvk = sb("rinvk", [P, 1])
        half = sb("half", [P, 3])
        eps = sb("eps", [P, 2, NITER])
        iota = sb("iota", [P, P])
        own = sb("own", [P, H])
        fold = sb("fold", [P, NQ])
        lng = sb("lng", [P, 1])
        lnb = sb("lnb", [P, 1])
        qg = sb("qg", [P, G])
        nkv = sb("nkv", [P, 2, G, PAIRS])
        cg = sb("cg", [P, G])
        cgs = sb("cgs", [P, G])
        rtq = sb("rtq", [P, G])
        rtk = sb("rtk", [P, G])
        NK = sb("NK", [P, G, H])
        NV = sb("NV", [H, G, D])
        wscr = sb("wscr", [P, 2, D])
        gscr = sb("gscr", [P, D])
        RS = sb("RS", [P, CTX])
        RU = sb("RU", [P, CTX])
        RE = sb("RE", [P, CTX])
        rsmax = sb("rsmax", [P, 1])
        rm = sb("rm", [P, 1])
        rna = sb("rna", [P, 1])
        rsum = sb("rsum", [P, 1])
        rln = sb("rln", [P, 1])
        rm8 = sb("rm8", [P, 8])
        qhalf = sb("qhalf", [P, P])
        kvcode = sb("kvcode", [P, 4, KV_ROWS])
        kvcol = sb("kvcol", [P, 2, 4])
        qrow_t = sb("qrow_t", [P, Q_ROWS])
        qcode = sb("qcode", [P, BLK, G * B])
        rcount = sb("rcount", [P, BLK, G * B])
        rcnt = sb("rcnt", [P, BLK, B])

        EARLY = 14080
        early = sb("early", [P, EARLY])
        STAGE = 14720
        stage = sb("stage", [P, STAGE])

        def part(region, at, shape):
            size = int(np.prod(shape))
            names = "abcd"[:len(shape)]
            v = region[:, at:at + size]
            if len(shape) == 1:
                return v, at + size
            spec = f"p ({' '.join(names)}) -> p {' '.join(names)}"
            return v.rearrange(spec, **{n: s for n, s in zip(names, shape)}), at + size

        o = 0
        xnT, o = part(early, o, [B, N])
        xlnT, o = part(early, o, [B, N])
        xln, o = part(early, o, [B * 7, D])
        early_of_projections = o
        wqk, o = part(early, o, [PAIRS, 2 * P])
        W2B, o = part(early, o, [H, D])
        dead_in_b = o
        GA, o = part(early, o, [HA, D])
        wvT, o = part(early, o, [HA, D])
        assert o <= EARLY, o

        o = 0
        xn = sT[:].rearrange("p b (k d) -> p (b k) d", d=D)
        xh2 = loc[:].rearrange("p b (k d) -> p (b k) d", d=D)
        bv, o = part(stage, o, [PAIRS, D])
        bo, o = part(stage, o, [PAIRS, D])
        aq, o = part(stage, o, [HA, D])
        ak, o = part(stage, o, [HA, D])
        RTk, o = part(stage, o, [B, KV_ROWS])
        RTq, o = part(stage, o, [WQ * B, Q_ROWS])
        before_routed = o
        nkb, o = part(stage, o, [G, PAIRS, H])
        nvb, o = part(stage, o, [G, PAIRS, H])
        routed_weights = o
        cq, o = part(stage, o, [G * PAIRS, D])
        ck, o = part(stage, o, [G * PAIRS, D])
        cv, o = part(stage, o, [G * PAIRS, D])
        co, o = part(stage, o, [G * PAIRS, D])
        assert o <= STAGE, o
        stats = sb("stats", [P, NB, 6])
        mv = sb("mv", [P, NB, 2])
        var3 = sb("var3", [P, 3, NB])
        rs3 = sb("rs3", [P, 3, NB])
        tmp3 = sb("tmp3", [P, 3, NB])

        o = 0
        yT, o = part(stage, o, [2, N])
        vN, o = part(stage, o, [2, BLK, D])
        simA, o = part(stage, o, [2, 3, N])
        assert o <= before_routed, o
        end_of_a = o

        o = 0
        pB, o = part(stage, o, [2, NW, P])
        pTB, o = part(stage, o, [2, NW, P])
        kT, o = part(stage, o, [N])
        o = end_of_a
        qbd, o = part(stage, o, [NW, P])
        assert o <= routed_weights, o
        o = routed_weights
        r1, o = part(stage, o, [2, BLK, 4, DH])
        r2, o = part(stage, o, [2, BLK, 4, DH])
        rot, o = part(stage, o, [2, BLK, 2 * P])
        axB, o = part(stage, o, [2, NW, P])
        nmB = sb("nmB", [P, 2, NW])
        rsB = sb("rsB", [P, 2, NW])
        riB = sb("riB", [P, NW])
        assert o <= STAGE, o

        o = 0
        qsel, o = part(early, o, [G, B, 2 * P])
        pC, o = part(early, o, [3, 4, P])
        axC, o = part(early, o, [H, WQ, NQ])
        pTC, o = part(early, o, [2, 4 * P])
        assert o >= early_of_projections, o
        U, o = part(early, o, [WQ, H, NQ])
        assert o <= dead_in_b, o
        OHQ, o = part(early, dead_in_b, [NB, P])
        assert o <= EARLY, o
        o = 0
        ntmp, o = part(stage, o, [WQ, H])
        oT, o = part(stage, o, [B, BLK, G, W])
        OHS, o = part(stage, o, [2, BLK, P])
        oN, o = part(stage, o, [2, BLK, D])
        sN, o = part(stage, o, [2, BLK, D])
        assert o <= routed_weights, o
        o = routed_weights
        XN, o = part(stage, o, [6, D])
        XT, o = part(stage, o, [2, P])
        OH, o = part(stage, o, [2, 4, P])
        qrep, o = part(stage, o, [WQ, 4, NQ])
        yN, o = part(stage, o, [2, BLK, D])
        eN, o = part(stage, o, [2, BLK, D])
        res, o = part(stage, o, [NB, D])
        assert o <= STAGE, o
        nsC = sb("nsC", [P, WQ * 4])
        nmC = sb("nmC", [P, 3, 4])
        dnC = sb("dnC", [P, 3, 4])
        pnC = sb("pnC", [P, WQ * 4])
        rsC = sb("rsC", [P, 3, 4])
        riC = sb("riC", [P, WQ * 4])
        pnall = sb("pnall", [P, WQ * 4])
        pn16 = sb("pn16", [P, WQ * 4, 4])
        pnT = sb("pnT", [H, WQ * NQ])

        ps = ctx.enter_context(nc.psum_tensor("ps", [P, 8, N], F32))

        s_x = [sem(f"s_x{b}") for b in range(B)]
        s_ident = sem("s_ident")
        s_const = sem("s_const")
        s_wa = sem("s_wa")
        s_wb = sem("s_wb")
        s_wv = sem("s_wv")
        s_wqk = sem("s_wqk")
        s_wc = sem("s_wc")
        s_null = sem("s_null")
        s_cleared = sem("s_cleared")
        s_rt = sem("s_rt")
        s_var = sem("s_var")
        s_ln = sem("s_ln")
        s_xn = sem("s_xn")
        s_xh2 = sem("s_xh2")
        s_bf = sem("s_bf")
        prep_out = sem("prep_out")
        prep_in = sem("prep_in")
        w_out = sem("w_out")
        w_in = sem("w_in")
        logits = sem("logits")
        r_start = sem("r_start")
        r_u = sem("r_u")
        r_l = sem("r_l")
        g_loaded = sem("g_loaded")
        y_out = sem("y_out")
        y_in = sem("y_in")
        v_out = sem("v_out")
        v_in = sem("v_in")
        sc_out = sem("sc_out")
        relu_in = sem("relu_in")
        diag_in = sem("diag_in")
        pv_done = sem("pv_done")
        sT_in = sem("sT_in")
        codes = sem("codes")
        qk_out = sem("qk_out")
        roped = sem("roped")
        rot_in = sem("rot_in")
        qkT_out = sem("qkT_out")
        qT_in = sem("qT_in")
        kT_in = sem("kT_in")
        sim_out = sem("sim_out")
        max_in = sem("max_in")
        exp_in = sem("exp_in")
        norm_in = sem("norm_in")
        pT_out = sem("pT_out")
        pT_in = sem("pT_in")
        ax_out = sem("ax_out")
        ax_in = sem("ax_in")
        w2_loaded = sem("w2_loaded")
        out_out = sem("out_out")
        loc_in = sem("loc_in")
        loc_zero = sem("loc_zero")
        qbd_zero = sem("qbd_zero")
        code_out = sem("code_out")
        qcode_in = sem("qcode_in")
        ohq_in = sem("ohq_in")
        qsel_out = sem("qsel_out")
        qsel_in = sem("qsel_in")
        rep_in = sem("rep_in")
        oT_zero = sem("oT_zero")
        u_out = sem("u_out")
        u_act = sem("u_act")
        u_dve = sem("u_dve")
        null_out = sem("null_out")
        null_in = sem("null_in")
        oh_in = sem("oh_in")
        gx_out = sem("gx_out")
        xn_in = sem("xn_in")
        xt_out = sem("xt_out")
        xt_in = sem("xt_in")
        csim_out = sem("csim_out")
        cmax_in = sem("cmax_in")
        cexp_in = sem("cexp_in")
        cnorm_in = sem("cnorm_in")
        cpT_out = sem("cpT_out")
        cpT_in = sem("cpT_in")
        cax_out = sem("cax_out")
        cax_in = sem("cax_in")
        pn16_in = sem("pn16_in")
        pnT_out = sem("pnT_out")
        pnT_in = sem("pnT_in")
        cout_out = sem("cout_out")
        cout_in = sem("cout_in")
        ft_out = sem("ft_out")
        ft_in = sem("ft_in")
        fin_out = sem("fin_out")
        y_ready = sem("y_ready")
        sy_ready = sem("sy_ready")
        e_ready = sem("e_ready")
        res_in = sem("res_in")
        s_out = sem("s_out")

        N_CONST = len(CONSTS) - 1 + 7

        def at_least(eng, s, n):
            if not isinstance(n, int) or n > 0:
                eng.wait_ge(s, n)

        def sweep(eng, n, body):
            body(0, True, False)
            with eng.Fori(1, n - 1) as i:
                body(i, False, False)
            body(n - 1, False, True)

        def sequences(eng, body):
            body(0, 0, 0, None)
            for g in range(G):
                if g > 0:
                    body(g, 0, g * B, (g - 1, B - 1, g * B - 1))
                with eng.Fori(1, B) as b:
                    body(g, b, b + g * B, (g, b - 1, b + (g * B - 1)))

        LAST = (G - 1, B - 1, G * B - 1)

        A_STEPS = [[(m, m * P, m * P, (m + 1) * P) for m in range(BLK)],
                   [(0, 0, P, N), (2, 3 * P, 3 * P, N)],
                   [(1, 0, 2 * P, N)]]

        block = ctx.enter_context(nc.Block())

        J_GA, J_W2B, J_XNT, J_XLNT, J_XLN, J_END = 0, 2, 6, 10, 14, 21
        W_NULL, W_W2C = 2 * UNITS, 2 * UNITS + 1
        STEP_HEADS = NITER // UNITS

        @block.sync
        def _(sp):
            xv = dram["x"].rearrange("b (k p) d -> p (b k) d", p=P)
            for b in range(B):
                sp.dma_start(x[:, b * BLK:(b + 1) * BLK, :], xv[:, b * BLK:(b + 1) * BLK, :]).then_inc(s_x[b], 16)
            sp.dma_start(aq[:], dram["Wq"].rearrange("h e d -> e h d")).then_inc(s_wa, 16)
            sp.dma_start(ak[:], dram["Wk"].rearrange("h e d -> e h d")).then_inc(s_wa, 16)
            sp.dma_start(ident[:], dram["ident"]).then_inc(s_ident, 16)
            sp.dma_start(bv, dram["bv"]).then_inc(s_wb, 16)
            sp.dma_start(bo, dram["bo"]).then_inc(s_wb, 16)
            sp.dma_start(rtq[:], dram["rt_q"]).then_inc(s_const, 16)
            sp.dma_start(rtk[:], dram["rt_kv"]).then_inc(s_const, 16)
            sp.dma_start(lng[:], dram["ln_g"]).then_inc(s_const, 16)
            sp.dma_start(lnb[:], dram["ln_b"]).then_inc(s_const, 16)
            sp.dma_start(qg[:], dram["qg"]).then_inc(s_const, 16)
            sp.dma_start(cg[:], dram["cg"]).then_inc(s_const, 16)
            sp.dma_start(nkv[:], dram["null"]).then_inc(s_const, 16)
            tiles = [causal, cos, sin, windowf, rmask, rinvk, half, eps, iota, own, fold]
            for name, t in zip(CONSTS[1:], tiles):
                sp.dma_start(t[:], dram[name]).then_inc(s_const, 16)
            sp.dma_start(wvT, dram["WvT"]).then_inc(s_wv, 16)
            for t, name in ((cq, "cq"), (ck, "ck"), (cv, "cv"), (co, "co")):
                sp.dma_start(t, dram[name]).then_inc(s_wc, 16)
            sp.dma_start(wqk, dram["wqk"]).then_inc(s_wqk, 16)
            ov = out.rearrange("b (k p) d -> p (b k) d", p=P)
            for b in range(B):
                sp.wait_ge(res_in, b + 1)
                sp.dma_start(ov[:, b * BLK:(b + 1) * BLK, :], res[:, b * BLK:(b + 1) * BLK, :]).then_inc(s_out, 16)
            sp.wait_ge(s_out, 16 * B)

        @block.gpsimd
        def _(pool):
            pool.memset(nkb, 0.0).then_inc(s_cleared, 1)
            pool.memset(nvb, 0.0).then_inc(s_cleared, 1)
            pool.memset(RTk, 0.0).then_inc(s_cleared, 1)
            pool.memset(RTq, 0.0).then_inc(s_cleared, 1)
            pool.wait_ge(s_cleared, 4)
            pool.wait_ge(s_const, 16 * N_CONST)
            pool.wait_ge(s_ident, 16)
            flat = RTk.rearrange("p b r -> p (b r)")
            for w in range(KV_W0, WQ):
                for g in range(G):
                    at = kv_row(w, g, 0)
                    pool.tensor_copy(flat[:, at:at + (B - 1) * (KV_ROWS + 1) + 1:KV_ROWS + 1],
                                     rtk[:, g:g + 1].broadcast_to([P, B]))
            flat = RTq.rearrange("p c r -> p (c r)")
            for w in range(WQ):
                for g in range(G):
                    at = w * B * Q_ROWS + q_row(w, g, 0)
                    last = pool.tensor_copy(flat[:, at:at + (B - 1) * (Q_ROWS + 1) + 1:Q_ROWS + 1],
                                            rtq[:, g:g + 1].broadcast_to([P, B]))
            pool.drain()
            pool.tensor_copy(identb[:], ident[:]).then_inc(s_rt, 1)
            for i, t in enumerate((nkb, nvb)):
                for hf in range(2):
                    rows = slice(hf * DH, (hf + 1) * DH)
                    pool.drain()
                    for g in range(G):
                        flat = t[rows, g].rearrange("p a b -> p (a b)")
                        last = pool.tensor_copy(flat[:, hf::H + 2], nkv[rows, i, g, :])
            last.then_inc(s_null, 1)
            pool.drain()
            pool.memset(zerob[:], 0.0)
            pool.tensor_copy(windowb[:], windowf[:]).then_inc(s_bf, 1)

            pool.wait_ge(prep_in, J_GA + 2)

            def head(h):
                at_least(pool, y_out, 4 * h)
                pool.tensor_copy(gscr[:], GA[:, h, :]).then_inc(g_loaded, 1)
            head(0)
            head(1)
            pool.wait_ge(w_in, W_NULL + 1)
            pool.memset(qbd, 0.0).then_inc(qbd_zero, 1)
            pool.wait_ge(prep_in, J_END)
            pool.memset(loc[:], 0.0).then_inc(loc_zero, 1)
            with pool.Fori(2, HA) as h:
                head(h)

            pool.wait_ge(w_in, W_W2C + 8)

            def add(p, b, ahead):
                u = 4 * p + b + ahead
                k = (b + ahead) % 2
                pool.wait_ge(roped, u + 1)
                at_least(pool, qkT_out, u - 1)
                pool.tensor_tensor(rot[:, k].rearrange("p a b -> p (a b)"),
                                   r1[:, k].rearrange("p a b c -> p (a b c)"),
                                   r2[:, k].rearrange("p a b c -> p (a b c)"), ALU.add).then_inc(rot_in, 1)

            def w2_load(p):
                if not isinstance(p, int) or p > 0:
                    pool.wait_ge(out_out, 4 * p)
                pool.tensor_copy(wscr[:], W2B[:, bass.ts(p, 2), :]).then_inc(w2_loaded, 1)

            def pick_columns(b):
                if b == 0:
                    pool.wait_ge(qcode_in, 1)
                for j in range(BLK):
                    for g in range(G):
                        r = g * B + b
                        t = pool.tensor_scalar(OHQ[:, b * BLK + j, g * W:(g + 1) * W], iota[:, 0:W],
                                               qcode[:, j, r:r + 1], None, ALU.is_equal)
                t.then_inc(ohq_in, 1)

            add(0, 0, 0)
            add(0, 0, 1)

            def pair(p, first, last):
                for b in range(UNITS):
                    if not (last and b >= 2):
                        add(p, b, 2)
                    if b == 0:
                        w2_load(p)
                    if first:
                        pick_columns(b)
            sweep(pool, PAIRS, pair)

            pool.wait_ge(qsel_in, B)

            def onehots(g, b, it, k):
                at_least(pool, gx_out, it * 6 + k - 1)
                col = (k + 1 - KV_W0) * G * B + g * B
                pool.tensor_copy(kvcol[:, k % 2, :].unsqueeze(2), kvcode[:, :, bass.ds(b + col, 1)])
                pool.drain()
                for c in range((k + 3) // 2):
                    rows = min(P, W * (k + 2) - c * P)
                    if rows < P:
                        pool.drain()
                    t = pool.tensor_scalar(OH[0:rows, k % 2, c, :], iota[0:rows, :], kvcol[0:rows, k % 2, c:c + 1],
                                           None, ALU.is_equal)
                t.then_inc(oh_in, 1)
                if rows < P:
                    pool.drain()

            def sequence(g, b, it, before):
                onehots(g, b, it, 1)
                onehots(g, b, it, 2)
                at_least(pool, null_out, it)
                src = qsel[:, g, bass.ds(b, 1), NQ:].rearrange("p o (w q) -> p (o w) q", q=NQ)
                for r in range(4):
                    c = pool.tensor_copy(qrep[:, :, r, :], src)
                c.then_inc(rep_in, 1)
                for k in range(3, 6):
                    onehots(g, b, it, k)
                    if k == 3 and not before:
                        pool.wait_ge(loc_in, UNITS * PAIRS)
                        pool.memset(oT[:], 0.0).then_inc(oT_zero, 1)
            sequences(pool, sequence)

            for b in range(B):
                pool.wait_ge(y_ready, b + 1)
                pool.wait_ge(ft_in, 3 * b + 3)
                pool.tensor_tensor(sN[:, b % 2].rearrange("p j n -> p (j n)"),
                                   sN[:, b % 2].rearrange("p j n -> p (j n)"),
                                   yN[:, b % 2].rearrange("p j n -> p (j n)"), ALU.mult).then_inc(sy_ready, 1)

        @block.tensor
        def _(pe):
            def bank(i, n=1):
                return ps[:, i] if n == 1 else ps[:, i:i + n]

            def job(k):
                at_least(pe, prep_in, k - 3)
                return bank(4 + k % 4)

            def product(to, j, lhs, rhs):
                for k in range(4):
                    h = 8 * (j // 2) + 2 * k + j % 2
                    rows = slice(DH * (h % 2), DH * (h % 2 + 1))
                    t = pe.matmul(to[:, k * D:(k + 1) * D], lhs[rows, h // 2, :], rhs[rows, h // 2, :],
                                  start=True, stop=True)
                return t

            pe.wait_ge(s_wa, 32)
            for j in range(2):
                to = job(J_GA + j)
                for k in range(4):
                    t = pe.matmul(to[:, k * D:(k + 1) * D], aq[:, 4 * j + k, :], ak[:, 4 * j + k, :],
                                  start=True, stop=True)
                t.then_inc(prep_out, 1)
            pe.wait_ge(s_wb, 32)
            for j in range(4):
                product(job(J_W2B + j), j, bv, bo).then_inc(prep_out, 1)
            pe.wait_ge(s_ident, 16)
            for b in range(B):
                to = job(J_XNT + b)
                pe.wait_ge(s_xn, b + 1)
                for k in range(BLK):
                    t = pe.transpose(to[:, k * P:(k + 1) * P], xn[:, b * BLK + k, :], ident[:])
                t.then_inc(prep_out, 1)
            for b in range(B):
                to = job(J_XLNT + b)
                pe.wait_ge(s_xh2, b + 1)
                for k in range(BLK):
                    t = pe.transpose(to[:, k * P:(k + 1) * P], xh2[:, b * BLK + k, :], ident[:])
                t.then_inc(prep_out, 1)
            pe.wait_ge(prep_in, J_XNT + B)
            pe.wait_ge(s_rt, 1)
            for b in range(B):
                t = pe.matmul(ps[0:KV_ROWS, 0, 0:CTX], RTk[:, b, :], xnT[:, b, 0:CTX],
                              start=(b == 0), stop=(b == B - 1))
            t.then_inc(logits, 1)
            for w in range(WQ):
                for b in range(B):
                    t = pe.matmul(ps[Q_AT:Q_AT + Q_ROWS, 1, 0:W], RTq[:, w * B + b, :],
                                  xnT[:, b, W * (w + 1):W * (w + 2)],
                                  start=(w == 0 and b == 0), stop=(w == WQ - 1 and b == B - 1))
            t.then_inc(logits, 1)
            for j in range(7):
                to = job(J_XLN + j)
                for k in range(4):
                    b, w = divmod(4 * j + k, 7)
                    if k == 0:
                        pe.wait_ge(prep_in, J_XLNT + 1 + (4 * j + 3) // 7)
                    t = pe.transpose(to[:, k * P:(k + 1) * P], xlnT[:, b, W * w:W * w + P], ident[:])
                t.then_inc(prep_out, 1)

            pe.wait_ge(prep_in, J_END)
            pe.wait_ge(r_start, 1)
            pe.wait_ge(s_wv, 16)
            pe.wait_ge(s_bf, 1)
            for b in range(B):
                pe.matmul(bank(b), identb[:], zerob[:], start=True, stop=False)

            def a_y(h, b, jobs=0):
                u = 4 * h + b
                pe.wait_ge(g_loaded, h + 1)
                at_least(pe, v_in, u)
                if jobs:
                    pe.wait_ge(w_in, jobs)
                pe.matmul(bank(7), gscr[:], xnT[:, b, :], start=True, stop=True).then_inc(y_out, 1)

            def a_v(h, b):
                u = 4 * h + b
                pe.wait_ge(y_in, u + 1)
                for k in range(BLK):
                    t = pe.matmul(ps[:, 7, k * D:(k + 1) * D], xnT[:, b, k * P:(k + 1) * P],
                                  wvT[:, bass.ds(h, 1), :].rearrange("p o d -> p (o d)"), start=True, stop=True)
                t.then_inc(v_out, 1)

            def a_scores(h, b, s):
                u = 4 * h + b
                if s == 0:
                    pe.wait_ge(y_in, u + 1)
                if s == 0:
                    at_least(pe, diag_in, u)
                else:
                    at_least(pe, relu_in, 2 * u + s - 2)
                for m, at, q0, q1 in A_STEPS[s]:
                    t = pe.matmul(ps[:, 4 + s, at:at + q1 - q0], xnT[:, b, m * P:(m + 1) * P],
                                  yT[:, b % 2, q0:q1], start=True, stop=True)
                t.then_inc(sc_out, 1)

            def a_sums(h, b, s):
                u = 4 * h + b
                if s == 0:
                    pe.wait_ge(v_in, u + 1)
                    pe.wait_ge(diag_in, u + 1)
                else:
                    pe.wait_ge(relu_in, 2 * u + s)
                for m, at, q0, q1 in A_STEPS[s]:
                    t = pe.matmul(ps[:, b, q0:q1], vN[:, b % 2, m, :], simA[:, b % 2, s, at:at + q1 - q0],
                                  start=False, stop=False, skip_group_check=True)
                return t

            def weights(job, prior):
                pe.wait_ge(v_in, prior)
                at_least(pe, w_in, job)
                if job == 0:
                    pe.wait_ge(s_wc, 64)
                if job == W_NULL:
                    pe.wait_ge(s_null, 1)
                    for g in range(G):
                        for p in range(PAIRS):
                            pe.matmul(ps[:, 7, g * H:(g + 1) * H], cq[:, g * PAIRS + p, :], nkb[:, g, p, :],
                                      start=(p == 0), stop=(p == PAIRS - 1))
                        for p in range(PAIRS):
                            t = pe.matmul(ps[0:H, 7, P * (g + 1):P * (g + 2)], nvb[:, g, p, :],
                                          co[:, g * PAIRS + p, :], start=(p == 0), stop=(p == PAIRS - 1))
                elif job < W_NULL:
                    t = product(bank(7), job, cq, ck)
                else:
                    t = product(bank(7), job - W_W2C, cv, co)
                t.then_inc(w_out, 1)

            def close(b):
                pe.matmul(bank(b), identb[:], zerob[:], start=False, stop=True).then_inc(pv_done, 1)

            def b_project(p, b, ahead):
                u = 4 * p + b + ahead
                at_least(pe, roped, u)
                q, c = (p, b + ahead) if b + ahead < UNITS else (p + 1, b + ahead - UNITS)
                to = ps[:, 0:2].rearrange("p k (a n) -> p (k a) n", a=2)
                for k in range(BLK):
                    t = pe.matmul(to[:, k, :], xlnT[:, c, k * P:(k + 1) * P],
                                  wqk[:, bass.ds(q, 1), :].rearrange("p o n -> p (o n)"), start=True, stop=True)
                t.then_inc(qk_out, 1)

            a_y(0, 0)
            a_v(0, 0)

            def head(h, first, last):
                for b in range(UNITS):
                    nh, nb = (h, b + 1) if b < UNITS - 1 else (h + 1, 0)
                    more = not (last and b == UNITS - 1)
                    at = 2 * b + (0 if first else W_W2C)
                    jobs = (at, at + 1) if first or last else ()
                    a_scores(h, b, 0)
                    if b > 0:
                        a_sums(h, b - 1, 2)
                    elif not first:
                        a_sums(h - 1, UNITS - 1, 2)
                    if last and b > 0:
                        close(b - 1)
                    if jobs and not more:
                        weights(jobs[0], prior=4 * h + b + 1)
                        pe.wait_ge(s_wqk, 16)
                        pe.wait_ge(sT_in, 2)
                        b_project(0, 0, 0)
                    if more:
                        a_y(nh, nb, at if jobs and b > 0 else 0 if first else W_NULL + 1)
                    a_scores(h, b, 1)
                    if more and jobs:
                        a_v(nh, nb)
                    if jobs and not more:
                        weights(jobs[1], prior=4 * h + b + 1)
                    a_sums(h, b, 0)
                    if jobs and more:
                        weights(jobs[0], prior=4 * h + b + 2)
                    elif more:
                        a_v(nh, nb)
                    a_scores(h, b, 2)
                    a_sums(h, b, 1)
                    if jobs and more:
                        weights(jobs[1], prior=4 * h + b + 2)
                    if first and b == UNITS - 1:
                        weights(W_NULL, prior=4 * h + b + 2)
            sweep(pe, HA, head)
            a_sums(HA - 1, UNITS - 1, 2)
            close(UNITS - 1)
            pe.wait_ge(codes, 1)
            for c in range(4):
                n = min(P, CTX - c * P)
                pe.transpose(ps[0:n, 4, c * KV_ROWS:(c + 1) * KV_ROWS], RE[0:KV_ROWS, c * P:c * P + n],
                             ident[0:KV_ROWS, 0:KV_ROWS])
            rows = slice(Q_AT, Q_AT + Q_ROWS)
            pe.transpose(ps[:, 5, 0:Q_ROWS], qhalf[rows, :], ident[rows, rows]).then_inc(code_out, 1)

            def b_turn(p, b, ahead):
                u = 4 * p + b + ahead
                k = (b + ahead) % 2
                pe.wait_ge(rot_in, u + 1)
                at_least(pe, pT_in, u - 1)
                for i in range(2):
                    for t4 in range(BLK):
                        t = pe.transpose(ps[:, 2 + i, t4 * P:(t4 + 1) * P], rot[:, k, t4, i * P:(i + 1) * P],
                                         ident[:])
                t.then_inc(qkT_out, 1)

            def b_scores(p, b):
                u = 4 * p + b
                pe.wait_ge(qT_in, 2 * u + 2)
                pe.wait_ge(kT_in, u + 1)
                for i in range(2):
                    at_least(pe, exp_in, 2 * u + i - 1)
                    for k in range(4):
                        w = 4 * i + k
                        at = W * max(w - 1, 0)
                        pe.matmul(ps[:, 4 + i, k * P:(k + 1) * P], qbd[:, w, :], kT[:, at:at + P],
                                  start=(k == 0), stop=False)
                    pe.matmul(bank(4 + i), identb[:], windowb[:, i * P:i * P + N], start=False,
                              stop=True).then_inc(sim_out, 1)

            def b_turn_probs(p, b, ahead_turned):
                u = 4 * p + b
                for w in range(NW):
                    if w % 4 == 0:
                        pe.wait_ge(norm_in, 2 * u + 1 + w // 4)
                        if ahead_turned and w == 0:
                            pe.wait_ge(qT_in, 2 * u + 4)
                        elif ahead_turned:
                            pe.wait_ge(kT_in, u + 2)
                    t = pe.transpose(ps[:, 2 + w // 4, (w % 4) * P:(w % 4 + 1) * P], pB[:, b % 2, w, :], ident[:])
                t.then_inc(pT_out, 1)

            def b_mix(p, b, i):
                u = 4 * p + b
                pe.wait_ge(pT_in, u + 1)
                at_least(pe, ax_in, 2 * u + i)
                for k in range(4):
                    w = 4 * i + k
                    t = pe.matmul(ps[:, 6, k * P:(k + 1) * P], xln[:, b * 7 + max(w - 1, 0), :],
                                  pTB[:, b % 2, w, :], start=True, stop=True)
                t.then_inc(ax_out, 1)

            def b_out(p, b, i):
                u = 4 * p + b
                if i == 0:
                    pe.wait_ge(w2_loaded, p + 1)
                    at_least(pe, loc_in, u)
                pe.wait_ge(ax_in, 2 * u + i + 1)
                for hf in range(2):
                    t = pe.matmul(ps[:, 7, i * N // 2:(i + 1) * N // 2].rearrange("p (w q) -> p w q", q=W),
                                  wscr[:, hf, :], axB[:, b % 2, 4 * i:4 * i + 4, hf * W:(hf + 1) * W],
                                  start=(hf == 0), stop=(hf == 1))
                if i == 1:
                    t.then_inc(out_out, 1)

            def pick_queries(b):
                pe.wait_ge(ohq_in, b + 1)
                if b < 2:
                    pe.wait_ge(roped, UNITS * PAIRS)
                else:
                    pe.wait_ge(qsel_in, b - 1)
                for j in range(BLK):
                    t = pe.matmul(ps[:, b % 2, j * P:(j + 1) * P], xhat[:, b * BLK + j, :],
                                  OHQ[:, b * BLK + j, :], start=True, stop=True)
                t.then_inc(qsel_out, 1)

            b_project(0, 0, 1)
            pe.wait_ge(sT_in, B)
            b_turn(0, 0, 0)
            pe.wait_ge(qcode_in, 1)

            def pair(p, first, last):
                for b in range(UNITS):
                    before = (p, b - 1) if b > 0 else (None if first else (p - 1, UNITS - 1))
                    b_scores(p, b)
                    turned = not (last and b == UNITS - 1)
                    if not (last and b >= 2):
                        b_project(p, b, 2)
                    if before:
                        b_mix(*before, 0)
                    if last and b >= 2:
                        pick_queries(2 * b - 4)
                        pick_queries(2 * b - 3)
                    if turned:
                        b_turn(p, b, 1)
                    if before:
                        b_mix(*before, 1)
                        b_out(*before, 0)
                        b_out(*before, 1)
                    if turned:
                        b_turn_probs(p, b, turned)
            sweep(pe, PAIRS, pair)
            end = (PAIRS - 1, UNITS - 1)

            pe.wait_ge(exp_in, 2 * UNITS * PAIRS)

            def gather(b, it, k):
                at_least(pe, xt_in, it * 6 + k)
                if k > 0:
                    at_least(pe, oh_in, it * 5 + k)
                n = 1 if k == 0 else (k + 3) // 2
                for c in range(n):
                    rows = P if k == 0 else min(P, W * (k + 2) - c * P)
                    onehot = ident[:] if k == 0 else OH[0:rows, k % 2, c, :]
                    t = pe.matmul(ps[:, 4, 0:D], onehot,
                                  xhat[0:rows, bass.ds(b * BLK + c, 1), :].rearrange("p o d -> p (o d)"),
                                  start=(c == 0), stop=(c == n - 1))
                t.then_inc(gx_out, 1)

            def turn(it, k):
                at_least(pe, xn_in, it * 6 + k + 1)
                pe.transpose(ps[:, 4, P:2 * P], XN[:, k, :], ident[:]).then_inc(xt_out, 1)

            def expand(g, b, it, s):
                if s > 1:
                    at_least(pe, (u_act, u_dve)[s % 2], it * 4 + s // 2)
                elif s == 0:
                    at_least(pe, cout_in, it - 1)
                for i in range(2):
                    t = pe.matmul(ps[:, s % 2, i * WQ * NQ:(i + 1) * WQ * NQ], G2[:, g * H + 2 * s + i, :],
                                  qsel[:, g, bass.ds(b, 1), NQ:].rearrange("p o n -> p (o n)"),
                                  start=True, stop=True)
                t.then_inc(u_out, 1)

            def nulls(g, it):
                at_least(pe, rep_in, it + 1)
                pe.wait_ge(u_dve, it * 4 + 4)
                for w in range(WQ):
                    t = pe.matmul(ps[:, 1, w * H:(w + 1) * H], qrep[:, w].rearrange("p r q -> p (r q)"),
                                  NK[:, g, :], start=True, stop=True)
                t.then_inc(null_out, 1)

            def scores(it, w):
                k, n = max(w - 1, 0), (W if w == 0 else P)
                pe.wait_ge(xt_in, it * 6 + k + 1)
                if w == 0:
                    pe.wait_ge(u_act, it * 4 + 4)
                    pe.wait_ge(u_dve, it * 4 + 4)
                    at_least(pe, cexp_in, it * WQ)
                elif w >= 3:
                    pe.wait_ge(cexp_in, it * WQ + w - 2)
                for hg in range(4):
                    t = pe.matmul(ps[:, 5 + w % 3, hg * P:hg * P + n],
                                  U[:, w, 4 * hg:4 * hg + 4, :].rearrange("p h q -> p (h q)"),
                                  XT[:, k % 2, 0:n], start=True, stop=True)
                t.then_inc(csim_out, 1)

            def turn_probs(it, w):
                pe.wait_ge(cnorm_in, it * WQ + w + 1)
                at_least(pe, cpT_in, it * WQ + w)
                for hg in range(4):
                    t = pe.transpose(ps[:, 3, hg * P:(hg + 1) * P], pC[:, w % 3, hg, :], ident[:])
                t.then_inc(cpT_out, 1)

            def mix(it, w):
                n = W if w == 0 else P
                pe.wait_ge(cpT_in, it * WQ + w + 1)
                at_least(pe, cax_in, it * WQ + w)
                pe.matmul(ps[:, 2, :], XN[0:n, max(w - 1, 0), :], pTC[0:n, w % 2, :],
                          start=True, stop=True).then_inc(cax_out, 1)

            def null_probs(it):
                pe.wait_ge(pn16_in, it + 1)
                for w in range(WQ):
                    t = pe.matmul(ps[0:H, 1, 256 + w * NQ:256 + (w + 1) * NQ],
                                  pn16[:, 4 * w:4 * w + 4, :].rearrange("p a b -> p (a b)"), fold[:],
                                  start=True, stop=True)
                t.then_inc(pnT_out, 1)

            def project(g, it, part):
                if part == 0:
                    pe.wait_ge(cax_in, it * WQ + WQ)
                for h in range(part * H // 2, (part + 1) * H // 2):
                    pe.matmul(ps[:, 0, 0:WQ * NQ], W2C[:, g * H + h, :],
                              axC[:, h].rearrange("p w q -> p (w q)"), start=(h == 0), stop=False)
                if part == 1:
                    pe.wait_ge(pnT_in, it + 1)
                    pe.matmul(ps[:, 0, 0:WQ * NQ], NV[:, g, :], pnT[:], start=False, stop=True).then_inc(cout_out, 1)

            def sequence(g, b, it, before):
                if before:
                    pg, _, pit = before
                gather(b, it, 0)
                if not before:
                    pe.wait_ge(qsel_in, B)
                expand(g, b, it, 0)
                expand(g, b, it, 1)
                if before:
                    turn_probs(pit, 5)
                else:
                    b_turn_probs(*end, False)
                turn(it, 0)
                expand(g, b, it, 2)
                if before:
                    mix(pit, 4)
                expand(g, b, it, 3)
                if before:
                    turn_probs(pit, 6)
                else:
                    b_mix(*end, 0)
                expand(g, b, it, 4)
                gather(b, it, 1)
                if before:
                    mix(pit, 5)
                else:
                    b_mix(*end, 1)
                expand(g, b, it, 5)
                turn(it, 1)
                expand(g, b, it, 6)
                expand(g, b, it, 7)
                if before:
                    mix(pit, 6)
                else:
                    b_out(*end, 0)
                    b_out(*end, 1)
                gather(b, it, 2)
                nulls(g, it)
                scores(it, 0)
                scores(it, 1)
                turn(it, 2)
                if before:
                    project(pg, pit, 0)
                else:
                    pe.wait_ge(loc_in, UNITS * PAIRS)
                scores(it, 2)
                if before:
                    pe.wait_ge(null_in, it + 1)
                    null_probs(pit)
                turn_probs(it, 0)
                if before:
                    project(pg, pit, 1)
                for w in range(WQ - 3):
                    if w + 3 <= 5:
                        gather(b, it, w + 3)
                    scores(it, w + 3)
                    if w + 3 <= 5:
                        turn(it, w + 3)
                    turn_probs(it, w + 1)
                    mix(it, w)

            sequences(pe, sequence)

            def turn_back(b, early=True, late=True):
                at_least(pe, ft_in, 3 * b)
                if early:
                    for j in range(BLK):
                        to = slice(j * P, (j + 1) * P)
                        t = pe.transpose(ps[:, 4, to], OHQ[:, b * BLK + j, :], ident[:])
                    t.then_inc(ft_out, 1)
                    for j in range(BLK):
                        to = slice(j * P, (j + 1) * P)
                        t = pe.transpose(ps[:, 7, to], sT[:, b, to], ident[:])
                    t.then_inc(ft_out, 1)
                if late:
                    for j in range(BLK):
                        to = slice(j * P, (j + 1) * P)
                        t = pe.transpose(ps[:, 6, to], oT[:, b, j].rearrange("p g s -> p (g s)"), ident[:])
                    t.then_inc(ft_out, 1)

            def spread(b):
                pe.wait_ge(ft_in, 3 * b + 3)
                at_least(pe, y_ready, b)
                for j in range(BLK):
                    to = slice(j * P, (j + 1) * P)
                    pe.matmul(ps[:, 5, to], OHS[:, b % 2, j, :], oN[:, b % 2, j, :], start=True, stop=False)
                    t = pe.matmul(ps[:, 5, to], loc[:, b, to], ident[:], start=False, stop=True)
                t.then_inc(fin_out, 1)

            g, _, it = LAST
            turn_probs(it, 5)
            turn_back(0)
            mix(it, 4)
            turn_probs(it, 6)
            spread(0)
            mix(it, 5)
            null_probs(it)
            turn_back(1)
            mix(it, 6)
            spread(1)
            turn_back(2)
            project(g, it, 0)
            spread(2)
            turn_back(3, late=False)
            project(g, it, 1)
            pe.wait_ge(cout_in, G * B)
            turn_back(3, early=False)
            spread(3)

        @block.scalar
        def _(act):
            act.preload_act_table_set("natural_log_exp_and_others")
            act.wait_ge(s_var, 1)
            act.activation(tmp3[:, 0, :], var3[:, 0, :], ACT.Ln)
            act.drain()
            act.activation(rs3[:, 0, :], tmp3[:, 0, :], ACT.Exp, scale=-0.5).then_inc(s_ln, 1)

            def job(k):
                act.wait_ge(prep_out, k + 1)
                return ps[:, 4 + k % 4, :]

            def evacuate(j0, n, to):
                for j in range(n):
                    act.activation(to[:, 4 * j:4 * j + 4, :], job(j0 + j).rearrange("p (a b) -> p a b", b=D),
                                   ACT.Copy).then_inc(prep_in, 1)

            def by_half(to, j):
                at = 8 * (j // 2) + j % 2
                return to[:, at:at + 7:2, :]

            def evacuate_w2b(j0, j1):
                for j in range(j0, j1):
                    act.activation(by_half(W2B, j), job(J_W2B + j).rearrange("p (a b) -> p a b", b=D),
                                   ACT.Copy).then_inc(prep_in, 1)
            evacuate(J_GA, 2, GA)
            evacuate_w2b(0, 2)
            act.wait_ge(s_var, 2)
            act.activation(tmp3[:, 1:3, :], var3[:, 1:3, :], ACT.Ln)
            act.drain()
            act.activation(rs3[:, 1:3, :], tmp3[:, 1:3, :], ACT.Exp, scale=-0.5).then_inc(s_ln, 1)
            evacuate_w2b(2, 4)
            act.wait_ge(s_const, 16 * N_CONST)
            for b in range(B):
                act.activation(xnT[:, b, :], job(J_XNT + b), ACT.Copy).then_inc(prep_in, 1)
            for b in range(B):
                act.activation(xlnT[:, b, :], job(J_XLNT + b), ACT.Identity, bias=lnb[:, 0:1],
                               scale=lng[:, 0:1]).then_inc(prep_in, 1)
            evacuate(J_XLN, 7, xln)
            act.activation(cgs[:], cg[:], ACT.Copy, scale=SCALE)

            act.wait_ge(r_start, 1)

            def descend(i, first=False):
                if not first:
                    act.wait_ge(r_u, i)
                act.activation(RE[:], rmask[:] if first else RU[:], ACT.Exp, scale=eps[:, 0, bass.ds(i, 1)],
                               accum_out=rsum[:])
                act.drain()
                act.activation(rln[:], rsum[:], ACT.Ln, scale=rinvk[:, 0:1]).then_inc(r_l, 1)

            def a_y(h, b):
                act.wait_ge(y_out, 4 * h + b + 1)
                act.activation(yT[:, b % 2, :], ps[:, 7, :], ACT.Copy).then_inc(y_in, 1)

            def a_relu(h, b, s):
                act.wait_ge(sc_out, 3 * (4 * h + b) + s + 1)
                n = (N, 2 * P)[s - 1]
                act.activation(simA[:, b % 2, s, 0:n], ps[:, 4 + s, 0:n], ACT.Relu,
                               scale=1.0 / N).then_inc(relu_in, 1)

            def weights(job):
                act.wait_ge(w_out, job + 1)
                blocks = ps[:, 7, :].rearrange("p (a b) -> p a b", b=D)
                if job == W_NULL:
                    for g in range(G):
                        act.activation(NK[:, g, :], ps[:, 7, g * H:(g + 1) * H], ACT.Copy, scale=qg[:, g:g + 1])
                    t = act.activation(NV[:], ps[0:H, 7, P:P * (1 + G)].rearrange("p (g d) -> p g d", g=G), ACT.Copy)
                else:
                    to, gain, j = (G2, qg, job) if job < W_NULL else (W2C, cg, job - W_W2C)
                    g = j * G // 8
                    t = act.activation(by_half(to, j), blocks, ACT.Copy, scale=gain[:, g:g + 1])
                t.then_inc(w_in, 1)

            a_y(0, 0)

            def head(h, first=False, last=False, steps=False, jobs=None):
                for b in range(UNITS):
                    if not (last and b == UNITS - 1):
                        a_y(*((h, b + 1) if b < UNITS - 1 else (h + 1, 0)))
                    end = last and b == UNITS - 1
                    if end:
                        weights(jobs + 2 * b)
                    a_relu(h, b, 1)
                    if jobs is not None:
                        weights(jobs + 2 * b + end)
                    a_relu(h, b, 2)
                    if steps:
                        descend(4 * h + b, first=(first and b == 0))
                    if jobs is not None and not end:
                        weights(jobs + 2 * b + 1)
                if jobs == 0:
                    weights(W_NULL)
            head(0, first=True, steps=True, jobs=0)
            with act.Fori(1, STEP_HEADS) as h:
                head(h, steps=True)
            with act.Fori(STEP_HEADS, HA - 1) as h:
                head(h)
            head(HA - 1, last=True, jobs=W_W2C)

            def b_turned(p, b, ahead):
                u = 4 * p + b + ahead
                act.wait_ge(qkT_out, u + 1)
                at_least(act, sim_out, 2 * u)
                q = ps[:, 2, :].rearrange("p (w q) -> p w q", q=W)
                for hf in range(2):
                    rows = slice(DH * hf, DH * (hf + 1))
                    act.activation(qbd[rows, :, W * hf:W * (hf + 1)], q[rows], ACT.Copy,
                                   scale=SCALE).then_inc(qT_in, 1)

            def b_exp(p, b, i):
                u = 4 * p + b
                act.wait_ge(max_in, 2 * u + i + 1)
                if i == 0:
                    at_least(act, pT_out, u - 1)
                for w in range(4 * i, 4 * i + 4):
                    t = act.activation(pB[:, b % 2, w, :], ps[:, 4 + w // 4, (w % 4) * P:(w % 4 + 1) * P], ACT.Exp,
                                       bias=nmB[:, b % 2, w:w + 1], accum_out=rsB[:, b % 2, w:w + 1])
                t.then_inc(exp_in, 1)

            def b_mixed(p, b, i):
                u = 4 * p + b
                act.wait_ge(ax_out, 2 * u + i + 1)
                if i == 0:
                    at_least(act, out_out, u - 1)
                act.activation(axB[:, b % 2, 4 * i:4 * i + 4, :],
                               ps[:, 6, :].rearrange("p (w n) -> p w n", n=P), ACT.Copy).then_inc(ax_in, 1)

            act.wait_ge(qbd_zero, 1)
            b_turned(0, 0, 0)

            def pair(p, first, last):
                for b in range(UNITS):
                    before = (p, b - 1) if b > 0 else (None if first else (p - 1, UNITS - 1))
                    b_exp(p, b, 0)
                    b_exp(p, b, 1)
                    if before:
                        b_mixed(*before, 0)
                        b_mixed(*before, 1)
                    if not (last and b == UNITS - 1):
                        b_turned(p, b, 1)
            sweep(act, PAIRS, pair)
            end = (PAIRS - 1, UNITS - 1)

            def gathered(it, k):
                act.wait_ge(gx_out, it * 6 + k + 1)
                act.activation(XN[:, k, :], ps[:, 4, 0:D], ACT.Copy).then_inc(xn_in, 1)

            def turned(it, k):
                act.wait_ge(xt_out, it * 6 + k + 1)
                act.activation(XT[:, k % 2, :], ps[:, 4, P:2 * P], ACT.Copy).then_inc(xt_in, 1)

            def expanded(g, it, s):
                act.wait_ge(u_out, it * 8 + s + 1)
                act.activation(U[:, :, 2 * s:2 * s + 2, :].rearrange("p w h q -> p h w q"),
                               ps[:, 0, 0:2 * WQ * NQ].rearrange("p (h w q) -> p h w q", h=2, q=NQ),
                               ACT.Copy, scale=cgs[:, g:g + 1]).then_inc(u_act, 1)

            def probs(it, w):
                n, k = (W if w == 0 else P), w % 3
                act.wait_ge(cmax_in, it * WQ + w + 1)
                for hg in range(4):
                    act.activation(pC[:, k, hg, 0:n], ps[:, 5 + k, hg * P:hg * P + n], ACT.Exp,
                                   bias=nmC[:, k, hg:hg + 1], accum_out=rsC[:, k, hg:hg + 1])
                act.activation(pnC[:, 4 * w:4 * w + 4], dnC[:, k, :], ACT.Exp).then_inc(cexp_in, 1)

            def probs_turned(it, w):
                n = W if w == 0 else P
                act.wait_ge(cpT_out, it * WQ + w + 1)
                at_least(act, cax_out, it * WQ + w - 1)
                act.activation(pTC[0:n, w % 2, :], ps[0:n, 3, :], ACT.Copy).then_inc(cpT_in, 1)

            def mixed(it, w):
                act.wait_ge(cax_out, it * WQ + w + 1)
                act.activation(axC[:, :, w, :], ps[:, 2, :].rearrange("p (h q) -> p h q", q=NQ),
                               ACT.Copy).then_inc(cax_in, 1)

            def projected(g, b, it):
                act.wait_ge(cout_out, it + 1)
                act.activation(oT[:, bass.ds(b, 1), 0, g, NQ:].rearrange("p o s -> p (o s)"), ps[:, 0, 0:NQ], ACT.Copy)
                act.activation(oT[:, bass.ds(b, 1), 1:, g, :].rearrange("p o j s -> p (o j) s"),
                               ps[:, 0, NQ:WQ * NQ].rearrange("p (j s) -> p j s", s=W),
                               ACT.Copy).then_inc(cout_in, 1)

            def sequence(g, b, it, before):
                if before:
                    mixed(before[2], 3)
                gathered(it, 0)
                expanded(g, it, 0)
                turned(it, 0)
                expanded(g, it, 2)
                if before:
                    mixed(before[2], 4)
                else:
                    b_mixed(*end, 0)
                expanded(g, it, 4)
                gathered(it, 1)
                if before:
                    mixed(before[2], 5)
                else:
                    b_mixed(*end, 1)
                turned(it, 1)
                expanded(g, it, 6)
                if before:
                    mixed(before[2], 6)
                gathered(it, 2)
                probs(it, 0)
                turned(it, 2)
                probs(it, 1)
                probs(it, 2)
                if before:
                    projected(*before)
                else:
                    act.wait_ge(oT_zero, 1)
                for w in range(WQ - 3):
                    if w + 3 <= 5:
                        gathered(it, w + 3)
                    if w > 0:
                        mixed(it, w - 1)
                    if w + 3 <= 5:
                        turned(it, w + 3)
                    if w + 1 in ON_ACT:
                        probs_turned(it, w + 1)
                    probs(it, w + 3)

            sequences(act, sequence)

            def turned_back(b, parts=(0, 1, 2)):
                for i in parts:
                    t, k = ((OHS, 4), (sN, 7), (oN, 6))[i]
                    act.wait_ge(ft_out, 3 * b + i + 1)
                    if i == 0:
                        at_least(act, fin_out, b - 1)
                    if i == 1:
                        at_least(act, res_in, b - 1)
                    act.activation(t[:, b % 2], ps[:, k, :].rearrange("p (j n) -> p j n", j=BLK),
                                   ACT.Copy).then_inc(ft_in, 1)

            def exps(b):
                act.wait_ge(y_ready, b + 1)
                at_least(act, res_in, b - 1)
                act.activation(eN[:, b % 2], yN[:, b % 2], ACT.Exp, scale=-1.0).then_inc(e_ready, 1)

            it = LAST[2]
            mixed(it, 3)
            turned_back(0)
            mixed(it, 4)
            exps(0)
            mixed(it, 5)
            turned_back(1)
            mixed(it, 6)
            exps(1)
            turned_back(2)
            turned_back(3, (0,))
            exps(2)
            turned_back(3, (1,))
            projected(*LAST)
            turned_back(3, (2,))
            exps(3)

        @block.vector
        def _(dve):
            def rsqrt_step(n0, n1):
                r, v, t = rs3[:, n0:n1], var3[:, n0:n1], tmp3[:, n0:n1]
                dve.tensor_tensor(t, r, r, ALU.mult)
                dve.drain()
                dve.tensor_tensor(t, t, v, ALU.mult)
                dve.drain()
                dve.tensor_scalar(t, t, -0.5, 1.5, ALU.mult, ALU.add)
                dve.drain()
                dve.tensor_tensor(r, r, t, ALU.mult)
                dve.drain()

            for b in range(B):
                dve.wait_ge(s_x[b], 16)
                for k in range(b * BLK, (b + 1) * BLK):
                    dve.bn_stats(stats[:, k, :], x[:, k, :])
            dve.drain()
            for k in range(NB):
                dve.bn_aggr(mv[:, k, :], stats[:, k, :])
            dve.drain()
            dve.tensor_scalar(var3[:, 0, :], mv[:, :, 1], 1e-5, None, ALU.add).then_inc(s_var, 1)
            dve.wait_ge(s_ln, 1)
            rsqrt_step(0, 1)
            for k in range(NB):
                t = dve.tensor_scalar(xn[:, k, :], x[:, k, :], mv[:, k, 0:1], rs3[:, 0, k:k + 1],
                                      ALU.subtract, ALU.mult)
                if k % BLK == BLK - 1:
                    t.then_inc(s_xn, 1)
            dve.tensor_tensor(tmp3[:, 0, :], rs3[:, 0, :], rs3[:, 0, :], ALU.mult)
            dve.drain()
            dve.tensor_tensor(tmp3[:, 0, :], tmp3[:, 0, :], mv[:, :, 1], ALU.mult)
            dve.drain()
            dve.tensor_scalar(var3[:, 1, :], tmp3[:, 0, :], 1e-5, None, ALU.add)
            dve.tensor_scalar(var3[:, 2, :], tmp3[:, 0, :], 1e-24 / D, 2.0**40, ALU.max, ALU.mult).then_inc(s_var, 1)
            dve.wait_ge(s_ln, 2)
            rsqrt_step(1, 3)
            for k in range(NB):
                t = dve.tensor_scalar(xh2[:, k, :], xn[:, k, :], rs3[:, 1, k:k + 1], None, ALU.mult)
                if k % BLK == BLK - 1:
                    t.then_inc(s_xh2, 1)
            for k in range(NB):
                dve.tensor_scalar(xhat[:, k, :], xn[:, k, :], rs3[:, 2, k:k + 1], 2.0**20, ALU.mult, ALU.mult)
            dve.wait_ge(s_const, 16 * N_CONST)
            dve.memset(RS[:], 0.0)
            dve.drain()
            qrows = slice(Q_AT, Q_AT + Q_ROWS)
            dve.tensor_copy(RS[qrows, W:], rmask[qrows, W:])
            dve.wait_ge(logits, 2)
            dve.tensor_tensor(RS[0:KV_ROWS, :], ps[0:KV_ROWS, 0, 0:CTX], rmask[0:KV_ROWS, :], ALU.add)
            dve.tensor_copy(RS[qrows, 0:W], ps[qrows, 1, 0:W])
            dve.drain()
            dve.tensor_reduce(rsmax[:], RS[:], AX.X, ALU.max)
            dve.memset(rm[:], 0.0)
            dve.drain()
            dve.nop().then_inc(r_start, 1)

            def new_bound(i):
                dve.wait_ge(r_l, i + 1)
                dve.tensor_scalar(rna[:], rln[:], eps[:, 1, bass.ds(i, 1)], rm[:, 0:1], ALU.mult, ALU.add)
                dve.drain()

            def descend(i):
                new_bound(i - 1)
                dve.tensor_tensor(rm[:], rsmax[:], rna[:], ALU.min)
                dve.drain()
                dve.tensor_scalar(RU[:], RS[:], rna[:, 0:1], rm[:, 0:1], ALU.min, ALU.subtract).then_inc(r_u, 1)

            def pick(rows, n):
                dve.max(rm8[rows, :], RU[rows, 0:n])
                dve.drain()
                dve.match_replace(RU[rows, 0:n], rm8[rows, :], RU[rows, 0:n], TAKEN)
                dve.drain()

            def a_v(h, b):
                dve.wait_ge(v_out, 4 * h + b + 1)
                dve.tensor_copy(vN[:, b % 2], ps[:, 7, :].rearrange("p (k d) -> p k d", d=D)).then_inc(v_in, 1)

            def a_diag(h, b):
                dve.wait_ge(sc_out, 3 * (4 * h + b) + 1)
                blocks = lambda t: t.rearrange("p (m n) -> p m n", n=P)
                dve.scalar_tensor_tensor(out=blocks(simA[:, b % 2, 0, :]), in0=blocks(ps[:, 4, :]), scalar=0.0,
                                         in1=causal[:].unsqueeze(1).broadcast_to([P, BLK, P]),
                                         op0=ALU.max, op1=ALU.mult).then_inc(diag_in, 1)

            a_v(0, 0)

            def exponents():
                new_bound(NITER - 1)
                dve.tensor_scalar(RU[:], RS[:], rna[:, 0:1], 0.0, ALU.subtract, ALU.min)
                dve.drain()
                dve.tensor_scalar(RU[:], RU[:], 1.0 / EPS[NITER], LOWEST, ALU.mult, ALU.max)
                dve.drain()

            def number():
                dve.tensor_scalar(RS[:], RU[:], TAKEN / 2, None, ALU.is_lt)
                dve.drain()
                dve.memset(RU[:], 1.0)
                dve.drain()
                dve.tensor_tensor_scan(RE[:], RU[:], RS[:], 0.0, ALU.mult, ALU.add)
                dve.drain()
                dve.scalar_tensor_tensor(out=RE[:], in0=RE[:], scalar=half[:, 0:1], in1=RS[:], op0=ALU.add, op1=ALU.mult)
                dve.drain()
                for i in range(2):
                    t = dve.tensor_scalar(qhalf[qrows, i * W:(i + 1) * W], RE[qrows, 0:W], half[qrows, i + 1:i + 2],
                                          None, ALU.mult)
                t.then_inc(codes, 1)

            def sums(b):
                dve.wait_ge(pv_done, b + 1)
                dve.tensor_tensor(sT[:, b, :], ps[:, b, :], xnT[:, b, :], ALU.add).then_inc(sT_in, 1)

            PICK_UNITS = (HA - 1 - STEP_HEADS) * UNITS
            assert NKV // 8 == 2 * PICK_UNITS

            def head(h, first=False, steps=False, picks=False, last=False):
                for b in range(UNITS):
                    a_diag(h, b)
                    if picks:
                        pick(slice(0, KV_ROWS), CTX)
                    if not (last and b == UNITS - 1):
                        a_v(*((h, b + 1) if b < UNITS - 1 else (h + 1, 0)))
                    if steps and not (first and b == 0):
                        descend(4 * h + b)
                    if picks:
                        pick(slice(0, KV_ROWS), CTX)
                        if b % (UNITS * PICK_UNITS // (NQ // 8) // UNITS) == 0:
                            pick(qrows, W)
                    if last:
                        if b == 0:
                            number()
                        else:
                            sums(b - 1)
            head(0, first=True, steps=True)
            with dve.Fori(1, STEP_HEADS) as h:
                head(h, steps=True)
            exponents()
            with dve.Fori(STEP_HEADS, HA - 1) as h:
                head(h, picks=True)
            head(HA - 1, last=True)

            def b_rope(p, b, ahead):
                u = 4 * p + b + ahead
                k, c = (b + ahead) % 2, (b + ahead) % UNITS
                dve.wait_ge(qk_out, u + 1)
                at_least(dve, rot_in, u - 1)
                src = ps[:, 0:2].rearrange("p k (a h e) -> p (k a) h e", a=2, e=DH)
                e2 = DH // 2
                table = lambda t, lo, n: t[:, :, lo:lo + n].unsqueeze(2).broadcast_to([P, BLK, 4, n])
                dve.tensor_tensor(r1[:, k], src, table(cos, 0, DH), ALU.mult)
                dve.tensor_tensor(r2[:, k, :, :, 0:e2], src[:, :, :, e2:DH], table(sin, 0, e2), ALU.mult)
                dve.tensor_tensor(r2[:, k, :, :, e2:DH], src[:, :, :, 0:e2], table(sin, e2, e2),
                                  ALU.mult).then_inc(roped, 1)

            def b_kturned(p, b, ahead):
                u = 4 * p + b + ahead
                dve.wait_ge(qkT_out, u + 1)
                at_least(dve, sim_out, 2 * u)
                dve.tensor_copy(kT, ps[:, 3, :]).then_inc(kT_in, 1)

            dve.wait_ge(w_in, W_NULL + 1)
            b_rope(0, 0, 0)
            sums(UNITS - 1)

            dve.wait_ge(code_out, 1)
            dve.memset(kvcode[:, 3], 0.0)
            dve.drain()
            dve.tensor_copy(kvcode[:, 0:3, :], ps[:, 4, 0:3 * KV_ROWS].rearrange("p (c r) -> p c r", c=3))
            dve.tensor_copy(kvcode[0:W, 3, :], ps[0:W, 4, 3 * KV_ROWS:4 * KV_ROWS])
            dve.tensor_copy(qrow_t[:], ps[:, 5, 0:Q_ROWS])
            dve.drain()
            gb = G * B
            dve.tensor_copy(qcode[:, 0, :], qrow_t[:, 0:gb])
            odd_even = qrow_t[:, gb:].rearrange("p (j o r) -> p j o r", o=2, r=gb)
            dve.tensor_tensor(qcode[:, 1:, :], odd_even[:, :, 0, :], odd_even[:, :, 1, :], ALU.add)
            dve.drain()
            b_kturned(0, 0, 0)
            dve.tensor_scalar(rcount[:], qcode[:], 0.5, None, ALU.is_gt).then_inc(qcode_in, 1)
            dve.drain()
            dve.tensor_tensor(rcnt[:], rcount[:, :, 0:B], rcount[:, :, B:], ALU.add)
            dve.drain()
            dve.tensor_scalar(rcnt[:], rcnt[:], 1.0, None, ALU.add)
            dve.drain()
            dve.reciprocal(rcnt[:], rcnt[:])

            def b_max(p, b):
                for i in range(2):
                    dve.wait_ge(sim_out, 2 * (4 * p + b) + i + 1)
                    dve.tensor_reduce(nmB[:, b % 2, 4 * i:4 * i + 4], ps[:, 4 + i].rearrange("p (w n) -> p w n", n=P),
                                      AX.X, ALU.max, negate=True).then_inc(max_in, 1)

            def b_norm(p, b, i):
                ws = slice(4 * i, 4 * i + 4)
                dve.wait_ge(exp_in, 2 * (4 * p + b) + i + 1)
                dve.reciprocal(riB[:, ws], rsB[:, b % 2, ws])
                dve.drain()
                dve.tensor_tensor(pB[:, b % 2, ws], pB[:, b % 2, ws],
                                  riB[:, ws].unsqueeze(2).broadcast_to([P, 4, P]), ALU.mult).then_inc(norm_in, 1)

            def b_probs(p, b):
                u = 4 * p + b
                dve.wait_ge(pT_out, u + 1)
                at_least(dve, ax_out, 2 * u - 2)
                dve.tensor_copy(pTB[:, b % 2], ps[:, 2:4].rearrange("p k (w n) -> p (k w) n", n=P)).then_inc(pT_in, 1)

            def b_add(p, b):
                dve.wait_ge(out_out, 4 * p + b + 1)
                dve.tensor_tensor(loc[:, b, :], loc[:, b, :], ps[:, 7, :], ALU.add).then_inc(loc_in, 1)

            dve.wait_ge(pv_done, B)
            dve.wait_ge(loc_zero, 1)
            def picked(b):
                dve.wait_ge(qsel_out, b + 1)
                dve.tensor_copy(qsel[:, :, b, :].rearrange("p g (j s) -> p g j s", s=W),
                                ps[:, b % 2, :].rearrange("p (j g s) -> p g j s", g=G, s=W)).then_inc(qsel_in, 1)

            b_rope(0, 0, 1)

            def pair(p, first, last):
                for b in range(UNITS):
                    before = (p, b - 1) if b > 0 else (None if first else (p - 1, UNITS - 1))
                    b_max(p, b)
                    b_norm(p, b, 0)
                    if not (last and b >= 2):
                        b_rope(p, b, 2)
                    else:
                        picked(2 * b - 4)
                        picked(2 * b - 3)
                    if not (last and b == UNITS - 1):
                        b_kturned(p, b, 1)
                    b_norm(p, b, 1)
                    if before:
                        b_add(*before)
                    if not (last and b == UNITS - 1):
                        b_probs(p, b)
            sweep(dve, PAIRS, pair)
            end = (PAIRS - 1, UNITS - 1)

            dve.memset(pC[:, 0], 0.0)

            def expanded(g, it, s):
                dve.wait_ge(u_out, it * 8 + s + 1)
                dve.tensor_scalar(U[:, :, 2 * s:2 * s + 2, :].rearrange("p w h q -> p h w q"),
                                  ps[:, 1, 0:2 * WQ * NQ].rearrange("p (h w q) -> p h w q", h=2, q=NQ),
                                  cgs[:, g:g + 1], None, ALU.mult).then_inc(u_dve, 1)

            def null_logits(it):
                dve.wait_ge(null_out, it + 1)
                dve.tensor_tensor(ntmp, ps[:, 1, 0:WQ * H].rearrange("p (w h) -> p w h", h=H),
                                  own[:].unsqueeze(1).broadcast_to([P, WQ, H]), ALU.mult)
                dve.drain()
                dve.tensor_reduce(nsC[:], ntmp.rearrange("p w (a b) -> p (w a) b", b=4), AX.X, ALU.add,
                                  negate=True)
                dve.drain()
                dve.tensor_scalar(nsC[:], nsC[:], SCALE, None, ALU.mult).then_inc(null_in, 1)
                dve.drain()

            def maxima(it, w):
                n, k = (W if w == 0 else P), w % 3
                dve.wait_ge(csim_out, it * WQ + w + 1)
                nm = nmC[:, k, :]
                null = nsC[:, 4 * w:4 * w + 4]
                dve.tensor_reduce(nm, ps[:, 5 + k, :].rearrange("p (h n) -> p h n", n=P)[:, :, 0:n], AX.X,
                                  ALU.max, negate=True)
                dve.drain()
                dve.tensor_tensor(nm, nm, null, ALU.min)
                dve.drain()
                dve.tensor_tensor(dnC[:, k, :], nm, null, ALU.subtract).then_inc(cmax_in, 1)

            def norms(it, w):
                n, k = (W if w == 0 else P), w % 3
                dve.wait_ge(cexp_in, it * WQ + w + 1)
                at = slice(4 * w, 4 * w + 4)
                dve.tensor_tensor(riC[:, at], rsC[:, k, :], pnC[:, at], ALU.add)
                dve.drain()
                dve.reciprocal(riC[:, at], riC[:, at])
                dve.drain()
                dve.tensor_tensor(pC[:, k, :, 0:n], pC[:, k, :, 0:n],
                                  riC[:, at].unsqueeze(2).broadcast_to([P, 4, n]), ALU.mult).then_inc(cnorm_in, 1)

            def probs_turned(it, w):
                n = W if w == 0 else P
                dve.wait_ge(cpT_out, it * WQ + w + 1)
                at_least(dve, cax_out, it * WQ + w - 1)
                dve.tensor_copy(pTC[0:n, w % 2, :], ps[0:n, 3, :]).then_inc(cpT_in, 1)

            def spread_null(it):
                dve.drain()
                dve.tensor_tensor(pnall[:], pnC[:], riC[:], ALU.mult)
                dve.drain()
                at_least(dve, pnT_out, it)
                dve.tensor_tensor(pn16[:], pnall[:].unsqueeze(2).broadcast_to([P, WQ * 4, 4]),
                                  own[:, 0:4].unsqueeze(1).broadcast_to([P, WQ * 4, 4]),
                                  ALU.mult).then_inc(pn16_in, 1)

            def null_turned(it):
                dve.wait_ge(pnT_out, it + 1)
                dve.tensor_copy(pnT[:], ps[0:H, 1, 256:256 + WQ * NQ]).then_inc(pnT_in, 1)

            def sequence(g, b, it, before):
                expanded(g, it, 1)
                if before:
                    pit = before[2]
                    norms(pit, 6)
                    probs_turned(pit, 5)
                else:
                    b_probs(*end)
                expanded(g, it, 3)
                if before:
                    probs_turned(pit, 6)
                    spread_null(pit)
                expanded(g, it, 5)
                expanded(g, it, 7)
                if not before:
                    b_add(*end)
                null_logits(it)
                maxima(it, 0)
                maxima(it, 1)
                norms(it, 0)
                maxima(it, 2)
                if before:
                    null_turned(pit)
                norms(it, 1)
                probs_turned(it, 0)
                for w in range(WQ - 3):
                    maxima(it, w + 3)
                    norms(it, w + 2)
                    if w + 1 not in ON_ACT:
                        probs_turned(it, w + 1)

            sequences(dve, sequence)
            it = LAST[2]
            norms(it, 6)
            probs_turned(it, 5)
            spread_null(it)
            probs_turned(it, 6)

            def mean(b):
                dve.wait_ge(fin_out, b + 1)
                at_least(dve, sy_ready, b - 1)
                dve.tensor_tensor(yN[:, b % 2], ps[:, 5, :].rearrange("p (j n) -> p j n", j=BLK),
                                  rcnt[:, :, b:b + 1].broadcast_to([P, BLK, D]), ALU.mult).then_inc(y_ready, 1)

            mean(0)
            null_turned(it)
            for b in range(B):
                k = b % 2
                dve.wait_ge(e_ready, b + 1)
                dve.tensor_scalar(eN[:, k], eN[:, k], 1.0, None, ALU.add)
                dve.drain()
                dve.reciprocal(eN[:, k], eN[:, k])
                if b + 2 < B:
                    mean(b + 1)
                dve.wait_ge(sy_ready, b + 1)
                dve.drain()
                dve.tensor_tensor(eN[:, k], sN[:, k], eN[:, k], ALU.mult)
                dve.drain()
                dve.tensor_tensor(res[:, b * BLK:(b + 1) * BLK, :], eN[:, k], x[:, b * BLK:(b + 1) * BLK, :],
                                  ALU.add).then_inc(res_in, 1)
                if b + 2 == B:
                    mean(b + 1)


def kernel(L0_attn_x, L0_attn_Wq, L0_attn_Wk, L0_attn_Wv, L0_ffn_ln_g, L0_ffn_ln_b, L0_ffn_w_qkv, L0_ffn_w_lo,
           L0_ffn_rt_q, L0_ffn_rt_kv, L0_ffn_qnorm_g, L0_ffn_cnorm_g, L0_ffn_null_kv, L0_ffn_w_q, L0_ffn_w_kv,
           L0_ffn_w_out):
    import concourse.bacc as _bacc
    from concourse.bass_utils import run_bass_kernel_spmd as _run

    a = lambda t: np.asarray(t)
    inner = H * DH
    qkv = a(L0_ffn_w_qkv)
    rows = lambda w: w.reshape(PAIRS, P, D).transpose(1, 0, 2)
    grouped = lambda w: w.reshape(G * PAIRS, P, D).transpose(1, 0, 2)
    kv, null = a(L0_ffn_w_kv), a(L0_ffn_null_kv)
    arrays = {
        "x": a(L0_attn_x), "Wq": a(L0_attn_Wq), "Wk": a(L0_attn_Wk),
        "WvT": a(L0_attn_Wv).transpose(2, 0, 1),
        "ln_g": a(L0_ffn_ln_g).reshape(D, 1), "ln_b": a(L0_ffn_ln_b).reshape(D, 1),
        "wqk": qkv[:2 * inner].reshape(2, PAIRS, P, D).transpose(3, 1, 0, 2).reshape(D, PAIRS, 2 * P),
        "bv": rows(qkv[2 * inner:]), "bo": rows(a(L0_ffn_w_lo).T),
        "qg": a(L0_ffn_qnorm_g).T, "cg": a(L0_ffn_cnorm_g).T,
        "rt_q": a(L0_ffn_rt_q).T, "rt_kv": a(L0_ffn_rt_kv).T,
        "cq": grouped(a(L0_ffn_w_q)), "ck": grouped(kv[:, :inner]), "cv": grouped(kv[:, inner:]),
        "co": grouped(a(L0_ffn_w_out).transpose(0, 2, 1)),
        "null": null.reshape(2, G, PAIRS, P).transpose(3, 0, 1, 2),
        **shape_constants(),
    }
    arrays = {f"in_{k}": np.ascontiguousarray(v) for k, v in arrays.items()}
    nc = _bacc.Bacc("TRN2", target_bir_lowering=False, num_devices=1)
    dram = {k[3:]: nc.dram_tensor(k, v.shape, mybir.dt.from_np(v.dtype), kind="ExternalInput").ap()
            for k, v in arrays.items()}
    out = nc.dram_tensor("out", (B, N, D), F32, kind="ExternalOutput").ap()
    build(nc, dram, out)
    r = _run(nc, [arrays], core_ids=[0])
    return r.results[0]["out"]
```
